# Optimizing a Trainium2 kernel written in Bass

```python
import numpy as np
import jax
import jax.numpy as jnp

def _softmax(x, axis=-1):
    return jax.nn.softmax(x, axis=axis)

def _gelu(x):
    return jax.nn.gelu(x, approximate=True)

def _silu(x):
    return jax.nn.silu(x)

def _sigmoid(x):
    return jax.nn.sigmoid(x)

def _layernorm(x, axis=-1, eps=1e-05):
    m = jnp.mean(x, axis=axis, keepdims=True)
    v = jnp.var(x, axis=axis, keepdims=True)
    return (x - m) / jnp.sqrt(v + eps)

def _scatter_add(tgt, idx, src, axis=0):
    return tgt.at[idx].add(src)

def _segment_sum(src, seg, n):
    return jax.ops.segment_sum(src, seg, n)
kernel_name = 'mk_seq_preln_d2_jaxref_r8_14936e'

def setup_inputs(seed: int=0):
    np.random.seed(seed)
    _w = jnp.asarray

    def _L0_attn_setup():
        import jax, jax.numpy as jnp
        import numpy as np
        D_MODEL = 128
        N_HEADS = 16
        D_HEAD = D_MODEL // N_HEADS
        BLOCK = 128
        B, T = (2, 256)

        def _flash_attention(Q, K, V, block_size, scale):
            Bb, H, Tt, d = Q.shape
            n_blocks = Tt // block_size
            Kb = K.reshape(Bb, H, n_blocks, block_size, d).transpose(2, 0, 1, 3, 4)
            Vb = V.reshape(Bb, H, n_blocks, block_size, d).transpose(2, 0, 1, 3, 4)
            starts = jnp.arange(n_blocks) * block_size
            q_pos = jnp.arange(Tt)

            def step(carry, xs):
                m, l, acc = carry
                kb, vb, st = xs
                scores = scale * jnp.einsum('bhtd,bhsd->bhts', Q, kb)
                kv_pos = st + jnp.arange(block_size)
                future = kv_pos[None, :] > q_pos[:, None]
                scores = jnp.where(future[None, None], -jnp.inf, scores)
                m_new = jnp.maximum(m, jnp.max(scores, axis=-1, keepdims=True))
                p = jnp.exp(scores - m_new)
                corr = jnp.exp(m - m_new)
                l = corr * l + jnp.sum(p, axis=-1, keepdims=True)
                acc = corr * acc + jnp.einsum('bhts,bhsd->bhtd', p, vb)
                return ((m_new, l, acc), None)
            m0 = jnp.full((Bb, H, Tt, 1), -jnp.inf, dtype=jnp.float32)
            l0 = jnp.zeros((Bb, H, Tt, 1), dtype=jnp.float32)
            a0 = jnp.zeros((Bb, H, Tt, d), dtype=jnp.float32)
            (m, l, acc), _ = jax.lax.scan(step, (m0, l0, a0), (Kb, Vb, starts))
            return acc / jnp.maximum(l, 1e-12)
        key = jax.random.key(seed)
        ks = jax.random.split(key, 5)
        x = jax.random.normal(ks[0], (B, T, D_MODEL), dtype=jnp.float32)

        def init_w(k):
            return jax.random.normal(k, (D_MODEL, D_MODEL), dtype=jnp.float32) / np.sqrt(D_MODEL).astype(np.float32)
        return {'x': x, 'Wq': init_w(ks[1]), 'Wk': init_w(ks[2]), 'Wv': init_w(ks[3]), 'Wo': init_w(ks[4])}
    _L0_attn_in = _L0_attn_setup()

    def _L0_ffn_setup():
        import jax, jax.numpy as jnp
        import numpy as np
        B, L, H = (8, 256, 128)
        E, K, R = (8, 2, 64)

        def _gates(cls_tok, Wr):
            logits = cls_tok @ Wr.T
            top_vals, top_idx = jax.lax.top_k(logits, K)
            neg_inf = jnp.full_like(logits, -jnp.inf)
            rows = jnp.arange(logits.shape[0])[:, None]
            masked = neg_inf.at[rows, top_idx].set(top_vals)
            return jax.nn.softmax(masked, axis=-1)
        key = jax.random.key(seed)
        k1, k2, k3, k4 = jax.random.split(key, 4)
        x = jax.random.normal(k1, (B, L, H), dtype=jnp.float32)
        Wr = jax.random.normal(k2, (E, H), dtype=jnp.float32) * (1.0 / np.sqrt(H))
        A = jax.random.normal(k3, (E, R, H), dtype=jnp.float32) * (1.0 / np.sqrt(H))
        Bw = jax.random.normal(k4, (E, H, R), dtype=jnp.float32) * (1.0 / np.sqrt(R))
        return {'x': x, 'Wr': Wr, 'A': A, 'Bw': Bw}
    _L0_ffn_in = _L0_ffn_setup()

    def _L1_attn_setup():
        import jax, jax.numpy as jnp
        import numpy as np
        D_MODEL = 128
        NUM_HEADS = 4
        KEY_DIM = 128
        VALUE_DIM = 256
        HEAD_QK = KEY_DIM // NUM_HEADS
        HEAD_V = VALUE_DIM // NUM_HEADS
        EPS = 1e-05
        CHUNK = 64
        ROPE_BASE = 10000.0

        def apply_rotary(q, k):
            n, d = (q.shape[1], q.shape[-1])
            inv_freq = 1.0 / ROPE_BASE ** (jnp.arange(0, d, 2, dtype=jnp.float32) / d)
            t = jnp.arange(n, dtype=jnp.float32)
            freqs = jnp.outer(t, inv_freq)
            cos = jnp.cos(freqs)[None, :, None, :]
            sin = jnp.sin(freqs)[None, :, None, :]

            def rot(x):
                x1, x2 = jnp.split(x, 2, axis=-1)
                return jnp.concatenate([x1 * cos - x2 * sin, x2 * cos + x1 * sin], axis=-1)
            return (rot(q), rot(k))

        def chunk_retention(q, k, v, gamma, chunk=CHUNK):
            B, H, N, dk = q.shape
            dv = v.shape[-1]
            NC = N // chunk
            qc = jnp.moveaxis(q.reshape(B, H, NC, chunk, dk), 2, 0)
            kc = jnp.moveaxis(k.reshape(B, H, NC, chunk, dk), 2, 0)
            vc = jnp.moveaxis(v.reshape(B, H, NC, chunk, dv), 2, 0)
            idx = jnp.arange(chunk)
            rel = idx[:, None] - idx[None, :]
            D = jnp.where(rel >= 0, gamma[:, None, None] ** rel, 0.0)
            cross_q = (gamma[:, None] ** (idx + 1))[None, :, :, None]
            cross_k = (gamma[:, None] ** (chunk - 1 - idx))[None, :, :, None]
            gC = (gamma ** chunk)[None, :, None, None]

            def step(S, qkv):
                qb, kb, vb = qkv
                attn = jnp.einsum('bhid,bhjd->bhij', qb, kb) * D[None]
                o_intra = jnp.einsum('bhij,bhjd->bhid', attn, vb)
                o_inter = jnp.einsum('bhid,bhde->bhie', qb * cross_q, S)
                S_new = gC * S + jnp.einsum('bhjd,bhje->bhde', kb * cross_k, vb)
                return (S_new, o_intra + o_inter)
            S0 = jnp.zeros((B, H, dk, dv), dtype=q.dtype)
            _, o = jax.lax.scan(step, S0, (qc, kc, vc))
            return jnp.moveaxis(o, 0, 2).reshape(B, H, N, dv)

        def rmsnorm(x, w):
            var = jnp.mean(x * x, axis=-1, keepdims=True)
            return x * jax.lax.rsqrt(var + EPS) * w
        key = jax.random.key(seed)
        ks = jax.random.split(key, 7)
        B, N = (2, 512)
        s = 0.02
        return {'x': jax.random.normal(ks[0], (B, N, D_MODEL), dtype=jnp.float32), 'Wq': jax.random.normal(ks[1], (D_MODEL, D_MODEL), dtype=jnp.float32) * s, 'Wk': jax.random.normal(ks[2], (D_MODEL, D_MODEL), dtype=jnp.float32) * s, 'Wv': jax.random.normal(ks[3], (D_MODEL, VALUE_DIM), dtype=jnp.float32) * s, 'Wg': jax.random.normal(ks[4], (D_MODEL, VALUE_DIM), dtype=jnp.float32) * s, 'Wo': jax.random.normal(ks[5], (VALUE_DIM, D_MODEL), dtype=jnp.float32) * s, 'gn_weight': jnp.ones((HEAD_V,), dtype=jnp.float32)}
    _L1_attn_in = _L1_attn_setup()

    def _L1_ffn_setup():
        import jax, jax.numpy as jnp
        import numpy as np
        DIM = 128
        DEPTH = 6
        HEADS = 16
        DIM_HEAD = 64
        WINDOW = 32
        INNER = HEADS * DIM_HEAD
        DIM_INNER = int(DIM * 4 * 2 / 3)
        QK_SCALE = 8.0

        def shift_tokens(t):
            a, s = jnp.split(t, 2, -1)
            s = jnp.pad(s, ((0, 0), (1, 0), (0, 0)))[:, :-1]
            return jnp.concatenate([a, s], -1)

        def l2norm(t):
            return t / jnp.maximum(jnp.linalg.norm(t, axis=-1, keepdims=True), 1e-12)

        def rotate_half(x):
            x1, x2 = jnp.split(x, 2, -1)
            return jnp.concatenate([-x2, x1], -1)

        def rotary_tables(n):
            half = jnp.arange(0, DIM_HEAD, 2, dtype=jnp.float32)
            inv_freq = 1.0 / 10000.0 ** (half / DIM_HEAD)
            t = jnp.arange(n, dtype=jnp.float32)
            freqs = t[:, None] * inv_freq[None, :]
            freqs = jnp.concatenate([freqs, freqs], -1)
            base_scale = (half + 0.4 * DIM_HEAD) / (1.4 * DIM_HEAD)
            power = (t - n // 2) / (WINDOW // 2)
            scale = base_scale[None, :] ** power[:, None]
            scale = jnp.concatenate([scale, scale], -1)
            return (freqs, scale)

        def local_attention(q, k, v):
            b, h, n, d = q.shape
            w = WINDOW
            nw = n // w
            bq = q.reshape(b, h, nw, w, d)
            bk = k.reshape(b, h, nw, w, d)
            bv = v.reshape(b, h, nw, w, d)

            def look(t):
                p = jnp.pad(t, ((0, 0), (0, 0), (1, 0), (0, 0), (0, 0)))
                return jnp.concatenate([p[:, :, :nw], p[:, :, 1:]], axis=3)
            bk2, bv2 = (look(bk), look(bv))
            seq = jnp.arange(n).reshape(nw, w)
            seq_p = jnp.pad(seq, ((1, 0), (0, 0)), constant_values=-1)
            jt = jnp.concatenate([seq_p[:nw], seq_p[1:]], axis=1)
            it = seq[:, :, None]
            jb = jt[:, None, :]
            mask = (it < jb) | (it > jb + w) | (jb == -1)
            sim = jnp.einsum('bhwie,bhwje->bhwij', bq, bk2) * QK_SCALE
            sim = jnp.where(mask, -jnp.finfo(sim.dtype).max, sim)
            attn = jax.nn.softmax(sim, -1)
            out = jnp.einsum('bhwij,bhwje->bhwie', attn, bv2)
            return out.reshape(b, h, n, d)

        def attn_layer(x, Wqkv, qs, ksc, Wo):
            b, n, _ = x.shape
            qkv = x @ Wqkv
            q, k, v = jnp.split(qkv, 3, -1)
            sh = lambda t: t.reshape(b, n, HEADS, DIM_HEAD).transpose(0, 2, 1, 3)
            q, k, v = (sh(q), sh(k), sh(v))
            q = l2norm(q) * qs
            k = l2norm(k) * ksc
            freqs, scale = rotary_tables(n)
            cos, sin = (jnp.cos(freqs), jnp.sin(freqs))
            q = q * cos * scale + rotate_half(q) * sin * scale
            inv = 1.0 / scale
            k = k * cos * inv + rotate_half(k) * sin * inv
            out = local_attention(q, k, v)
            out = out.transpose(0, 2, 1, 3).reshape(b, n, INNER)
            return out @ Wo

        def ffn_layer(x, g, bln, W1, b1, W2, b2):
            mu = x.mean(-1, keepdims=True)
            var = ((x - mu) ** 2).mean(-1, keepdims=True)
            xn = (x - mu) / jnp.sqrt(var + 1e-05) * g + bln
            hg = xn @ W1 + b1
            a, gate = jnp.split(hg, 2, -1)
            return a * jax.nn.gelu(gate, approximate=False) @ W2 + b2
        key = jax.random.key(seed)
        ks = jax.random.split(key, 8)
        B, N = (2, 256)
        init = lambda k, shape: jax.random.normal(k, shape, jnp.float32) * 0.02
        return {'x': jax.random.normal(ks[0], (B, N, DIM), jnp.float32), 'Wqkv': init(ks[1], (DEPTH, DIM, 3 * INNER)), 'q_scale': jnp.ones((DEPTH, DIM_HEAD), jnp.float32), 'k_scale': jnp.ones((DEPTH, DIM_HEAD), jnp.float32), 'Wo': init(ks[2], (DEPTH, INNER, DIM)), 'ln_g': jnp.ones((DEPTH, DIM), jnp.float32), 'ln_b': jnp.zeros((DEPTH, DIM), jnp.float32), 'W1': init(ks[3], (DEPTH, DIM, 2 * DIM_INNER)), 'b1': jnp.zeros((DEPTH, 2 * DIM_INNER), jnp.float32), 'W2': init(ks[4], (DEPTH, DIM_INNER, DIM)), 'b2': jnp.zeros((DEPTH, DIM), jnp.float32)}
    _L1_ffn_in = _L1_ffn_setup()
    _d = {'L0_attn_x': _L0_attn_in['x'], 'L0_attn_Wq': _L0_attn_in['Wq'], 'L0_attn_Wk': _L0_attn_in['Wk'], 'L0_attn_Wv': _L0_attn_in['Wv'], 'L0_attn_Wo': _L0_attn_in['Wo'], 'L0_ffn_Wr': _L0_ffn_in['Wr'], 'L0_ffn_A': _L0_ffn_in['A'], 'L0_ffn_Bw': _L0_ffn_in['Bw'], 'L1_attn_Wq': _L1_attn_in['Wq'], 'L1_attn_Wk': _L1_attn_in['Wk'], 'L1_attn_Wv': _L1_attn_in['Wv'], 'L1_attn_Wg': _L1_attn_in['Wg'], 'L1_attn_Wo': _L1_attn_in['Wo'], 'L1_attn_gn_weight': _L1_attn_in['gn_weight'], 'L1_ffn_Wqkv': _L1_ffn_in['Wqkv'], 'L1_ffn_q_scale': _L1_ffn_in['q_scale'], 'L1_ffn_k_scale': _L1_ffn_in['k_scale'], 'L1_ffn_Wo': _L1_ffn_in['Wo'], 'L1_ffn_ln_g': _L1_ffn_in['ln_g'], 'L1_ffn_ln_b': _L1_ffn_in['ln_b'], 'L1_ffn_W1': _L1_ffn_in['W1'], 'L1_ffn_b1': _L1_ffn_in['b1'], 'L1_ffn_W2': _L1_ffn_in['W2'], 'L1_ffn_b2': _L1_ffn_in['b2']}
    _x0 = _d['L0_attn_x']
    _d['L0_attn_x'] = jax.random.normal(jax.random.fold_in(jax.random.key(seed), 1), (16, 256, 128), dtype=_x0.dtype)
    del _x0
    return _d

def reference(L0_attn_x, L0_attn_Wq, L0_attn_Wk, L0_attn_Wv, L0_attn_Wo, L0_ffn_Wr, L0_ffn_A, L0_ffn_Bw, L1_attn_Wq, L1_attn_Wk, L1_attn_Wv, L1_attn_Wg, L1_attn_Wo, L1_attn_gn_weight, L1_ffn_Wqkv, L1_ffn_q_scale, L1_ffn_k_scale, L1_ffn_Wo, L1_ffn_ln_g, L1_ffn_ln_b, L1_ffn_W1, L1_ffn_b1, L1_ffn_W2, L1_ffn_b2):

    def _L0_attn_ref(x, Wq, Wk, Wv, Wo):
        import jax, jax.numpy as jnp
        import numpy as np
        D_MODEL = 128
        N_HEADS = 16
        D_HEAD = D_MODEL // N_HEADS
        BLOCK = 128
        B, T = (2, 256)

        def _flash_attention(Q, K, V, block_size, scale):
            Bb, H, Tt, d = Q.shape
            n_blocks = Tt // block_size
            Kb = K.reshape(Bb, H, n_blocks, block_size, d).transpose(2, 0, 1, 3, 4)
            Vb = V.reshape(Bb, H, n_blocks, block_size, d).transpose(2, 0, 1, 3, 4)
            starts = jnp.arange(n_blocks) * block_size
            q_pos = jnp.arange(Tt)

            def step(carry, xs):
                m, l, acc = carry
                kb, vb, st = xs
                scores = scale * jnp.einsum('bhtd,bhsd->bhts', Q, kb)
                kv_pos = st + jnp.arange(block_size)
                future = kv_pos[None, :] > q_pos[:, None]
                scores = jnp.where(future[None, None], -jnp.inf, scores)
                m_new = jnp.maximum(m, jnp.max(scores, axis=-1, keepdims=True))
                p = jnp.exp(scores - m_new)
                corr = jnp.exp(m - m_new)
                l = corr * l + jnp.sum(p, axis=-1, keepdims=True)
                acc = corr * acc + jnp.einsum('bhts,bhsd->bhtd', p, vb)
                return ((m_new, l, acc), None)
            m0 = jnp.full((Bb, H, Tt, 1), -jnp.inf, dtype=jnp.float32)
            l0 = jnp.zeros((Bb, H, Tt, 1), dtype=jnp.float32)
            a0 = jnp.zeros((Bb, H, Tt, d), dtype=jnp.float32)
            (m, l, acc), _ = jax.lax.scan(step, (m0, l0, a0), (Kb, Vb, starts))
            return acc / jnp.maximum(l, 1e-12)
        Bx, Tx, _ = x.shape
        scale = 1.0 / np.sqrt(D_HEAD).astype(np.float32)

        def proj(W):
            y = jnp.einsum('btm,nm->btn', x, W)
            return y.reshape(Bx, Tx, N_HEADS, D_HEAD).transpose(0, 2, 1, 3)
        Q, K, V = (proj(Wq), proj(Wk), proj(Wv))
        O = _flash_attention(Q.astype(jnp.float32), K.astype(jnp.float32), V.astype(jnp.float32), BLOCK, scale)
        O = O.astype(x.dtype).transpose(0, 2, 1, 3).reshape(Bx, Tx, D_MODEL)
        return jnp.einsum('btm,nm->btn', O, Wo)

    def _L0_ffn_ref(x, Wr, A, Bw):
        import jax, jax.numpy as jnp
        import numpy as np
        B, L, H = (8, 256, 128)
        E, K, R = (8, 2, 64)

        def _gates(cls_tok, Wr):
            logits = cls_tok @ Wr.T
            top_vals, top_idx = jax.lax.top_k(logits, K)
            neg_inf = jnp.full_like(logits, -jnp.inf)
            rows = jnp.arange(logits.shape[0])[:, None]
            masked = neg_inf.at[rows, top_idx].set(top_vals)
            return jax.nn.softmax(masked, axis=-1)
        gates = _gates(x[:, 0, :], Wr)
        mid = jnp.einsum('blh,erh->belr', x, A)
        expert_out = jnp.einsum('belr,ehr->belh', mid, Bw)
        weighted = jnp.einsum('be,belh->blh', gates, expert_out)
        return x + weighted

    def _L1_attn_ref(x, Wq, Wk, Wv, Wg, Wo, gn_weight):
        import jax, jax.numpy as jnp
        import numpy as np
        D_MODEL = 128
        NUM_HEADS = 4
        KEY_DIM = 128
        VALUE_DIM = 256
        HEAD_QK = KEY_DIM // NUM_HEADS
        HEAD_V = VALUE_DIM // NUM_HEADS
        EPS = 1e-05
        CHUNK = 64
        ROPE_BASE = 10000.0

        def apply_rotary(q, k):
            n, d = (q.shape[1], q.shape[-1])
            inv_freq = 1.0 / ROPE_BASE ** (jnp.arange(0, d, 2, dtype=jnp.float32) / d)
            t = jnp.arange(n, dtype=jnp.float32)
            freqs = jnp.outer(t, inv_freq)
            cos = jnp.cos(freqs)[None, :, None, :]
            sin = jnp.sin(freqs)[None, :, None, :]

            def rot(x):
                x1, x2 = jnp.split(x, 2, axis=-1)
                return jnp.concatenate([x1 * cos - x2 * sin, x2 * cos + x1 * sin], axis=-1)
            return (rot(q), rot(k))

        def chunk_retention(q, k, v, gamma, chunk=CHUNK):
            B, H, N, dk = q.shape
            dv = v.shape[-1]
            NC = N // chunk
            qc = jnp.moveaxis(q.reshape(B, H, NC, chunk, dk), 2, 0)
            kc = jnp.moveaxis(k.reshape(B, H, NC, chunk, dk), 2, 0)
            vc = jnp.moveaxis(v.reshape(B, H, NC, chunk, dv), 2, 0)
            idx = jnp.arange(chunk)
            rel = idx[:, None] - idx[None, :]
            D = jnp.where(rel >= 0, gamma[:, None, None] ** rel, 0.0)
            cross_q = (gamma[:, None] ** (idx + 1))[None, :, :, None]
            cross_k = (gamma[:, None] ** (chunk - 1 - idx))[None, :, :, None]
            gC = (gamma ** chunk)[None, :, None, None]

            def step(S, qkv):
                qb, kb, vb = qkv
                attn = jnp.einsum('bhid,bhjd->bhij', qb, kb) * D[None]
                o_intra = jnp.einsum('bhij,bhjd->bhid', attn, vb)
                o_inter = jnp.einsum('bhid,bhde->bhie', qb * cross_q, S)
                S_new = gC * S + jnp.einsum('bhjd,bhje->bhde', kb * cross_k, vb)
                return (S_new, o_intra + o_inter)
            S0 = jnp.zeros((B, H, dk, dv), dtype=q.dtype)
            _, o = jax.lax.scan(step, S0, (qc, kc, vc))
            return jnp.moveaxis(o, 0, 2).reshape(B, H, N, dv)

        def rmsnorm(x, w):
            var = jnp.mean(x * x, axis=-1, keepdims=True)
            return x * jax.lax.rsqrt(var + EPS) * w
        B, N, _ = x.shape
        H = NUM_HEADS
        q1 = (x @ Wq).reshape(B, N, H, HEAD_QK)
        k1 = (x @ Wk).reshape(B, N, H, HEAD_QK)
        q1, k1 = apply_rotary(q1, k1)
        q = jnp.transpose(q1, (0, 2, 1, 3)) * HEAD_QK ** (-0.5)
        k = jnp.transpose(k1, (0, 2, 1, 3))
        v = jnp.transpose((x @ Wv).reshape(B, N, H, HEAD_V), (0, 2, 1, 3))
        gamma = 1.0 - jnp.exp2(-5.0 - jnp.arange(H, dtype=jnp.float32))
        o = chunk_retention(q, k, v, gamma)
        o = jnp.transpose(o, (0, 2, 1, 3))
        o = rmsnorm(o, gn_weight)
        g = jax.nn.silu(x @ Wg)
        o = o.reshape(B, N, VALUE_DIM) * g
        return o @ Wo

    def _L1_ffn_ref(x, Wqkv, q_scale, k_scale, Wo, ln_g, ln_b, W1, b1, W2, b2):
        import jax, jax.numpy as jnp
        import numpy as np
        DIM = 128
        DEPTH = 6
        HEADS = 16
        DIM_HEAD = 64
        WINDOW = 32
        INNER = HEADS * DIM_HEAD
        DIM_INNER = int(DIM * 4 * 2 / 3)
        QK_SCALE = 8.0

        def shift_tokens(t):
            a, s = jnp.split(t, 2, -1)
            s = jnp.pad(s, ((0, 0), (1, 0), (0, 0)))[:, :-1]
            return jnp.concatenate([a, s], -1)

        def l2norm(t):
            return t / jnp.maximum(jnp.linalg.norm(t, axis=-1, keepdims=True), 1e-12)

        def rotate_half(x):
            x1, x2 = jnp.split(x, 2, -1)
            return jnp.concatenate([-x2, x1], -1)

        def rotary_tables(n):
            half = jnp.arange(0, DIM_HEAD, 2, dtype=jnp.float32)
            inv_freq = 1.0 / 10000.0 ** (half / DIM_HEAD)
            t = jnp.arange(n, dtype=jnp.float32)
            freqs = t[:, None] * inv_freq[None, :]
            freqs = jnp.concatenate([freqs, freqs], -1)
            base_scale = (half + 0.4 * DIM_HEAD) / (1.4 * DIM_HEAD)
            power = (t - n // 2) / (WINDOW // 2)
            scale = base_scale[None, :] ** power[:, None]
            scale = jnp.concatenate([scale, scale], -1)
            return (freqs, scale)

        def local_attention(q, k, v):
            b, h, n, d = q.shape
            w = WINDOW
            nw = n // w
            bq = q.reshape(b, h, nw, w, d)
            bk = k.reshape(b, h, nw, w, d)
            bv = v.reshape(b, h, nw, w, d)

            def look(t):
                p = jnp.pad(t, ((0, 0), (0, 0), (1, 0), (0, 0), (0, 0)))
                return jnp.concatenate([p[:, :, :nw], p[:, :, 1:]], axis=3)
            bk2, bv2 = (look(bk), look(bv))
            seq = jnp.arange(n).reshape(nw, w)
            seq_p = jnp.pad(seq, ((1, 0), (0, 0)), constant_values=-1)
            jt = jnp.concatenate([seq_p[:nw], seq_p[1:]], axis=1)
            it = seq[:, :, None]
            jb = jt[:, None, :]
            mask = (it < jb) | (it > jb + w) | (jb == -1)
            sim = jnp.einsum('bhwie,bhwje->bhwij', bq, bk2) * QK_SCALE
            sim = jnp.where(mask, -jnp.finfo(sim.dtype).max, sim)
            attn = jax.nn.softmax(sim, -1)
            out = jnp.einsum('bhwij,bhwje->bhwie', attn, bv2)
            return out.reshape(b, h, n, d)

        def attn_layer(x, Wqkv, qs, ksc, Wo):
            b, n, _ = x.shape
            qkv = x @ Wqkv
            q, k, v = jnp.split(qkv, 3, -1)
            sh = lambda t: t.reshape(b, n, HEADS, DIM_HEAD).transpose(0, 2, 1, 3)
            q, k, v = (sh(q), sh(k), sh(v))
            q = l2norm(q) * qs
            k = l2norm(k) * ksc
            freqs, scale = rotary_tables(n)
            cos, sin = (jnp.cos(freqs), jnp.sin(freqs))
            q = q * cos * scale + rotate_half(q) * sin * scale
            inv = 1.0 / scale
            k = k * cos * inv + rotate_half(k) * sin * inv
            out = local_attention(q, k, v)
            out = out.transpose(0, 2, 1, 3).reshape(b, n, INNER)
            return out @ Wo

        def ffn_layer(x, g, bln, W1, b1, W2, b2):
            mu = x.mean(-1, keepdims=True)
            var = ((x - mu) ** 2).mean(-1, keepdims=True)
            xn = (x - mu) / jnp.sqrt(var + 1e-05) * g + bln
            hg = xn @ W1 + b1
            a, gate = jnp.split(hg, 2, -1)
            return a * jax.nn.gelu(gate, approximate=False) @ W2 + b2
        for i in range(DEPTH):
            x = attn_layer(shift_tokens(x), Wqkv[i], q_scale[i], k_scale[i], Wo[i]) + x
            x = ffn_layer(shift_tokens(x), ln_g[i], ln_b[i], W1[i], b1[i], W2[i], b2[i]) + x
        return x
    x = L0_attn_x
    x = x + _L0_attn_ref(_layernorm(x, axis=-1), L0_attn_Wq, L0_attn_Wk, L0_attn_Wv, L0_attn_Wo)
    x = x + _L0_ffn_ref(_layernorm(x, axis=-1), L0_ffn_Wr, L0_ffn_A, L0_ffn_Bw)
    x = x + _L1_attn_ref(_layernorm(x, axis=-1), L1_attn_Wq, L1_attn_Wk, L1_attn_Wv, L1_attn_Wg, L1_attn_Wo, L1_attn_gn_weight)
    x = x + _L1_ffn_ref(_layernorm(x, axis=-1), L1_ffn_Wqkv, L1_ffn_q_scale, L1_ffn_k_scale, L1_ffn_Wo, L1_ffn_ln_g, L1_ffn_ln_b, L1_ffn_W1, L1_ffn_b1, L1_ffn_W2, L1_ffn_b2)
    return x

_drawn_inputs = setup_inputs


def setup_inputs(seed=0):
    import zlib

    import numpy as np

    out = dict(_drawn_inputs(seed))
    spreads = {'L1_attn_gn_weight': (1.0, 0.6),
     'L1_ffn_q_scale': (1.0, 0.6),
     'L1_ffn_k_scale': (1.0, 0.6),
     'L1_ffn_ln_g': (1.0, 0.6),
     'L1_ffn_ln_b': (0.0, 0.8),
     'L1_ffn_b1': (0.0, 0.8),
     'L1_ffn_b2': (0.0, 0.293)}
    factors = {'L1_attn_Wq': 3.101,
     'L1_attn_Wk': 3.102,
     'L1_attn_Wv': 3.083,
     'L1_attn_Wg': 3.136,
     'L1_attn_Wo': 3.112,
     'L1_ffn_W1': 5.744,
     'L1_ffn_W2': 5.643}
    for name, (base, spread) in spreads.items():
        noise = np.random.default_rng([zlib.crc32(name.encode()), seed]).standard_normal(out[name].shape)
        drawn = base * np.exp(spread * noise) if base else spread * noise
        out[name] = jnp.asarray(drawn.astype(out[name].dtype))
    for name, factor in factors.items():
        out[name] = (out[name] * factor).astype(out[name].dtype)
    return out
```

```python
from contextlib import ExitStack

import numpy as np

import concourse.bass as bass
from concourse import mybir

F32 = mybir.dt.float32
ALU = mybir.AluOpType
ACT = mybir.ActivationFunctionType
AX = mybir.AxisListType.X

P = 128
B, T, D = 16, 256, 128
PAD = 40
TILES = T // P
NEG = -1e30
EPS = 1e-5

CH = 512
NCH = B * T // CH
ROW = 4
PER = CH // T

AH, AD = 16, 8
A_SCALE = 1.0 / float(np.sqrt(np.float32(AD)))

E, R = 8, 64
EC = E * R // P

RH, RK, RV = 4, 32, 64

DEPTH, WH, WD, WIN = 6, 16, 64, 32
INNER = WH * WD
HALF = 8
STEPS = TILES * (WH // HALF)
NPAIR = HALF // 2
NWIN = P // WIN
MLP = 341
MC, MG = 114, 3

COUNTED = """
ln_copied ln_mean ln_centred ln_squared ln_var ln_logged ln_inverse ln_scaled
a_xcopy a_proj a_vproj a_qmasked a_ktaken a_vtaken a_scored a_masked a_maxed a_biased a_exped a_turned a_taken
a_summed a_totalled a_odone a_oturned a_otaken a_wo_done a_added
e_gated e_mixed e_made e_applied e_added
r_xcopy r_qk r_vg r_qktaken r_rotated r_vgtaken r_scored r_decayed r_summed r_squared r_ssum r_inv r_chain
r_gated r_turned r_took r_wo r_added r_ready
w_shifted0 w_shifted1 w_qk w_q_squared w_k_squared w_k_rotated w_q_rotated w_sums w_guarded w_added w_rnorm
w_normed w_turned w_k_turned w_q_turned w_v_made w_v_taken w_scored w_masked w_maxed w_lowered w_exped w_totals
w_inverse w_p_turned w_p_taken w_valued w_divided w_o_turned w_o_taken w_projected w_residual w_ready w_tabled
m_up m_gelued m_made m_down m_residual
""".split()


def passed(count):
    return count + 1


def scoped(phase):
    def run(nc, sem, *args):
        with ExitStack() as stack:
            phase(nc, sem, lambda name, shape: stack.enter_context(nc.sbuf_tensor(name, shape, F32)), *args)
    return run


def program(nc, h, out):
    def sb(name, shape):
        return nc.alloc_sbuf_tensor(name, shape, F32)

    sems = {}

    def sem(name):
        if name not in sems:
            sems[name] = nc.alloc_semaphore(name)
        return sems[name]

    xT = sb("xT", [P, B + 1, PAD + T])
    ident = sb("ident", [P, P])
    mean_w = sb("mean_w", [P, P])
    norm = sb("norm", [P, B * T])
    logv = sb("logv", [P, B * T])
    eps_col = sb("eps_col", [P, 1])
    banks = nc.alloc_psum_tensor("banks", [P, 8, 512], F32)

    a_w = sb("a_w", [P, 4, P])
    a_hm = sb("a_hm", [P, 4])
    a_mask = sb("a_mask", [P, 2, P])
    e_wr = sb("e_wr", [P, E])
    e_a = sb("e_a", [P, EC, P])
    e_b = sb("e_b", [P, EC, P])
    e_spread = sb("e_spread", [E, EC * P])
    e_before = sb("e_before", [B, E, E])
    r_w = sb("r_w", [P, 4, P])
    r_wv = sb("r_wv", [P, RH * RV])
    r_wg = sb("r_wg", [P, RH * RV])
    r_wo = sb("r_wo", [P, 2, P])
    r_gn = sb("r_gn", [P, RV])
    r_tab = sb("r_tab", [P, 2, 2, T])
    r_decay = sb("r_decay", [P, RH, T])

    w_qkv = sb("w_qkv", [P, 3 * INNER])
    w_o = sb("w_o", [P, WH // 2, P])
    w_base = sb("w_base", [P, 2 * TILES, 2 * WD])
    w_scl = sb("w_scl", [P, 2 * WD])
    w_tab = sb("w_tab", [P, 2 * TILES, 2 * WD])
    w_mask = sb("w_mask", [P, TILES, 2 * WIN])
    m_w1 = sb("m_w1", [P, 2 * MG, MC])
    m_w2 = sb("m_w2", [MC, MG, P])
    m_col = sb("m_col", [P, 3 + 2 * MG])

    loaded = sem("loaded")
    n_loads = [0]

    with nc.Block() as block:
        @block.sync
        def _(sp):
            def load(dst, src):
                sp.dma_start(dst, src).then_inc(loaded, 16)
                n_loads[0] += 1
            for b in range(0, B, 4):
                load(xT[:, b:b + 4, PAD:], h["x"][:, b:b + 4, :])
            for dst, name in ((ident, "ident"), (a_w, "a_w"), (a_hm, "a_hm"), (a_mask, "a_mask"),
                              (e_wr, "e_wr"), (e_a, "e_a"), (e_b, "e_b"), (e_spread, "e_spread"),
                              (r_w, "r_w"), (r_wv, "r_wv"), (r_wg, "r_wg"), (r_wo, "r_wo"),
                              (r_tab, "r_tab"), (r_decay, "r_decay"), (w_base, "w_base"),
                              (w_mask, "w_mask")):
                load(dst[:], h[name])
            load(e_before[:], h["e_before"].partition_broadcast(B))
            load(r_gn[:], h["r_gn"].partition_broadcast(P))
            load_window_weights(sp, sem("w_weights"), h, 0, w_qkv, w_o, w_scl)
            for name in COUNTED:
                sp.sem_inc(sem(name), 1)
            sp.wait_ge(loaded, 16 * n_loads[0])

        @block.vector
        def _(dve):
            nc.vector.memset(xT[:, :, 0:PAD], 0.0)
            nc.vector.memset(xT[:, B, PAD:], 0.0)
            nc.vector.memset(mean_w[:], 1.0 / D)
            nc.vector.memset(eps_col[:], EPS)

    layer_norm(nc, sem, 0, False, xT, norm, logv, mean_w, eps_col, banks, None)
    head_attention(nc, sem, xT, norm, banks, ident, a_w, a_hm, a_mask)
    layer_norm(nc, sem, 1, False, xT, norm, logv, mean_w, eps_col, banks, None)
    experts(nc, sem, xT, norm, banks, ident, e_wr, e_a, e_b, e_spread, e_before)
    layer_norm(nc, sem, 2, False, xT, norm, logv, mean_w, eps_col, banks, None)
    retention(nc, sem, xT, norm, logv, banks, ident, eps_col, r_w, r_wv, r_wg, r_wo, r_gn, r_tab, r_decay)

    layer_norm(nc, sem, 3, False, xT, norm, logv, mean_w, eps_col, banks, None)
    kept = sb("kept", [P, B, T])
    moved = sem("moved")
    with nc.Block() as block:
        @block.vector
        def _(dve):
            for b in range(0, B, PER):
                nc.vector.tensor_copy(kept[:, b:b + PER, :], xT[:, b:b + PER, PAD:PAD + T]).then_inc(moved, 1)

        @block.scalar
        def _(act):
            for b in range(0, B, PER):
                act.wait_ge(moved, b // PER + 1)
                nc.scalar.activation(xT[:, b:b + PER, PAD:PAD + T],
                                     norm[:, b * T:(b + PER) * T].rearrange("p (b t) -> p b t", b=PER), ACT.Copy)

    with nc.Fori(0, DEPTH) as layer:
        window_attention(nc, sem, layer, h, xT, norm, logv, banks, ident, w_qkv, w_o, w_base, w_scl, w_tab,
                         w_mask, m_w1, m_w2, m_col)
        layer_norm(nc, sem, layer + 4, True, xT, norm, logv, mean_w, eps_col, banks, m_col)
        gated_mlp(nc, sem, layer, h, xT, norm, banks, m_w1, m_w2, m_col, w_qkv, w_o, w_scl)

    stored, summed = sem("stored"), sem("summed")
    with nc.Block() as block:
        @block.vector
        def _(dve):
            for b in range(0, B, PER):
                nc.vector.tensor_tensor(kept[:, b:b + PER, :], kept[:, b:b + PER, :], xT[:, b:b + PER, PAD:PAD + T],
                                        ALU.add).then_inc(summed, 1)

        @block.sync
        def _(sp):
            for b in range(0, B, PER):
                sp.wait_ge(summed, b // PER + 1)
                sp.dma_start(out[:, b:b + PER, :], kept[:, b:b + PER, :]).then_inc(stored, 16)
            sp.wait_ge(stored, 16 * (B // PER))


def layer_norm(nc, sem, turn, mlp, xT, norm, logv, mean_w, eps_col, banks, col):
    copied, mean_in, centred = sem("ln_copied"), sem("ln_mean"), sem("ln_centred")
    squared, var_in, logged = sem("ln_squared"), sem("ln_var"), sem("ln_logged")
    inverse, scaled = sem("ln_inverse"), sem("ln_scaled")
    done = NCH * turn

    def chunk(buf, c):
        return buf[:, bass.ds(c * CH, CH)]

    with nc.Block() as block:
        @block.gpsimd
        def _(pool):
            with pool.Fori(0, NCH) as c:
                dst = chunk(norm, c).rearrange("p (b t) -> p b t", b=PER)
                if mlp:
                    nc.gpsimd.tensor_copy(dst[0:64], xT[0:64, bass.ds(c * PER, PER), PAD:PAD + T]).then_inc(copied, 1)
                    pool.wait_ge(copied, passed((done + c) * 2 + 1))
                    pool.sem_inc(sem("gate"), 1)
                    nc.gpsimd.tensor_copy(dst[64:P], xT[64:P, bass.ds(c * PER, PER), PAD - 1:PAD + T - 1])\
                        .then_inc(copied, 1)
                    pool.wait_ge(copied, passed((done + c) * 2 + 2))
                else:
                    nc.gpsimd.tensor_copy(dst, xT[:, bass.ds(c * PER, PER), PAD:PAD + T]).then_inc(copied, 2)

        @block.tensor
        def _(pe):
            with pe.Fori(0, NCH // ROW) as i:
                for k in range(ROW):
                    c = i * ROW + k
                    pe.wait_ge(copied, passed((done + c) * 2 + 2))
                    pe.wait_ge(centred, passed(done + i * ROW))
                    nc.tensor.matmul(banks[:, k, :], mean_w[:], chunk(norm, c), start=True, stop=True)\
                        .then_inc(mean_in, 1)
                for k in range(ROW):
                    c = i * ROW + k
                    pe.wait_ge(squared, passed(done + c + 1))
                    pe.wait_ge(logged, passed(done + i * ROW))
                    nc.tensor.matmul(banks[:, ROW + k, :], mean_w[:], chunk(logv, c), start=True, stop=True)\
                        .then_inc(var_in, 1)

        @block.vector
        def _(dve):
            with dve.Fori(0, NCH // ROW) as i:
                for k in range(ROW):
                    c = i * ROW + k
                    dve.wait_ge(mean_in, passed(done + c + 1))
                    nc.vector.tensor_tensor(chunk(norm, c), chunk(norm, c), banks[:, k, :], ALU.subtract)\
                        .then_inc(centred, 1)
            with dve.Fori(0, NCH) as c:
                dve.wait_ge(inverse, passed(done + c + 1))
                dve.wait_ge(centred, passed(done + NCH))
                nc.vector.tensor_tensor(chunk(norm, c), chunk(norm, c), chunk(logv, c), ALU.mult).then_inc(scaled, 1)
                if mlp:
                    dve.wait_ge(scaled, passed(done + c + 1))
                    nc.vector.tensor_scalar(chunk(norm, c), chunk(norm, c), col[:, 0:1], col[:, 1:2],
                                            ALU.mult, ALU.add)

        @block.scalar
        def _(act):
            with act.Fori(0, NCH // ROW) as i:
                for k in range(ROW):
                    c = i * ROW + k
                    act.wait_ge(centred, passed(done + c + 1))
                    act.sem_inc(sem("gate"), 1)
                    nc.scalar.activation(chunk(logv, c), chunk(norm, c), ACT.Square).then_inc(squared, 1)
                for k in range(ROW):
                    c = i * ROW + k
                    act.wait_ge(var_in, passed(done + c + 1))
                    act.sem_inc(sem("gate"), 1)
                    nc.scalar.activation(chunk(logv, c), banks[:, ROW + k, :], ACT.Ln, bias=eps_col[:])\
                        .then_inc(logged, 1)
            act.wait_ge(logged, passed(done + NCH))
            act.sem_inc(sem("gate"), 1)
            with act.Fori(0, NCH // ROW) as i:
                for k in range(ROW):
                    c = i * ROW + k
                    nc.scalar.activation(chunk(logv, c), chunk(logv, c), ACT.Exp, scale=-0.5).then_inc(inverse, 1)


@scoped
def head_attention(nc, sem, sb, xT, norm, banks, ident, w, head_mask, mask):
    xa = sb("a_x", [P, T])
    qm = sb("a_qm", [P, 4, T])
    kT = sb("a_kT", [P, T])
    v = sb("a_v", [P, TILES, P])
    KEYS = [P, 2 * P]
    probs = [sb(f"a_probs{i}", [P, 4 * 3 * P]) for i in range(2)]
    probsT = [sb(f"a_probsT{i}", [P, 12, P]) for i in range(2)]
    mx = sb("a_max", [P, 2, 8])
    bias = sb("a_bias", [P, 2, 8])
    total = sb("a_total", [P, 4, 2, 4])
    rtotal = sb("a_rtotal", [P, 4, 2, 4])
    o = sb("a_o", [P, TILES, P])
    oT = sb("a_oT", [P, T])

    xcopy, proj, vproj = sem("a_xcopy"), sem("a_proj"), sem("a_vproj")
    qmasked, ktaken, vtaken = sem("a_qmasked"), sem("a_ktaken"), sem("a_vtaken")
    scored, masked, maxed, biased = sem("a_scored"), sem("a_masked"), sem("a_maxed"), sem("a_biased")
    exped, turned, taken, summed = sem("a_exped"), sem("a_turned"), sem("a_taken"), sem("a_summed")
    totalled, odone, oturned, otaken = sem("a_totalled"), sem("a_odone"), sem("a_oturned"), sem("a_otaken")
    wo_done, added = sem("a_wo_done"), sem("a_added")

    def part(buf, tile):
        lo = 0 if tile == 0 else 4 * P
        return buf[:, lo:lo + 4 * KEYS[tile]].rearrange("p (s k) -> p s k", s=4)

    def score_bank(tile):
        if tile == 0:
            return banks[:, 2, :].rearrange("p (s k) -> p s k", s=4)
        return banks[:, 3:5, :].rearrange("p b (s k) -> p (b s) k", s=2)

    with nc.Block() as block:
        @block.gpsimd
        def _(pool):
            with pool.Fori(0, B) as b:
                pool.wait_ge(vproj, passed(b))
                pool.sem_inc(sem("gate"), 1)
                nc.gpsimd.tensor_copy(xa[:], norm[:, bass.ds(b * T, T)]).then_inc(xcopy, 1)

        @block.tensor
        def _(pe):
            with pe.Fori(0, B) as b:
                pe.wait_ge(added, passed(b))
                pe.wait_ge(xcopy, passed(b + 1))
                nc.tensor.matmul(banks[:, 0, 0:T], w[:, 0, :], xa[:], start=True, stop=True)
                nc.tensor.matmul(banks[:, 0, T:2 * T], w[:, 1, :], xa[:], start=True, stop=True).then_inc(proj, 1)
                pe.wait_ge(odone, passed(b))
                for t in range(TILES):
                    last = nc.tensor.matmul(banks[:, 1, t * P:(t + 1) * P], xa[:, t * P:(t + 1) * P], w[:, 2, :],
                                            start=True, stop=True)
                last.then_inc(vproj, 1)

                def scores(r):
                    if r == 0:
                        pe.wait_ge(qmasked, passed(b + 1))
                        pe.wait_ge(ktaken, passed(b + 1))
                    pe.wait_ge(masked, passed((b * 4 + r) * 2))
                    rows = slice(32 * r, 32 * r + 32)
                    for t in range(TILES):
                        for s in range(4):
                            last = nc.tensor.matmul(score_bank(t)[:, s, :], qm[rows, s, t * P:(t + 1) * P],
                                                    kT[rows, 0:KEYS[t]], start=True, stop=True)
                    last.then_inc(scored, 1)

                def values(r):
                    n = b * 4 + r
                    pe.wait_ge(exped, passed(n + 1))
                    pe.wait_ge(taken, passed(n * 2))
                    for j in range(12):
                        last = nc.tensor.transpose(banks[:, 5 + j // 4, (j % 4) * P:(j % 4 + 1) * P],
                                                   probs[r % 2][:, j * P:(j + 1) * P], ident[:])
                    last.then_inc(turned, 1)
                    if r == 0:
                        pe.wait_ge(vtaken, passed(b + 1))
                    pe.wait_ge(taken, passed(n * 2 + 2))
                    pt = probsT[r % 2]
                    for s in range(4):
                        hd = 4 * r + s
                        cols = slice(hd * AD, (hd + 1) * AD)
                        nc.tensor.matmul(banks[:, 1, T + hd * AD:T + (hd + 1) * AD], pt[:, s, :], v[:, 0, cols],
                                         start=True, stop=True)
                        for k in range(2):
                            last = nc.tensor.matmul(banks[:, 1, T + P + hd * AD:T + P + (hd + 1) * AD],
                                                    pt[:, 4 + 2 * s + k, :], v[:, k, cols],
                                                    start=(k == 0), stop=(k == 1))
                    last.then_inc(summed, 1)

                scores(0)
                for r in range(4):
                    if r < 3:
                        scores(r + 1)
                    values(r)
                pe.wait_ge(odone, passed(b + 1))
                for t in range(TILES):
                    last = nc.tensor.transpose(banks[:, 0, t * P:(t + 1) * P], o[:, t, :], ident[:])
                last.then_inc(oturned, 1)
                pe.wait_ge(otaken, passed(b + 1))
                nc.tensor.matmul(banks[:, 0, T:2 * T], w[:, 3, :], oT[:], start=True, stop=True).then_inc(wo_done, 1)

        @block.vector
        def _(dve):
            with dve.Fori(0, B) as b:
                dve.wait_ge(proj, passed(b + 1))
                nc.vector.tensor_tensor(qm[:], banks[:, 0, 0:T].unsqueeze(1).broadcast_to([P, 4, T]),
                                        head_mask[:].unsqueeze(2).broadcast_to([P, 4, T]), ALU.mult)\
                    .then_inc(qmasked, 1)

                def softmax(r):
                    n = b * 4 + r
                    if r >= 2:
                        dve.wait_ge(turned, passed(n - 1))
                    else:
                        dve.wait_ge(turned, passed(b * 4))
                    dve.wait_ge(scored, passed(n + 1))
                    nc.vector.tensor_tensor(part(probs[r % 2], 0), score_bank(0),
                                            mask[:, 1, :].unsqueeze(1).broadcast_to([P, 4, P]), ALU.add)\
                        .then_inc(masked, 1)
                    nc.vector.tensor_tensor(part(probs[r % 2], 1), score_bank(1),
                                            mask[:].rearrange("p a k -> p (a k)").unsqueeze(1)
                                            .broadcast_to([P, 4, 2 * P]), ALU.add).then_inc(masked, 1)
                    dve.wait_ge(masked, passed(n * 2 + 2))
                    for t in range(TILES):
                        nc.vector.tensor_reduce(mx[:, r % 2, t * 4:t * 4 + 4], part(probs[r % 2], t), AX, ALU.max)\
                            .then_inc(maxed, 1)
                    dve.wait_ge(maxed, passed(n * 2 + 2))
                    nc.vector.tensor_scalar(bias[:, r % 2, :], mx[:, r % 2, :], -A_SCALE, None, ALU.mult)\
                        .then_inc(biased, 1)

                def take(r):
                    n = b * 4 + r
                    dve.wait_ge(turned, passed(n + 1))
                    nc.vector.tensor_copy(probsT[r % 2][:, 4:12, :].rearrange("p j q -> p (j q)"),
                                          banks[:, 6:8, :].rearrange("p b c -> p (b c)")).then_inc(taken, 1)

                softmax(0)
                for r in range(4):
                    if r < 3:
                        softmax(r + 1)
                    take(r)
                dve.wait_ge(exped, passed(b * 4 + 4))
                nc.vector.reciprocal(rtotal[:], total[:]).then_inc(totalled, 1)
                dve.wait_ge(summed, passed(b * 4 + 4))
                dve.wait_ge(totalled, passed(b + 1))
                for t in range(TILES):
                    last = nc.vector.tensor_tensor(
                        o[:, t, :].rearrange("p (r s d) -> p r s d", r=4, s=4),
                        banks[:, 1, T + t * P:T + (t + 1) * P].rearrange("p (r s d) -> p r s d", r=4, s=4),
                        rtotal[:, :, t, :].unsqueeze(3).broadcast_to([P, 4, 4, AD]), ALU.mult)
                last.then_inc(odone, 1)
                dve.wait_ge(wo_done, passed(b + 1))
                rows = xT[:, bass.ds(b, 1), PAD:PAD + T].rearrange("p b t -> p (b t)")
                nc.vector.tensor_tensor(rows, rows, banks[:, 0, T:2 * T], ALU.add).then_inc(added, 1)

        @block.scalar
        def _(act):
            with act.Fori(0, B) as b:
                act.wait_ge(qmasked, passed(b + 1))
                nc.scalar.activation(kT[:], banks[:, 0, T:2 * T], ACT.Copy).then_inc(ktaken, 1)
                act.wait_ge(vproj, passed(b + 1))
                nc.scalar.activation(v[:].rearrange("p t n -> p (t n)"), banks[:, 1, 0:T], ACT.Copy)\
                    .then_inc(vtaken, 1)

                def exps(r):
                    n = b * 4 + r
                    act.wait_ge(biased, passed(n + 1))
                    for t in range(TILES):
                        for s in range(4):
                            i = t * 4 + s
                            last = nc.scalar.activation(part(probs[r % 2], t)[:, s, :], part(probs[r % 2], t)[:, s, :],
                                                        ACT.Exp, bias=bias[:, r % 2, i:i + 1], scale=A_SCALE,
                                                        accum_out=total[:, r, t, s:s + 1])
                    last.then_inc(exped, 1)

                def take(r):
                    act.wait_ge(turned, passed(b * 4 + r + 1))
                    nc.scalar.activation(probsT[r % 2][:, 0:4, :].rearrange("p j q -> p (j q)"), banks[:, 5, :],
                                         ACT.Copy).then_inc(taken, 1)

                exps(0)
                for r in range(4):
                    if r < 3:
                        exps(r + 1)
                    take(r)
                act.wait_ge(oturned, passed(b + 1))
                nc.scalar.activation(oT[:], banks[:, 0, 0:T], ACT.Copy).then_inc(otaken, 1)


@scoped
def experts(nc, sem, sb, xT, norm, banks, ident, wr, ea, eb, spread, before):
    lg = sb("e_lg", [B, E])
    top = sb("e_top", [B, 1])
    ahead = sb("e_ahead", [B, E, E])
    ties = sb("e_ties", [B, E, E])
    rank = sb("e_rank", [B, E])
    ex = sb("e_ex", [B, E])
    tot = sb("e_tot", [B, 1])
    gates = sb("e_gates", [B, E])
    gT = sb("e_gT", [E, B])
    gcol = sb("e_gcol", [P, EC, B])
    bg = [sb(f"e_bg{i}", [P, EC, P]) for i in range(2)]
    wb = [sb(f"e_wb{i}", [P, P]) for i in range(2)]
    chain, on_pe, on_act = sem("e_chain"), sem("e_pe"), sem("e_act")
    gated, mixed, made, applied, added = (sem("e_gated"), sem("e_mixed"), sem("e_made"), sem("e_applied"),
                                          sem("e_added"))
    steps = [0]

    with nc.Block() as block:
        @block.tensor
        def _(pe):
            first = norm[:].rearrange("p (b t) -> p b t", b=B)[:, :, 0]
            nc.tensor.matmul(banks[0:B, 4, 0:E], first, wr[:], start=True, stop=True).then_inc(on_pe, 1)
            pe.wait_ge(on_act, 2)
            nc.tensor.transpose(banks[0:E, 5, 0:B], gates[:], ident[0:B, 0:B]).then_inc(on_pe, 1)
            pe.wait_ge(on_act, 3)
            for c in range(EC):
                last = nc.tensor.matmul(banks[:, 6, c * B:(c + 1) * B], spread[:, c * P:(c + 1) * P], gT[:],
                                        start=True, stop=True)
            last.then_inc(on_pe, 1)
            with pe.Fori(0, B // 2) as i:
                for k in range(2):
                    b = i * 2 + k
                    pe.wait_ge(gated, passed(b + 1))
                    pe.wait_ge(made, passed(i * 2))
                    for c in range(EC):
                        last = nc.tensor.matmul(banks[:, k, 0:P], ea[:, c, :], bg[k][:, c, :],
                                                start=(c == 0), stop=(c == EC - 1))
                    last.then_inc(mixed, 1)
                for k in range(2):
                    b = i * 2 + k
                    pe.wait_ge(made, passed(b + 1))
                    pe.wait_ge(added, passed(i * 2))
                    nc.tensor.matmul(banks[:, 2 + k, 0:T], wb[k][:], norm[:, bass.ds(b * T, T)],
                                     start=True, stop=True).then_inc(applied, 1)

        @block.vector
        def _(dve):
            def link(ins):
                steps[0] += 1
                ins.then_inc(chain, 1)
                dve.wait_ge(chain, steps[0])
            dve.wait_ge(on_pe, 1)
            link(nc.vector.tensor_copy(lg[:], banks[0:B, 4, 0:E]))
            link(nc.vector.tensor_reduce(top[:], lg[:], AX, ALU.max))
            other, own = lg[:].unsqueeze(1).broadcast_to([B, E, E]), lg[:].unsqueeze(2).broadcast_to([B, E, E])
            link(nc.vector.tensor_tensor(ahead[:], other, own, ALU.is_gt))
            link(nc.vector.tensor_tensor(ties[:], other, own, ALU.is_equal))
            link(nc.vector.tensor_tensor(ties[:], ties[:], before[:], ALU.mult))
            link(nc.vector.tensor_tensor(ahead[:], ahead[:], ties[:], ALU.add))
            link(nc.vector.tensor_reduce(rank[:], ahead[:], AX, ALU.add))
            link(nc.vector.tensor_scalar(rank[:], rank[:], 2.0, None, ALU.is_lt))
            link(nc.vector.tensor_scalar(ex[:], lg[:], top[:], None, ALU.subtract))
            dve.wait_ge(on_act, 1)
            link(nc.vector.tensor_tensor(ex[:], ex[:], rank[:], ALU.mult))
            link(nc.vector.tensor_reduce(tot[:], ex[:], AX, ALU.add))
            link(nc.vector.reciprocal(tot[:], tot[:]))
            nc.vector.tensor_scalar(gates[:], ex[:], tot[:], None, ALU.mult).then_inc(on_act, 1)
            dve.wait_ge(on_pe, 2)
            nc.vector.tensor_copy(gT[:], banks[0:E, 5, 0:B]).then_inc(on_act, 1)
            dve.wait_ge(on_pe, 3)
            link(nc.vector.tensor_copy(gcol[:].rearrange("p c b -> p (c b)"), banks[:, 6, 0:EC * B]))
            with dve.Fori(0, B // 2) as i:
                for k in range(2):
                    b = i * 2 + k
                    dve.wait_ge(mixed, passed(i * 2))
                    nc.vector.tensor_tensor(bg[k][:], eb[:], gcol[:, :, bass.ds(b, 1)].broadcast_to([P, EC, P]),
                                            ALU.mult).then_inc(gated, 1)
                for k in range(2):
                    b = i * 2 + k
                    dve.wait_ge(mixed, passed(b + 1))
                    dve.wait_ge(applied, passed(i * 2))
                    nc.vector.tensor_tensor(wb[k][:], banks[:, k, 0:P], ident[:], ALU.add).then_inc(made, 1)
                for k in range(2):
                    b = i * 2 + k
                    dve.wait_ge(applied, passed(b + 1))
                    rows = xT[:, bass.ds(b, 1), PAD:PAD + T].rearrange("p b t -> p (b t)")
                    nc.vector.tensor_tensor(rows, rows, banks[:, 2 + k, 0:T], ALU.add).then_inc(added, 1)

        @block.scalar
        def _(act):
            act.wait_ge(chain, 9)
            nc.scalar.activation(ex[:], ex[:], ACT.Exp).then_inc(on_act, 1)


@scoped
def retention(nc, sem, sb, xT, norm, spare, banks, ident, eps_col, w, wv, wg, wo, gn, tab, decay):
    xa = sb("r_x", [P, T])
    rot = sb("r_rot", [P, 2, T])
    rot2 = sb("r_rot2", [P, 2, T])
    v = sb("r_v", [P, TILES, RH * RV])
    g = sb("r_g", [P, TILES, RH * RV])
    att = sb("r_att", [P, RH, 3, P])
    osb = sb("r_o", [P, TILES * RH, RV])
    osq = sb("r_osq", [P, TILES * RH, RV])
    ss = sb("r_ss", [P, TILES * RH])
    rs = sb("r_rs", [P, TILES * RH])
    power = sb("r_power", [P, TILES * RH])
    oT = sb("r_oT", [P, 2, T])
    NO = TILES * RH * RV
    xcopy, qk, vg, qktaken, rotated = sem("r_xcopy"), sem("r_qk"), sem("r_vg"), sem("r_qktaken"), sem("r_rotated")
    vgtaken, scored, decayed, summed = sem("r_vgtaken"), sem("r_scored"), sem("r_decayed"), sem("r_summed")
    otaken, squared, ssum, inv, chain = sem("r_otaken"), sem("r_squared"), sem("r_ssum"), sem("r_inv"), sem("r_chain")
    gated, turned, took, wo_done, added = sem("r_gated"), sem("r_turned"), sem("r_took"), sem("r_wo"), sem("r_added")
    ready = sem("r_ready")

    with nc.Block() as block:
        @block.gpsimd
        def _(pool):
            nc.gpsimd.memset(power[:], -0.5).then_inc(ready, 1)
            pool.wait_ge(ready, passed(1))
            with pool.Fori(0, B) as b:
                pool.wait_ge(vg, passed(b))
                pool.sem_inc(sem("gate"), 1)
                nc.gpsimd.tensor_copy(xa[:], norm[:, bass.ds(b * T, T)]).then_inc(xcopy, 1)
                pool.wait_ge(ssum, passed(b + 1))
                nc.gpsimd.tensor_tensor(rs[:], ss[:], power[:], ALU.pow).then_inc(inv, 1)

        @block.tensor
        def _(pe):
            with pe.Fori(0, B) as b:
                pe.wait_ge(xcopy, passed(b + 1))
                pe.wait_ge(added, passed(b))
                for j in range(4):
                    last = nc.tensor.matmul(banks[:, j % 2, (j // 2) * T:(j // 2 + 1) * T], w[:, j, :], xa[:],
                                            start=True, stop=True)
                last.then_inc(qk, 1)
                for t in range(TILES):
                    cols = slice(t * RH * RV, (t + 1) * RH * RV)
                    nc.tensor.matmul(banks[:, 2, cols], xa[:, t * P:(t + 1) * P], wv[:], start=True, stop=True)
                    last = nc.tensor.matmul(banks[:, 3, cols], xa[:, t * P:(t + 1) * P], wg[:], start=True, stop=True)
                last.then_inc(vg, 1)
                pe.wait_ge(rotated, passed(b + 1))
                for hd in range(RH):
                    rows = slice(hd * RK, (hd + 1) * RK)
                    nc.tensor.matmul(banks[:, 4 + hd, 0:2 * P], rot[rows, 1, 0:P], rot[rows, 0, :],
                                     start=True, stop=True)
                    last = nc.tensor.matmul(banks[:, 4 + hd, 2 * P:3 * P], rot[rows, 1, P:2 * P],
                                            rot[rows, 0, P:2 * P], start=True, stop=True)
                last.then_inc(scored, 1)
                pe.wait_ge(vgtaken, passed(b * 2 + 2))
                pe.wait_ge(decayed, passed(b * 2 + 2))
                for hd in range(RH):
                    cols = slice(hd * RV, (hd + 1) * RV)
                    nc.tensor.matmul(banks[:, 2, hd * RV:(hd + 1) * RV], att[:, hd, 0, :], v[:, 0, cols],
                                     start=True, stop=True)
                    for k in range(2):
                        last = nc.tensor.matmul(banks[:, 2, (RH + hd) * RV:(RH + hd + 1) * RV], att[:, hd, 1 + k, :],
                                                v[:, k, cols], start=(k == 0), stop=(k == 1))
                last.then_inc(summed, 1)
                pe.wait_ge(gated, passed(b + 1))
                for t in range(TILES):
                    for c in range(2):
                        last = nc.tensor.transpose(
                            banks[:, 0, (c * 2 + t) * P:(c * 2 + t + 1) * P],
                            osb[:, t * RH:(t + 1) * RH, :].rearrange("p h d -> p (h d)")[:, c * P:(c + 1) * P],
                            ident[:])
                last.then_inc(turned, 1)
                pe.wait_ge(took, passed(b + 1))
                for c in range(2):
                    last = nc.tensor.matmul(banks[:, 1, 0:T], wo[:, c, :], oT[:, c, :], start=(c == 0), stop=(c == 1))
                last.then_inc(wo_done, 1)

        @block.vector
        def _(dve):
            with dve.Fori(0, B) as b:
                dve.wait_ge(qk, passed(b + 1))
                nc.vector.tensor_tensor(rot[:].rearrange("p a t -> p (a t)"), banks[:, 0, :],
                                        tab[:, 0, :, :].rearrange("p a t -> p (a t)"), ALU.mult).then_inc(qktaken, 1)
                nc.vector.tensor_tensor(rot2[:].rearrange("p a t -> p (a t)"), banks[:, 1, :],
                                        tab[:, 1, :, :].rearrange("p a t -> p (a t)"), ALU.mult).then_inc(qktaken, 1)
                dve.wait_ge(qktaken, passed(b * 2 + 2))
                nc.vector.tensor_tensor(rot[:], rot[:], rot2[:], ALU.add).then_inc(rotated, 1)
                dve.wait_ge(scored, passed(b + 1))
                nc.vector.tensor_tensor(att[:, :, 0:2, :].rearrange("p h a q -> p h (a q)"), banks[:, 4:8, 0:2 * P],
                                        decay[:], ALU.mult).then_inc(decayed, 1)
                nc.vector.tensor_tensor(att[:, :, 2, :], banks[:, 4:8, 2 * P:3 * P], decay[:, :, 0:P], ALU.mult)\
                    .then_inc(decayed, 1)
                dve.wait_ge(squared, passed(b + 1))
                nc.vector.tensor_reduce(ss[:], osq[:], AX, ALU.add).then_inc(chain, 1)
                dve.wait_ge(chain, passed(b * 3 + 1))
                nc.vector.tensor_scalar(ss[:], ss[:], 1.0 / RV, EPS, ALU.mult, ALU.add).then_inc(ssum, 1)
                nc.vector.tensor_tensor(osb[:], banks[:, 2, :].rearrange("p (h d) -> p h d", d=RV),
                                        gn[:].unsqueeze(1).broadcast_to([P, TILES * RH, RV]), ALU.mult)\
                    .then_inc(chain, 1)
                dve.wait_ge(inv, passed(b + 1))
                dve.wait_ge(chain, passed(b * 3 + 2))
                nc.vector.tensor_tensor(osb[:], osb[:], rs[:].unsqueeze(2).broadcast_to([P, TILES * RH, RV]),
                                        ALU.mult).then_inc(chain, 1)
                dve.wait_ge(chain, passed(b * 3 + 3))
                nc.vector.tensor_tensor(osb[:].rearrange("p h d -> p (h d)"), osb[:].rearrange("p h d -> p (h d)"),
                                        g[:].rearrange("p t n -> p (t n)"), ALU.mult).then_inc(gated, 1)
                dve.wait_ge(wo_done, passed(b + 1))
                rows = xT[:, bass.ds(b, 1), PAD:PAD + T].rearrange("p b t -> p (b t)")
                nc.vector.tensor_tensor(rows, rows, banks[:, 1, 0:T], ALU.add).then_inc(added, 1)

        @block.scalar
        def _(act):
            with act.Fori(0, B) as b:
                act.wait_ge(vg, passed(b + 1))
                nc.scalar.activation(g[:].rearrange("p t n -> p (t n)"), banks[:, 3, :], ACT.Silu)\
                    .then_inc(vgtaken, 1)
                nc.scalar.activation(v[:].rearrange("p t n -> p (t n)"), banks[:, 2, :], ACT.Copy)\
                    .then_inc(vgtaken, 1)
                act.wait_ge(summed, passed(b + 1))
                nc.scalar.activation(osq[:].rearrange("p h d -> p (h d)"), banks[:, 2, :], ACT.Square)\
                    .then_inc(squared, 1)
                act.wait_ge(turned, passed(b + 1))
                nc.scalar.activation(oT[:].rearrange("p c t -> p (c t)"), banks[:, 0, :], ACT.Copy).then_inc(took, 1)


@scoped
def window_attention(nc, sem, sb, layer, h, xT, spare0, spare1, banks, ident, wqkv, wo, base, scl, tab, mask,
                     m_w1, m_w2, m_col):
    N = B * STEPS
    LAG = 3
    ADDED = (-2, -1, -1, 0)
    xs = [sb(f"w_xs{t}", [P, WIN + P]) for t in range(TILES)]
    sq = sb("w_sq", [P, 2, HALF, WD])
    t1 = [sb(f"w_t1{i}", [P, 2 * HALF * WD]) for i in range(2)]
    t2 = [sb(f"w_t2{i}", [P, 2 * HALF * WD]) for i in range(2)]
    ss = [sb(f"w_ss{i}", [P, 2 * HALF]) for i in range(2)]
    rn = [sb(f"w_rn{i}", [P, 2 * HALF]) for i in range(2)]
    power = sb("w_power", [P, 2 * HALF])
    qT = [sb(f"w_qT{i}", [P, NPAIR, P]) for i in range(2)]
    kT = sb("w_kT", [P, WH // 2, WIN + T])
    vd = [sb(f"w_vd{j}", [P, NWIN, NPAIR * WD]) for j in range(STEPS)]
    pr = [sb(f"w_pr{i}", [P, NPAIR, 2, 2 * WIN]) for i in range(2)]
    mx = [sb(f"w_mx{i}", [P, HALF]) for i in range(2)]
    tot = [sb(f"w_tot{i}", [P, HALF]) for i in range(2)]
    rl = [sb(f"w_rl{i}", [P, HALF]) for i in range(2)]
    prT = sb("w_prT", [P, NPAIR, P])
    on = [sb(f"w_on{i}", [P, NPAIR, 2, WD]) for i in range(2)]
    oT = [sb(f"w_oT{i}", [P, NPAIR, P]) for i in range(WH // HALF)]

    S = {n: sem("w_" + n) for n in (
        "weights mlp_weights shifted0 shifted1 qk q_squared k_squared k_rotated q_rotated sums guarded added rnorm normed turned "
        "k_turned q_turned v_made v_taken scored masked maxed lowered exped totals inverse p_turned p_taken "
        "valued divided o_turned o_taken projected residual ready tabled").split()}
    C = 2 * HALF * WD // 2

    def pairs(bank):
        return banks[:, bank:bank + 2, 0:NPAIR * WD].rearrange("p a (g d) -> p a g d", d=WD)

    def pipeline(eng, iteration):
        def one(j, seq, live):
            iteration(j, seq, lambda lag: layer * N + seq * STEPS + (j - lag + 1), live,
                      lambda k: layer * (B * TILES) + seq * TILES + k)
        for j in range(STEPS):
            one(j, 0, lambda lag: lag <= j)
        with eng.Fori(1, B) as seq:
            for j in range(STEPS):
                one(j, seq, lambda lag: True)
        for j in range(LAG):
            one(j, B, lambda lag: lag > j)

    with nc.Block() as block:
        @block.sync
        def _(sp):
            for dst, name in ((m_w1, "m_w1"), (m_w2, "m_w2"), (m_col, "m_col")):
                sp.dma_start(dst[:], h[name][bass.ds(layer, 1)].squeeze(0)).then_inc(S["mlp_weights"], 16)
            sp.wait_ge(S["mlp_weights"], layer * 48 + 48)
            sp.sem_inc(sem("gate"), 1)

        @block.gpsimd
        def _(pool):
            nc.gpsimd.memset(power[:], -0.5).then_inc(S["ready"], 1)
            nc.gpsimd.memset(kT[:, :, 0:WIN], 0.0).then_inc(S["ready"], 1)
            pool.wait_ge(S["ready"], passed(layer * 2 + 2))

            def shift(t, seq):
                src = xT[:, bass.ds(seq, 1), :].rearrange("p b t -> p (b t)")
                lo = PAD - WIN + t * P
                nc.gpsimd.tensor_copy(xs[t][0:64, :], src[0:64, lo:lo + WIN + P]).then_inc(S[f"shifted{t}"], 1)
                made = (layer * (B + 1 - t) + seq) * 2
                pool.wait_ge(S[f"shifted{t}"], passed(made + 1))
                pool.sem_inc(sem("gate"), 1)
                nc.gpsimd.tensor_copy(xs[t][64:P, :], src[64:P, lo - 1:lo - 1 + WIN + P])\
                    .then_inc(S[f"shifted{t}"], 1)
                pool.wait_ge(S[f"shifted{t}"], passed(made + 2))
                pool.sem_inc(sem("gate"), 1)

            pool.sem_inc(sem("gate"), 1)
            shift(0, 0)

            def iteration(j, seq, n, live, tiles):
                if live(0):
                    if j % 2 == 0:
                        if live(1):
                            pool.wait_ge(S["v_made"], passed(n(1) * 2))
                            pool.sem_inc(sem("gate"), 1)
                        if j == 0:
                            shift(1, seq)
                        else:
                            shift(0, seq + 1)
                    pool.wait_ge(S["q_rotated"], passed(n(0) * 2))
                    a, c = t1[j % 2], t2[j % 2]
                    v1 = a[:].rearrange("p (h s d) -> p h s d", s=2, d=WD // 2)
                    v2 = c[:].rearrange("p (h s d) -> p h s d", s=2, d=WD // 2)
                    nc.gpsimd.tensor_tensor(v1, v1, v2[:, :, ::-1, :], ALU.add).then_inc(S["added"], 1)
                    pool.wait_ge(S["guarded"], passed(n(0)))
                    nc.gpsimd.tensor_tensor(rn[j % 2][:], ss[j % 2][:], power[:], ALU.pow).then_inc(S["rnorm"], 1)
            pipeline(pool, iteration)

        @block.tensor
        def _(pe):
            pe.wait_ge(S["weights"], layer * 48 + 48)

            def iteration(j, seq, n, live, tiles):
                t, hh = j // 2, j % 2
                j1, j2, j3 = (j - 1) % STEPS, (j - 2) % STEPS, (j - 3) % STEPS
                x = xs[t]

                def values(a):
                    pe.wait_ge(S["v_taken"], passed((n(0) - 1) * 2 + a))
                    for w in (2 * a, 2 * a + 1):
                        for par in range(2):
                            cols = wqkv[:, 2 * INNER + hh * C:2 * INNER + (hh + 1) * C]\
                                .rearrange("p (g a d) -> p a g d", a=2, d=WD)[:, par]
                            lo = (w - 2 * a) * NPAIR * WD
                            last = nc.tensor.matmul(
                                banks[64 * par:64 * par + 64, 2, lo:lo + NPAIR * WD].rearrange("p (g d) -> p g d", d=WD),
                                x[:, WIN * w:WIN * (w + 2)], cols, start=True, stop=True)
                    last.then_inc(S["v_made"], 1)

                if live(0):
                    pe.wait_ge(S["k_squared"], passed(n(0) - 1))
                    pe.wait_ge(S["q_rotated"], passed((n(0) - 1) * 2))
                    if hh == 0:
                        pe.wait_ge(S[f"shifted{t}"], passed((layer * (B + 1 - t) + seq) * 2 + 2))
                    for i in range(2):
                        last = nc.tensor.matmul(banks[:, i, :], x[:, WIN:], wqkv[:, i * INNER + hh * C:i * INNER + (hh + 1) * C],
                                                start=True, stop=True)
                        last.then_inc(S["qk"], 1)
                if live(1):
                    pe.wait_ge(S["normed"], passed(n(1)))
                    if live(3):
                        pe.wait_ge(S["divided"], passed(n(3)))
                    for i in range(2):
                        for g in range(NPAIR):
                            lo = i * C + g * P
                            last = nc.tensor.transpose(banks[:, 3 + i, g * P:(g + 1) * P], t1[j1 % 2][:, lo:lo + P],
                                                       ident[:])
                        last.then_inc(S["turned"], 1)
                if live(0):
                    values(0)
                if live(2):
                    pe.wait_ge(S["inverse"], passed(n(2)))
                    if live(3):
                        pe.wait_ge(S["residual"], passed(tiles(ADDED[j])))
                    if live(4):
                        pe.wait_ge(S["o_taken"], passed(n(4)))
                    for g in range(NPAIR):
                        last = nc.tensor.transpose(banks[:, 7, g * P:(g + 1) * P],
                                                   pr[j2 % 2][:, g].rearrange("p a k -> p (a k)"), ident[:])
                    last.then_inc(S["p_turned"], 1)
                if live(1):
                    pe.wait_ge(S["k_turned"], passed(n(1)))
                    pe.wait_ge(S["q_turned"], passed(n(1)))
                    if live(2):
                        pe.wait_ge(S["masked"], passed(n(2)))
                    pe.sem_inc(sem("gate"), 1)
                    tk, hk = j1 // 2, j1 % 2
                    for par in range(2):
                        rows = slice(64 * par, 64 * par + 64)
                        for g in range(NPAIR):
                            for w in range(NWIN):
                                last = nc.tensor.matmul(
                                    banks[WIN * w:WIN * (w + 1), 5 + par, g * WD:(g + 1) * WD],
                                    qT[j1 % 2][rows, g, WIN * w:WIN * (w + 1)],
                                    kT[rows, hk * NPAIR + g, tk * P + WIN * w:tk * P + WIN * (w + 2)],
                                    start=True, stop=True)
                    last.then_inc(S["scored"], 1)
                if live(0):
                    values(1)
                if live(2):
                    pe.wait_ge(S["p_taken"], passed(n(2)))
                    pe.wait_ge(S["v_taken"], passed(n(2) * 2))
                    pe.sem_inc(sem("gate"), 1)
                    for par in range(2):
                        rows = slice(64 * par, 64 * par + 64)
                        for g in range(NPAIR):
                            for w in range(NWIN):
                                last = nc.tensor.matmul(
                                    banks[WIN * w:WIN * (w + 1), 3 + par, g * WD:(g + 1) * WD],
                                    prT[rows, g, WIN * w:WIN * (w + 1)], vd[j2][rows, w, g * WD:(g + 1) * WD],
                                    start=True, stop=True)
                    last.then_inc(S["valued"], 1)
                if live(3):
                    if live(2):
                        pe.wait_ge(S["p_taken"], passed(n(2)))
                    else:
                        pe.wait_ge(S["o_taken"], passed(n(4)))
                        pe.wait_ge(S["residual"], passed(tiles(ADDED[j])))
                    pe.wait_ge(S["divided"], passed(n(3)))
                    for g in range(NPAIR):
                        last = nc.tensor.transpose(banks[:, 7, g * P:(g + 1) * P],
                                                   on[j3 % 2][:, g].rearrange("p a d -> p (a d)"), ident[:])
                    last.then_inc(S["o_turned"], 1)
                    if j3 % 2 == 1:
                        pe.wait_ge(S["o_taken"], passed(n(3)))
                        for g in range(WH // 2):
                            last = nc.tensor.matmul(banks[:, 7, 0:P], wo[:, g, :], oT[g // NPAIR][:, g % NPAIR, :],
                                                    start=(g == 0), stop=(g == WH // 2 - 1))
                        last.then_inc(S["projected"], 1)
            pipeline(pe, iteration)

        @block.vector
        def _(dve):
            dve.wait_ge(S["weights"], layer * 48 + 48)
            nc.vector.tensor_tensor(tab[:], base[:], scl[:].unsqueeze(1).broadcast_to([P, 2 * TILES, 2 * WD]),
                                    ALU.mult).then_inc(S["tabled"], 1)
            dve.wait_ge(S["tabled"], passed(layer + 1))

            def iteration(j, seq, n, live, tiles):
                t = j // 2
                j1, j2, j3 = (j - 1) % STEPS, (j - 2) % STEPS, (j - 3) % STEPS
                if live(1):
                    dve.wait_ge(S["rnorm"], passed(n(1)))
                    dve.wait_ge(S["added"], passed(n(1)))
                    v1 = t1[j1 % 2][:].rearrange("p (h d) -> p h d", d=WD)
                    nc.vector.tensor_tensor(v1, v1, rn[j1 % 2][:].unsqueeze(2).broadcast_to([P, 2 * HALF, WD]),
                                            ALU.mult).then_inc(S["normed"], 1)
                if live(0):
                    for i, name in ((1, "k_rotated"), (0, "q_rotated")):
                        if i == 1:
                            dve.wait_ge(S["qk"], passed(n(0) * 2))
                            if live(2):
                                dve.wait_ge(S["turned"], passed(n(2) * 2))
                        else:
                            dve.wait_ge(S["q_squared"], passed(n(0)))
                        src = banks[:, i, :].rearrange("p (h d) -> p h d", d=WD)
                        for cs, dst in ((0, t1), (1, t2)):
                            nc.vector.tensor_tensor(
                                dst[j % 2][:, i * C:(i + 1) * C].rearrange("p (h d) -> p h d", d=WD), src,
                                tab[:, 2 * t + cs, i * WD:(i + 1) * WD].unsqueeze(1).broadcast_to([P, HALF, WD]),
                                ALU.mult).then_inc(S[name], 1)
                    dve.wait_ge(S["k_squared"], passed(n(0)))
                    nc.vector.tensor_reduce(ss[j % 2][:], sq[:].rearrange("p a h d -> p (a h) d"), AX, ALU.add)\
                        .then_inc(S["sums"], 1)
                    dve.wait_ge(S["sums"], passed(n(0)))
                    nc.vector.tensor_scalar(ss[j % 2][:], ss[j % 2][:], 1e-24, None, ALU.max)\
                        .then_inc(S["guarded"], 1)
                if live(1):
                    dve.wait_ge(S["scored"], passed(n(1)))
                    p = pr[j1 % 2]
                    rows = p[:].rearrange("p g a k -> p (g a) k")
                    nc.vector.tensor_tensor(p[:].rearrange("p g a k -> p a g k"), pairs(5),
                                            mask[:, j1 // 2, :].unsqueeze(1).unsqueeze(1)
                                            .broadcast_to([P, 2, NPAIR, 2 * WIN]), ALU.add).then_inc(S["masked"], 1)
                    dve.wait_ge(S["masked"], passed(n(1)))
                    nc.vector.tensor_reduce(mx[j1 % 2][:], rows, AX, ALU.max).then_inc(S["maxed"], 1)
                    dve.wait_ge(S["maxed"], passed(n(1)))
                    nc.vector.tensor_tensor(rows, rows, mx[j1 % 2][:].unsqueeze(2).broadcast_to([P, HALF, 2 * WIN]),
                                            ALU.subtract).then_inc(S["lowered"], 1)
                if live(2):
                    dve.wait_ge(S["valued"], passed(n(2)))
                    nc.vector.tensor_tensor(on[j2 % 2][:].rearrange("p g a d -> p a g d"), pairs(3),
                                            rl[j2 % 2][:].rearrange("p (g a) -> p a g", a=2).unsqueeze(3)
                                            .broadcast_to([P, 2, NPAIR, WD]), ALU.mult).then_inc(S["divided"], 1)
                if live(1):
                    dve.wait_ge(S["exped"], passed(n(1)))
                    nc.vector.tensor_reduce(tot[j1 % 2][:], pr[j1 % 2][:].rearrange("p g a k -> p (g a) k"), AX,
                                            ALU.add).then_inc(S["totals"], 1)
                    dve.wait_ge(S["totals"], passed(n(1)))
                    nc.vector.reciprocal(rl[j1 % 2][:], tot[j1 % 2][:]).then_inc(S["inverse"], 1)
                if live(3) and j3 % 2 == 1:
                    dve.wait_ge(S["projected"], passed(tiles(ADDED[j] + 1)))
                    s = seq - 1
                    lo = PAD + (j3 // 2) * P
                    rows = xT[:, bass.ds(s, 1), lo:lo + P].rearrange("p b t -> p (b t)")
                    nc.vector.tensor_tensor(rows, rows, banks[:, 7, 0:P], ALU.add).then_inc(S["residual"], 1)
            pipeline(dve, iteration)

        @block.scalar
        def _(act):
            def iteration(j, seq, n, live, tiles):
                j1, j2, j3 = (j - 1) % STEPS, (j - 2) % STEPS, (j - 3) % STEPS

                def values(a):
                    act.wait_ge(S["v_made"], passed((n(0) - 1) * 2 + a + 1))
                    nc.scalar.activation(vd[j][:, 2 * a:2 * a + 2, :].rearrange("p w n -> p (w n)"), banks[:, 2, :],
                                         ACT.Copy).then_inc(S["v_taken"], 1)
                if live(0):
                    act.wait_ge(S["qk"], passed(n(0) * 2 - 1))
                    act.wait_ge(S["sums"], passed(n(0) - 1))
                    nc.scalar.activation(sq[:, 0].rearrange("p h d -> p (h d)"), banks[:, 0, :], ACT.Square)\
                        .then_inc(S["q_squared"], 1)
                if live(1):
                    act.wait_ge(S["turned"], passed(n(1) * 2))
                    nc.scalar.activation(qT[j1 % 2][:].rearrange("p g q -> p (g q)"), banks[:, 3, :], ACT.Copy)\
                        .then_inc(S["q_turned"], 1)
                    hk, lo = j1 % 2, WIN + (j1 // 2) * P
                    nc.scalar.activation(kT[:, hk * NPAIR:(hk + 1) * NPAIR, lo:lo + P],
                                         banks[:, 4, :].rearrange("p (g k) -> p g k", k=P), ACT.Copy)\
                        .then_inc(S["k_turned"], 1)
                if live(0):
                    act.wait_ge(S["k_rotated"], passed(n(0) * 2))
                    nc.scalar.activation(sq[:, 1].rearrange("p h d -> p (h d)"), banks[:, 1, :], ACT.Square)\
                        .then_inc(S["k_squared"], 1)
                    values(0)
                if live(2):
                    act.wait_ge(S["p_turned"], passed(n(2)))
                    nc.scalar.activation(prT[:].rearrange("p g q -> p (g q)"), banks[:, 7, :], ACT.Copy)\
                        .then_inc(S["p_taken"], 1)
                if live(0):
                    values(1)
                if live(1):
                    act.wait_ge(S["lowered"], passed(n(1)))
                    rows = pr[j1 % 2][:].rearrange("p g a k -> p (g a k)")
                    nc.scalar.activation(rows, rows, ACT.Exp).then_inc(S["exped"], 1)
                if live(3):
                    act.wait_ge(S["o_turned"], passed(n(3)))
                    nc.scalar.activation(oT[j3 % 2][:].rearrange("p g q -> p (g q)"), banks[:, 7, :], ACT.Copy)\
                        .then_inc(S["o_taken"], 1)
            pipeline(act, iteration)


def load_window_weights(sp, weights, h, layer, wqkv, wo, scl):
    def of(name):
        return h[name][bass.ds(layer, 1)] if not isinstance(layer, int) else h[name][layer:layer + 1]
    sp.dma_start(wqkv[:], of("w_qkv").squeeze(0)).then_inc(weights, 16)
    sp.dma_start(wo[:], of("w_o").squeeze(0)).then_inc(weights, 16)
    sp.dma_start(scl[:], of("w_scl").broadcast_to([P, 2 * WD])).then_inc(weights, 16)


@scoped
def gated_mlp(nc, sem, sb, layer, h, xT, norm, banks, w1, w2, col, wqkv, wo, scl):
    gel = [sb(f"m_gel{m}", [MC, CH]) for m in range(MG)]
    hid = [[sb(f"m_hid{k}{m}", [MC, CH]) for m in range(MG)] for k in range(2)]
    up, gelued, made = sem("m_up"), sem("m_gelued"), sem("m_made")
    down, residual, weights = sem("m_down"), sem("m_residual"), sem("w_weights")
    done = layer * NCH

    def b1(m, vg):
        return col[0:MC, 3 + 2 * m + vg:4 + 2 * m + vg]

    with nc.Block() as block:
        @block.sync
        def _(sp):
            load_window_weights(sp, weights, h, (layer + 1) % DEPTH, wqkv, wo, scl)
            sp.wait_ge(weights, (layer + 2) * 48)
            sp.sem_inc(sem("gate"), 1)

        @block.tensor
        def _(pe):
            def w_up(c, m, first=False):
                if not first:
                    pe.wait_ge(made, passed((done + c - 1) * MG + m + 1))
                for vg in range(2):
                    last = nc.tensor.matmul(banks[0:MC, 2 * m + vg, :], w1[:, 2 * m + vg, :],
                                            norm[:, bass.ds(c * CH, CH)], start=True, stop=True)
                last.then_inc(up, 1)

            def w_down(c, k, m):
                if m == 0:
                    pe.wait_ge(residual, passed(done + c - k))
                pe.wait_ge(made, passed((done + c) * MG + m + 1))
                last = nc.tensor.matmul(banks[:, 6 + k, :], w2[:, m, :], hid[k][m][:],
                                        start=(m == 0), stop=(m == MG - 1))
                if m == MG - 1:
                    last.then_inc(down, 1)

            for m in range(MG):
                w_up(0, m, True)
            with pe.Fori(0, NCH // 2 - 1) as i:
                for k in range(2):
                    for m in range(MG):
                        w_up(i * 2 + k + 1, m)
                        w_down(i * 2 + k, k, m)
            for m in range(MG):
                w_up(NCH - 1, m)
                w_down(NCH - 2, 0, m)
            for m in range(MG):
                w_down(NCH - 1, 1, m)

        @block.scalar
        def _(act):
            def gelus(c, first=False):
                for m in range(MG):
                    act.wait_ge(up, passed((done + c) * MG + m + 1))
                    if not first:
                        act.wait_ge(made, passed((done + c - 1) * MG + m + 1))
                    nc.scalar.activation(gel[m][:], banks[0:MC, 2 * m + 1, :], ACT.Gelu, bias=b1(m, 1))\
                        .then_inc(gelued, 1)

            gelus(0, True)
            gelus(1)
            with act.Fori(1, NCH // 2) as i:
                gelus(i * 2)
                gelus(i * 2 + 1)

        @block.vector
        def _(dve):
            def hidden(c, k):
                for m in range(MG):
                    dve.wait_ge(gelued, passed((done + c) * MG + m + 1))
                    nc.vector.scalar_tensor_tensor(out=hid[k][m][:], in0=banks[0:MC, 2 * m, :], scalar=b1(m, 0),
                                                   in1=gel[m][:], op0=ALU.add, op1=ALU.mult).then_inc(made, 1)

            def add(c, k):
                dve.wait_ge(down, passed(done + c + 1))
                rows = xT[:, bass.ds(c * PER, PER), PAD:PAD + T]
                nc.vector.scalar_tensor_tensor(out=rows, in0=banks[:, 6 + k, :].rearrange("p (b t) -> p b t", b=PER),
                                               scalar=col[:, 2:3], in1=rows, op0=ALU.add, op1=ALU.add)\
                    .then_inc(residual, 1)

            hidden(0, 0)
            with dve.Fori(0, NCH // 2 - 1) as i:
                for k in range(2):
                    hidden(i * 2 + k + 1, 1 - k)
                    add(i * 2 + k, k)
            hidden(NCH - 1, 1)
            add(NCH - 2, 0)
            add(NCH - 1, 1)


def arranged(x, **w):
    f = np.float32
    h = {k: np.asarray(v) for k, v in w.items()}
    t = {}
    t["x"] = np.asarray(x).transpose(2, 0, 1)
    t["ident"] = np.eye(P, dtype=f)
    t["a_w"] = np.stack([h["L0_attn_" + n].T for n in ("Wq", "Wk", "Wv", "Wo")], 1)
    p = np.arange(P)
    t["a_hm"] = (p[:, None] // AD % 4 == np.arange(4)).astype(f)
    t["a_mask"] = np.stack([np.zeros((P, P)), np.where(p[None] <= p[:, None], 0, NEG)], 1).astype(f)
    t["e_wr"] = h["L0_ffn_Wr"].T
    t["e_a"] = h["L0_ffn_A"].reshape(EC, P, D).transpose(1, 0, 2)
    t["e_b"] = h["L0_ffn_Bw"].transpose(0, 2, 1).reshape(EC, P, D).transpose(1, 0, 2)
    t["e_spread"] = (np.arange(E * R)[None] // R == np.arange(E)[:, None]).astype(f)
    t["e_before"] = (np.arange(E)[None] < np.arange(E)[:, None]).astype(f)

    def swapped(m):
        return m.reshape(D, RH, 2, RK // 2)[:, :, ::-1].reshape(D, RH * RK)
    t["r_w"] = np.stack([h["L1_attn_Wq"], swapped(h["L1_attn_Wq"]), h["L1_attn_Wk"], swapped(h["L1_attn_Wk"])], 1)
    t["r_wv"], t["r_wg"] = h["L1_attn_Wv"], h["L1_attn_Wg"]
    t["r_wo"] = h["L1_attn_Wo"].reshape(2, P, D).transpose(1, 0, 2)
    t["r_gn"] = h["L1_attn_gn_weight"]
    freq = (f(1) / f(10000) ** (np.arange(0, RK, 2, dtype=f) / f(RK))).astype(f)
    ang = (np.arange(T, dtype=f)[None] * freq[:, None]).astype(f)
    cos, sin = np.tile(np.cos(ang), (2 * RH, 1)), np.tile(np.concatenate([-np.sin(ang), np.sin(ang)]), (RH, 1))
    both = np.stack([cos, sin], 1)
    t["r_tab"] = np.stack([both * f(RK ** -0.5), both], 2).astype(f)
    gamma = 1 - 2.0 ** (-5.0 - np.arange(RH))
    rel = np.arange(T)[None] - p[:, None]
    t["r_decay"] = np.where(rel[:, None] >= 0, gamma[None, :, None] ** np.maximum(rel, 0)[:, None], 0).astype(f)

    half = np.arange(0, WD, 2, dtype=f)
    freq = (f(1) / f(10000) ** (half / f(WD))).astype(f)
    pos = np.arange(T, dtype=f)
    ang = (pos[:, None] * freq[None]).astype(f)
    power = ((pos - T // 2) / f(WIN // 2)).astype(f)
    scale = ((half + f(0.4 * WD)) / f(1.4 * WD)).astype(f)[None] ** power[:, None]
    cos, sin = np.cos(ang), np.sin(ang)
    tab = np.stack([np.stack([np.concatenate([cos * m, cos * m], 1) for m in (scale * f(8), 1 / scale)], 1),
                    np.stack([np.concatenate([sin * m, -sin * m], 1) for m in (scale * f(8), 1 / scale)], 1)], 1)
    t["w_base"] = tab.reshape(TILES, P, 2, 2 * WD).transpose(1, 0, 2, 3).reshape(P, 2 * TILES, 2 * WD).astype(f)
    i, j = (p % WIN)[:, None], np.arange(2 * WIN)[None]
    seen = (j >= i) & (j <= i + WIN)
    first = seen & ((j >= WIN) | (p[:, None] >= WIN))
    t["w_mask"] = np.where(np.stack([first] + [seen] * (TILES - 1), 1), 0, NEG).astype(f)
    t["w_qkv"] = h["L1_ffn_Wqkv"]
    t["w_o"] = h["L1_ffn_Wo"].reshape(DEPTH, WH // 2, P, D).transpose(0, 2, 1, 3)
    t["w_scl"] = np.concatenate([h["L1_ffn_q_scale"], h["L1_ffn_k_scale"]], 1)

    def groups(m):
        m = m.reshape(*m.shape[:-1], 2, MLP)
        m = np.concatenate([m, np.zeros((*m.shape[:-1], MG * MC - MLP), m.dtype)], -1)
        return np.moveaxis(m.reshape(*m.shape[:-1], MG, MC), -2, -3).reshape(*m.shape[:-2], 2 * MG, MC)
    t["m_w1"] = groups(h["L1_ffn_W1"])
    w2 = h["L1_ffn_W2"]
    w2 = np.concatenate([w2, np.zeros((DEPTH, MG * MC - MLP, D), w2.dtype)], 1)
    t["m_w2"] = w2.reshape(DEPTH, MG, MC, D).transpose(0, 2, 1, 3)
    b1 = groups(h["L1_ffn_b1"])
    b1 = np.concatenate([b1, np.zeros((DEPTH, 2 * MG, P - MC), b1.dtype)], 2).transpose(0, 2, 1)
    t["m_col"] = np.concatenate([np.stack([h["L1_ffn_ln_g"], h["L1_ffn_ln_b"], h["L1_ffn_b2"]], 2), b1], 2)
    return {k: np.ascontiguousarray(v) for k, v in t.items()}


def kernel(L0_attn_x, **weights):
    from concourse import bacc
    from concourse.bass_utils import run_bass_kernel_spmd

    nc = bacc.Bacc("TRN2", target_bir_lowering=False, num_devices=1)
    arrays = arranged(L0_attn_x, **weights)
    h = {k: nc.dram_tensor(k + "_in", a.shape, mybir.dt.from_np(a.dtype), kind="ExternalInput").ap()
         for k, a in arrays.items()}
    out = nc.dram_tensor("out", (D, B, T), F32, kind="ExternalOutput").ap()
    program(nc, h, out)
    r = run_bass_kernel_spmd(nc, [{k + "_in": a for k, a in arrays.items()}], core_ids=[0])
    return np.ascontiguousarray(r.results[0]["out"].transpose(1, 2, 0))
```

```python
from contextlib import ExitStack

import numpy as np

import concourse.bass as bass
from concourse import mybir

F32 = mybir.dt.float32
ALU = mybir.AluOpType
ACT = mybir.ActivationFunctionType
AX = mybir.AxisListType.X

P = 128
B, T, D = 16, 256, 128
PAD = 40
TILES = T // P
NEG = -1e30
EPS = 1e-5

CH = 512
NCH = B * T // CH
ROW = 4
PER = CH // T

AH, AD = 16, 8
A_SCALE = 1.0 / float(np.sqrt(np.float32(AD)))

E, R = 8, 64
EC = E * R // P

RH, RK, RV = 4, 32, 64

DEPTH, WH, WD, WIN = 6, 16, 64, 32
INNER = WH * WD
HALF = 8
STEPS = TILES * (WH // HALF)
NPAIR = HALF // 2
NWIN = P // WIN
MLP = 341
MC, MG = 114, 3

COUNTED = """
ln_mean ln_centred ln_squared ln_var ln_logged ln_inverse ln_scaled
a_xcopy a_proj a_vproj a_qmasked a_ktaken a_vtaken a_scored a_masked a_maxed a_biased a_exped a_turned a_taken
a_summed a_totalled a_odone a_oturned a_otaken a_wo_done a_added
e_gated e_mixed e_made e_applied e_added
r_xcopy r_qk r_vg r_qktaken r_rotated r_vgtaken r_scored r_decayed r_summed r_squared r_ssum r_inv r_chain
r_gated r_turned r_took r_wo r_added r_ready
w_shifted0 w_shifted1 w_qk w_q_squared w_k_squared w_k_rotated w_q_rotated w_sums w_guarded w_added w_rnorm
w_normed w_turned w_k_turned w_q_turned w_v_made w_v_taken w_scored w_masked w_minned w_exped
w_inverse w_p_turned w_p_taken w_valued w_divided w_o_turned w_o_taken w_projected w_residual w_ready w_tabled
m_up m_gelued m_made m_down m_residual
""".split()


def passed(count):
    return count + 1


def scoped(phase):
    def run(nc, sem, *args):
        with ExitStack() as stack:
            phase(nc, sem, lambda name, shape: stack.enter_context(nc.sbuf_tensor(name, shape, F32)), *args)
    return run


def program(nc, h, out):
    def sb(name, shape):
        return nc.alloc_sbuf_tensor(name, shape, F32)

    sems = {}

    def sem(name):
        if name not in sems:
            sems[name] = nc.alloc_semaphore(name)
        return sems[name]

    xT = sb("xT", [P, B + 1, PAD + T])
    ident = sb("ident", [P, P])
    mean_w = sb("mean_w", [P, P])
    half_mean = [sb(f"half_mean{i}", [P, P]) for i in range(2)]
    norm = sb("norm", [P, B * T])
    logv = sb("logv", [P, B * T])
    eps_col = sb("eps_col", [P, 1])
    banks = nc.alloc_psum_tensor("banks", [P, 8, 512], F32)

    a_w = sb("a_w", [P, 4, P])
    a_hm = sb("a_hm", [P, AH])
    a_mask = sb("a_mask", [P, 2, P])
    e_wr = sb("e_wr", [P, E])
    e_a = sb("e_a", [P, EC, P])
    e_b = sb("e_b", [P, EC, P])
    e_spread = sb("e_spread", [E, EC * P])
    e_before = sb("e_before", [B, E, E])
    r_w = sb("r_w", [P, 4, P])
    r_wv = sb("r_wv", [P, RH * RV])
    r_wg = sb("r_wg", [P, RH * RV])
    r_wo = sb("r_wo", [P, 2, P])
    r_gn = sb("r_gn", [P, RV])
    r_tab = sb("r_tab", [P, 2, 2, T])
    r_decay = sb("r_decay", [P, RH, T])

    w_qkv = sb("w_qkv", [P, 3 * INNER])
    w_o = sb("w_o", [P, WH // 2, P])
    w_base = sb("w_base", [P, 2 * TILES, 2 * WD])
    w_scl = sb("w_scl", [P, 2 * WD])
    w_tab = sb("w_tab", [P, 2 * TILES, 2 * WD])
    w_mask = sb("w_mask", [P, TILES, 2 * WIN])
    m_w1 = sb("m_w1", [P, 2 * MG, MC])
    m_w2 = sb("m_w2", [MC, MG, P])
    m_col = sb("m_col", [P, 3 + 2 * MG])

    loaded = sem("loaded")
    n_loads = [0]

    with nc.Block() as block:
        @block.sync
        def _(sp):
            def load(dst, src):
                sp.dma_start(dst, src).then_inc(loaded, 16)
                n_loads[0] += 1
            for b in range(0, B, 4):
                load(xT[:, b:b + 4, PAD:], h["x"][:, b:b + 4, :])
            for dst, name in ((ident, "ident"), (a_w, "a_w"), (a_hm, "a_hm"), (a_mask, "a_mask"),
                              (e_wr, "e_wr"), (e_a, "e_a"), (e_b, "e_b"), (e_spread, "e_spread"),
                              (r_w, "r_w"), (r_wv, "r_wv"), (r_wg, "r_wg"), (r_wo, "r_wo"),
                              (r_tab, "r_tab"), (r_decay, "r_decay"), (w_base, "w_base"),
                              (w_mask, "w_mask")):
                load(dst[:], h[name])
            load(e_before[:], h["e_before"].partition_broadcast(B))
            load(r_gn[:], h["r_gn"].partition_broadcast(P))
            load_window_weights(sp, sem("w_weights"), h, 0, w_qkv, w_o, w_scl)
            for name in COUNTED:
                sp.sem_inc(sem(name), 1)
            sp.wait_ge(loaded, 16 * n_loads[0])

        @block.vector
        def _(dve):
            nc.vector.memset(xT[:, :, 0:PAD], 0.0)
            nc.vector.memset(xT[:, B, PAD:], 0.0)
            nc.vector.memset(mean_w[:], 1.0 / D)
            for i in range(2):
                for half in range(2):
                    nc.vector.memset(half_mean[i][64 * half:64 * half + 64], 1.0 / D if half == i else 0.0)
            nc.vector.memset(eps_col[:], EPS)

    layer_norm(nc, sem, 0, False, xT, norm, logv, mean_w, half_mean, eps_col, banks, None)
    head_attention(nc, sem, xT, norm, banks, ident, a_w, a_hm, a_mask)
    layer_norm(nc, sem, 1, False, xT, norm, logv, mean_w, half_mean, eps_col, banks, None)
    experts(nc, sem, xT, norm, banks, ident, e_wr, e_a, e_b, e_spread, e_before)
    layer_norm(nc, sem, 2, False, xT, norm, logv, mean_w, half_mean, eps_col, banks, None)
    retention(nc, sem, xT, norm, logv, banks, ident, eps_col, r_w, r_wv, r_wg, r_wo, r_gn, r_tab, r_decay)

    layer_norm(nc, sem, 3, False, xT, norm, logv, mean_w, half_mean, eps_col, banks, None)
    kept = sb("kept", [P, B, T])
    moved = sem("moved")
    with nc.Block() as block:
        @block.vector
        def _(dve):
            for b in range(0, B, PER):
                nc.vector.tensor_copy(kept[:, b:b + PER, :], xT[:, b:b + PER, PAD:PAD + T]).then_inc(moved, 1)

        @block.scalar
        def _(act):
            for b in range(0, B, PER):
                act.wait_ge(moved, b // PER + 1)
                nc.scalar.activation(xT[:, b:b + PER, PAD:PAD + T],
                                     norm[:, b * T:(b + PER) * T].rearrange("p (b t) -> p b t", b=PER), ACT.Copy)

    with nc.Fori(0, DEPTH) as layer:
        window_attention(nc, sem, layer, h, xT, norm, logv, banks, ident, w_qkv, w_o, w_base, w_scl, w_tab,
                         w_mask, m_w1, m_w2, m_col)
        layer_norm(nc, sem, layer + 4, True, xT, norm, logv, mean_w, half_mean, eps_col, banks, m_col,
                   lambda sp: load_window_weights(sp, sem("w_weights"), h, (layer + 1) % DEPTH, w_qkv, w_o, w_scl))
        gated_mlp(nc, sem, layer, xT, norm, banks, m_w1, m_w2, m_col)

    stored, summed = sem("stored"), sem("summed")
    with nc.Block() as block:
        @block.vector
        def _(dve):
            for b in range(0, B, PER):
                nc.vector.tensor_tensor(kept[:, b:b + PER, :], kept[:, b:b + PER, :], xT[:, b:b + PER, PAD:PAD + T],
                                        ALU.add).then_inc(summed, 1)

        @block.sync
        def _(sp):
            for b in range(0, B, PER):
                sp.wait_ge(summed, b // PER + 1)
                sp.dma_start(out[:, b:b + PER, :], kept[:, b:b + PER, :]).then_inc(stored, 16)
            sp.wait_ge(stored, 16 * (B // PER))


def layer_norm(nc, sem, turn, mlp, xT, norm, logv, mean_w, half_mean, eps_col, banks, col, prefetch=None):
    mean_in, centred = sem("ln_mean"), sem("ln_centred")
    squared, var_in, logged = sem("ln_squared"), sem("ln_var"), sem("ln_logged")
    inverse, scaled = sem("ln_inverse"), sem("ln_scaled")
    done = NCH * turn

    parts = [(slice(0, P // 2), 0), (slice(P // 2, P), 1)] if mlp else [(slice(0, P), 0)]
    mean_of = half_mean if mlp else [mean_w]

    def chunk(buf, c):
        return buf[:, bass.ds(c * CH, CH)]

    def of(buf):
        return buf.rearrange("p (b t) -> p b t", b=PER)

    def stream(c, rows, back):
        return xT[rows, bass.ds(c * PER, PER), PAD - back:PAD - back + T]

    with nc.Block() as block:
        if prefetch:
            @block.sync
            def _(sp):
                prefetch(sp)

        @block.tensor
        def _(pe):
            with pe.Fori(0, NCH // ROW) as i:
                for k in range(ROW):
                    c = i * ROW + k
                    pe.wait_ge(centred, passed((done + i * ROW) * 2))
                    pe.sem_inc(sem("gate"), 1)
                    for m, (rows, back) in zip(mean_of, parts):
                        last = nc.tensor.matmul(of(banks[:, k, :]), m[:], stream(c, slice(0, P), back),
                                                start=(rows.start == 0), stop=(rows.stop == P))
                    last.then_inc(mean_in, 1)
                for k in range(ROW):
                    c = i * ROW + k
                    pe.wait_ge(squared, passed(done + c + 1))
                    pe.wait_ge(logged, passed(done + i * ROW))
                    nc.tensor.matmul(banks[:, ROW + k, :], mean_w[:], chunk(logv, c), start=True, stop=True)\
                        .then_inc(var_in, 1)

        @block.vector
        def _(dve):
            with dve.Fori(0, NCH // ROW) as i:
                for k in range(ROW):
                    c = i * ROW + k
                    dve.wait_ge(mean_in, passed(done + c + 1))
                    for rows, back in parts:
                        nc.vector.tensor_tensor(of(chunk(norm, c)[rows]), stream(c, rows, back),
                                                of(banks[rows, k, :]), ALU.subtract)\
                            .then_inc(centred, 2 // len(parts))
            with dve.Fori(0, NCH) as c:
                dve.wait_ge(inverse, passed(done + c + 1))
                dve.wait_ge(centred, passed((done + NCH) * 2))
                nc.vector.tensor_tensor(chunk(norm, c), chunk(norm, c), chunk(logv, c), ALU.mult).then_inc(scaled, 1)
                if mlp:
                    dve.wait_ge(scaled, passed(done + c + 1))
                    nc.vector.tensor_scalar(chunk(norm, c), chunk(norm, c), col[:, 0:1], col[:, 1:2],
                                            ALU.mult, ALU.add)

        @block.scalar
        def _(act):
            with act.Fori(0, NCH // ROW) as i:
                for k in range(ROW):
                    c = i * ROW + k
                    act.wait_ge(centred, passed((done + c + 1) * 2))
                    act.sem_inc(sem("gate"), 1)
                    nc.scalar.activation(chunk(logv, c), chunk(norm, c), ACT.Square).then_inc(squared, 1)
                for k in range(ROW):
                    c = i * ROW + k
                    act.wait_ge(var_in, passed(done + c + 1))
                    act.sem_inc(sem("gate"), 1)
                    nc.scalar.activation(chunk(logv, c), banks[:, ROW + k, :], ACT.Ln, bias=eps_col[:])\
                        .then_inc(logged, 1)
            act.wait_ge(logged, passed(done + NCH))
            act.sem_inc(sem("gate"), 1)
            with act.Fori(0, NCH // ROW) as i:
                for k in range(ROW):
                    c = i * ROW + k
                    nc.scalar.activation(chunk(logv, c), chunk(logv, c), ACT.Exp, scale=-0.5).then_inc(inverse, 1)


@scoped
def head_attention(nc, sem, sb, xT, norm, banks, ident, w, head_mask, mask):
    xa = sb("a_x", [P, T])
    q = sb("a_q", [P, T])
    kT = sb("a_kT", [P, T])
    qm = [sb(f"a_qm{i}", [P, 4, T]) for i in range(2)]
    v = sb("a_v", [P, TILES, P])
    KEYS = [P, 2 * P]
    probs = [sb(f"a_probs{i}", [P, 4 * 3 * P]) for i in range(2)]
    probsT = [sb(f"a_probsT{i}", [P, 12, P]) for i in range(2)]
    mx = sb("a_max", [P, 2, 8])
    bias = sb("a_bias", [P, 2, 8])
    total = sb("a_total", [P, 4, 2, 4])
    rtotal = sb("a_rtotal", [P, 4, 2, 4])
    o = sb("a_o", [P, TILES, P])
    oT = sb("a_oT", [P, T])

    xcopy, proj, vproj = sem("a_xcopy"), sem("a_proj"), sem("a_vproj")
    qmasked, ktaken, vtaken = sem("a_qmasked"), sem("a_ktaken"), sem("a_vtaken")
    scored, masked, maxed, biased = sem("a_scored"), sem("a_masked"), sem("a_maxed"), sem("a_biased")
    exped, turned, taken, summed = sem("a_exped"), sem("a_turned"), sem("a_taken"), sem("a_summed")
    totalled, odone, oturned, otaken = sem("a_totalled"), sem("a_odone"), sem("a_oturned"), sem("a_otaken")
    wo_done, added = sem("a_wo_done"), sem("a_added")

    def part(buf, tile):
        lo = 0 if tile == 0 else 4 * P
        return buf[:, lo:lo + 4 * KEYS[tile]].rearrange("p (s k) -> p s k", s=4)

    def score_bank(tile):
        if tile == 0:
            return banks[:, 2, :].rearrange("p (s k) -> p s k", s=4)
        return banks[:, 3:5, :].rearrange("p b (s k) -> p (b s) k", s=2)

    def pipeline(eng, sequence):
        sequence(0, True, False)
        with eng.Fori(1, B - 1) as b:
            sequence(b, False, False)
        sequence(B - 1, False, True)

    def ahead(b, r):
        return (b, r + 2) if r < 2 else (b + 1, r - 2)

    with nc.Block() as block:
        @block.gpsimd
        def _(pool):
            def copy(b):
                pool.wait_ge(vproj, passed(b))
                pool.sem_inc(sem("gate"), 1)
                nc.gpsimd.tensor_copy(xa[:], norm[:, bass.ds(b * T, T)]).then_inc(xcopy, 1)

            def mask_queries(b, r, early=False):
                if not early:
                    pool.wait_ge(scored, passed(b * 4 + r - 1))
                if r == 0:
                    pool.wait_ge(ktaken, passed(b + 1))
                heads = head_mask[:, 4 * r:4 * r + 4].unsqueeze(2).broadcast_to([P, 4, T])
                nc.gpsimd.tensor_tensor(qm[r % 2][:], q[:].unsqueeze(1).broadcast_to([P, 4, T]), heads,
                                        ALU.mult).then_inc(qmasked, 1)

            def sequence(b, first, last):
                mask_queries(b, 2)
                mask_queries(b, 3)
                if not last:
                    copy(b + 1)
                    mask_queries(b + 1, 0)
                    mask_queries(b + 1, 1)

            copy(0)
            mask_queries(0, 0, True)
            mask_queries(0, 1, True)
            pipeline(pool, sequence)

        @block.tensor
        def _(pe):
            def project(b):
                pe.wait_ge(xcopy, passed(b + 1))
                nc.tensor.matmul(banks[:, 0, 0:T], w[:, 0, :], xa[:], start=True, stop=True)
                nc.tensor.matmul(banks[:, 0, T:2 * T], w[:, 1, :], xa[:], start=True, stop=True).then_inc(proj, 1)

            def project_values(b):
                pe.wait_ge(ktaken, passed(b + 1))
                for t in range(TILES):
                    last = nc.tensor.matmul(banks[:, 0, t * P:(t + 1) * P], xa[:, t * P:(t + 1) * P], w[:, 2, :],
                                            start=True, stop=True)
                last.then_inc(vproj, 1)

            def scores(b, r):
                n = b * 4 + r
                pe.wait_ge(qmasked, passed(n + 1))
                if r == 0:
                    pe.wait_ge(ktaken, passed(b + 1))
                pe.wait_ge(masked, passed(n * 2))
                for t in range(TILES):
                    for s in range(4):
                        last = nc.tensor.matmul(score_bank(t)[:, s, :], qm[r % 2][:, s, t * P:(t + 1) * P],
                                                kT[:, 0:KEYS[t]], start=True, stop=True)
                last.then_inc(scored, 1)

            def turn(b, r):
                n = b * 4 + r
                pe.wait_ge(exped, passed(n + 1))
                pe.wait_ge(taken, passed(n * 2))
                for j in range(12):
                    last = nc.tensor.transpose(banks[:, 5 + j // 4, (j % 4) * P:(j % 4 + 1) * P],
                                               probs[r % 2][:, j * P:(j + 1) * P], ident[:])
                last.then_inc(turned, 1)

            def values(b, r):
                n = b * 4 + r
                if r == 0:
                    pe.wait_ge(odone, passed(b))
                    pe.wait_ge(vtaken, passed(b + 1))
                pe.wait_ge(taken, passed(n * 2 + 2))
                pt = probsT[r % 2]
                for s in range(4):
                    hd = 4 * r + s
                    cols = slice(hd * AD, (hd + 1) * AD)
                    nc.tensor.matmul(banks[:, 1, hd * AD:(hd + 1) * AD], pt[:, s, :], v[:, 0, cols],
                                     start=True, stop=True)
                    for k in range(2):
                        last = nc.tensor.matmul(banks[:, 1, P + hd * AD:P + (hd + 1) * AD],
                                                pt[:, 4 + 2 * s + k, :], v[:, k, cols],
                                                start=(k == 0), stop=(k == 1))
                last.then_inc(summed, 1)

            def turn_outputs(b):
                pe.wait_ge(vtaken, passed(b + 1))
                pe.wait_ge(odone, passed(b + 1))
                for t in range(TILES):
                    last = nc.tensor.transpose(banks[:, 0, t * P:(t + 1) * P], o[:, t, :], ident[:])
                last.then_inc(oturned, 1)

            def project_outputs(b):
                pe.wait_ge(otaken, passed(b + 1))
                nc.tensor.matmul(banks[:, 0, T:2 * T], w[:, 3, :], oT[:], start=True, stop=True).then_inc(wo_done, 1)

            def sequence(b, first, last):
                for r in range(4):
                    turn(b, r)
                    if r == 0 and not first:
                        pe.wait_ge(vtaken, passed(b + 1))
                        turn_outputs(b - 1)
                    if r < 2 or not last:
                        scores(*ahead(b, r))
                    if r == 0 and not first:
                        project_outputs(b - 1)
                    if r == 1 and not last:
                        pe.wait_ge(added, passed(b))
                        project(b + 1)
                    if r == 2 and not last:
                        project_values(b + 1)
                    values(b, r)

            project(0)
            project_values(0)
            scores(0, 0)
            scores(0, 1)
            pe.wait_ge(vtaken, passed(1))
            pipeline(pe, sequence)
            turn_outputs(B - 1)
            project_outputs(B - 1)

        @block.vector
        def _(dve):
            def softmax(b, r):
                n = b * 4 + r
                dve.wait_ge(scored, passed(n + 1))
                nc.vector.tensor_tensor(part(probs[r % 2], 0), score_bank(0),
                                        mask[:, 1, :].unsqueeze(1).broadcast_to([P, 4, P]), ALU.add)\
                    .then_inc(masked, 1)
                nc.vector.tensor_tensor(part(probs[r % 2], 1), score_bank(1),
                                        mask[:].rearrange("p a k -> p (a k)").unsqueeze(1)
                                        .broadcast_to([P, 4, 2 * P]), ALU.add).then_inc(masked, 1)
                dve.wait_ge(masked, passed(n * 2 + 2))
                for t in range(TILES):
                    nc.vector.tensor_reduce(mx[:, r % 2, t * 4:t * 4 + 4], part(probs[r % 2], t), AX, ALU.max)\
                        .then_inc(maxed, 1)
                dve.wait_ge(maxed, passed(n * 2 + 2))
                nc.vector.tensor_scalar(bias[:, r % 2, :], mx[:, r % 2, :], -A_SCALE, None, ALU.mult)\
                    .then_inc(biased, 1)

            def take(b, r):
                n = b * 4 + r
                dve.wait_ge(turned, passed(n + 1))
                nc.vector.tensor_copy(probsT[r % 2][:, 4:12, :].rearrange("p j q -> p (j q)"),
                                      banks[:, 6:8, :].rearrange("p b c -> p (b c)")).then_inc(taken, 1)
                dve.wait_ge(exped, passed(n + 1))
                if r == 0:
                    dve.wait_ge(odone, passed(b))
                nc.vector.reciprocal(rtotal[:, r], total[:, r]).then_inc(totalled, 1)

            def add(b):
                dve.wait_ge(wo_done, passed(b + 1))
                rows = xT[:, bass.ds(b, 1), PAD:PAD + T].rearrange("p b t -> p (b t)")
                nc.vector.tensor_tensor(rows, rows, banks[:, 0, T:2 * T], ALU.add).then_inc(added, 1)

            def sequence(b, first, last):
                for r in range(4):
                    take(b, r)
                    if r < 2 or not last:
                        softmax(*ahead(b, r))
                    if r == 0 and not first:
                        add(b - 1)
                dve.wait_ge(summed, passed(b * 4 + 4))
                dve.wait_ge(totalled, passed(b * 4 + 4))
                for t in range(TILES):
                    last = nc.vector.tensor_tensor(
                        o[:, t, :].rearrange("p (r s d) -> p r s d", r=4, s=4),
                        banks[:, 1, t * P:(t + 1) * P].rearrange("p (r s d) -> p r s d", r=4, s=4),
                        rtotal[:, :, t, :].unsqueeze(3).broadcast_to([P, 4, 4, AD]), ALU.mult)
                last.then_inc(odone, 1)

            softmax(0, 0)
            softmax(0, 1)
            pipeline(dve, sequence)
            add(B - 1)

        @block.scalar
        def _(act):
            def take_queries_keys(b):
                act.wait_ge(proj, passed(b + 1))
                nc.scalar.activation(q[:], banks[:, 0, 0:T], ACT.Copy)
                nc.scalar.activation(kT[:], banks[:, 0, T:2 * T], ACT.Copy).then_inc(ktaken, 1)

            def take_values(b):
                act.wait_ge(summed, passed(b * 4))
                act.wait_ge(vproj, passed(b + 1))
                nc.scalar.activation(v[:].rearrange("p t n -> p (t n)"), banks[:, 0, 0:T], ACT.Copy)\
                    .then_inc(vtaken, 1)

            def exps(b, r):
                act.wait_ge(biased, passed(b * 4 + r + 1))
                for t in range(TILES):
                    for s in range(4):
                        i = t * 4 + s
                        last = nc.scalar.activation(part(probs[r % 2], t)[:, s, :], part(probs[r % 2], t)[:, s, :],
                                                    ACT.Exp, bias=bias[:, r % 2, i:i + 1], scale=A_SCALE,
                                                    accum_out=total[:, r, t, s:s + 1])
                last.then_inc(exped, 1)

            def take(b, r):
                act.wait_ge(turned, passed(b * 4 + r + 1))
                nc.scalar.activation(probsT[r % 2][:, 0:4, :].rearrange("p j q -> p (j q)"), banks[:, 5, :],
                                     ACT.Copy).then_inc(taken, 1)

            def take_outputs(b):
                act.wait_ge(oturned, passed(b + 1))
                nc.scalar.activation(oT[:], banks[:, 0, 0:T], ACT.Copy).then_inc(otaken, 1)

            def sequence(b, first, last):
                for r in range(4):
                    take(b, r)
                    if r == 0 and not first:
                        take_outputs(b - 1)
                    if r < 3:
                        exps(b, r + 1)
                    elif not last:
                        exps(b + 1, 0)
                    if r == 1 and not last:
                        take_queries_keys(b + 1)
                if not last:
                    take_values(b + 1)

            take_queries_keys(0)
            take_values(0)
            exps(0, 0)
            pipeline(act, sequence)
            take_outputs(B - 1)


@scoped
def experts(nc, sem, sb, xT, norm, banks, ident, wr, ea, eb, spread, before):
    lg = sb("e_lg", [B, E])
    top = sb("e_top", [B, 1])
    ahead = sb("e_ahead", [B, E, E])
    ties = sb("e_ties", [B, E, E])
    rank = sb("e_rank", [B, E])
    ex = sb("e_ex", [B, E])
    tot = sb("e_tot", [B, 1])
    gates = sb("e_gates", [B, E])
    gT = sb("e_gT", [E, B])
    gcol = sb("e_gcol", [P, EC, B])
    bg = [sb(f"e_bg{i}", [P, EC, P]) for i in range(2)]
    wb = [sb(f"e_wb{i}", [P, P]) for i in range(2)]
    chain, on_pe, on_act = sem("e_chain"), sem("e_pe"), sem("e_act")
    gated, mixed, made, applied, added = (sem("e_gated"), sem("e_mixed"), sem("e_made"), sem("e_applied"),
                                          sem("e_added"))
    steps = [0]

    with nc.Block() as block:
        @block.tensor
        def _(pe):
            first = norm[:].rearrange("p (b t) -> p b t", b=B)[:, :, 0]
            nc.tensor.matmul(banks[0:B, 4, 0:E], first, wr[:], start=True, stop=True).then_inc(on_pe, 1)
            pe.wait_ge(on_act, 2)
            nc.tensor.transpose(banks[0:E, 5, 0:B], gates[:], ident[0:B, 0:B]).then_inc(on_pe, 1)
            pe.wait_ge(on_act, 3)
            for c in range(EC):
                last = nc.tensor.matmul(banks[:, 6, c * B:(c + 1) * B], spread[:, c * P:(c + 1) * P], gT[:],
                                        start=True, stop=True)
            last.then_inc(on_pe, 1)
            with pe.Fori(0, B // 2) as i:
                for k in range(2):
                    b = i * 2 + k
                    pe.wait_ge(gated, passed(b + 1))
                    pe.wait_ge(made, passed(i * 2))
                    for c in range(EC):
                        last = nc.tensor.matmul(banks[:, k, 0:P], ea[:, c, :], bg[k][:, c, :],
                                                start=(c == 0), stop=(c == EC - 1))
                    last.then_inc(mixed, 1)
                for k in range(2):
                    b = i * 2 + k
                    pe.wait_ge(made, passed(b + 1))
                    pe.wait_ge(added, passed(i * 2))
                    nc.tensor.matmul(banks[:, 2 + k, 0:T], wb[k][:], norm[:, bass.ds(b * T, T)],
                                     start=True, stop=True).then_inc(applied, 1)

        @block.vector
        def _(dve):
            def link(ins):
                steps[0] += 1
                ins.then_inc(chain, 1)
                dve.wait_ge(chain, steps[0])
            dve.wait_ge(on_pe, 1)
            link(nc.vector.tensor_copy(lg[:], banks[0:B, 4, 0:E]))
            link(nc.vector.tensor_reduce(top[:], lg[:], AX, ALU.max))
            other, own = lg[:].unsqueeze(1).broadcast_to([B, E, E]), lg[:].unsqueeze(2).broadcast_to([B, E, E])
            link(nc.vector.tensor_tensor(ahead[:], other, own, ALU.is_gt))
            link(nc.vector.tensor_tensor(ties[:], other, own, ALU.is_equal))
            link(nc.vector.tensor_tensor(ties[:], ties[:], before[:], ALU.mult))
            link(nc.vector.tensor_tensor(ahead[:], ahead[:], ties[:], ALU.add))
            link(nc.vector.tensor_reduce(rank[:], ahead[:], AX, ALU.add))
            link(nc.vector.tensor_scalar(rank[:], rank[:], 2.0, None, ALU.is_lt))
            link(nc.vector.tensor_scalar(ex[:], lg[:], top[:], None, ALU.subtract))
            dve.wait_ge(on_act, 1)
            link(nc.vector.tensor_tensor(ex[:], ex[:], rank[:], ALU.mult))
            link(nc.vector.tensor_reduce(tot[:], ex[:], AX, ALU.add))
            link(nc.vector.reciprocal(tot[:], tot[:]))
            nc.vector.tensor_scalar(gates[:], ex[:], tot[:], None, ALU.mult).then_inc(on_act, 1)
            dve.wait_ge(on_pe, 2)
            nc.vector.tensor_copy(gT[:], banks[0:E, 5, 0:B]).then_inc(on_act, 1)
            dve.wait_ge(on_pe, 3)
            link(nc.vector.tensor_copy(gcol[:].rearrange("p c b -> p (c b)"), banks[:, 6, 0:EC * B]))
            with dve.Fori(0, B // 2) as i:
                for k in range(2):
                    b = i * 2 + k
                    dve.wait_ge(mixed, passed(i * 2))
                    nc.vector.tensor_tensor(bg[k][:], eb[:], gcol[:, :, bass.ds(b, 1)].broadcast_to([P, EC, P]),
                                            ALU.mult).then_inc(gated, 1)
                for k in range(2):
                    b = i * 2 + k
                    dve.wait_ge(mixed, passed(b + 1))
                    dve.wait_ge(applied, passed(i * 2))
                    nc.vector.tensor_tensor(wb[k][:], banks[:, k, 0:P], ident[:], ALU.add).then_inc(made, 1)
                for k in range(2):
                    b = i * 2 + k
                    dve.wait_ge(applied, passed(b + 1))
                    rows = xT[:, bass.ds(b, 1), PAD:PAD + T].rearrange("p b t -> p (b t)")
                    nc.vector.tensor_tensor(rows, rows, banks[:, 2 + k, 0:T], ALU.add).then_inc(added, 1)

        @block.scalar
        def _(act):
            act.wait_ge(chain, 9)
            nc.scalar.activation(ex[:], ex[:], ACT.Exp).then_inc(on_act, 1)


@scoped
def retention(nc, sem, sb, xT, norm, spare, banks, ident, eps_col, w, wv, wg, wo, gn, tab, decay):
    xa = sb("r_x", [P, T])
    rot = sb("r_rot", [P, 2, T])
    rot2 = sb("r_rot2", [P, 2, T])
    v = sb("r_v", [P, TILES, RH * RV])
    g = sb("r_g", [P, TILES, RH * RV])
    att = sb("r_att", [P, RH, 3, P])
    osb = sb("r_o", [P, TILES * RH, RV])
    osq = sb("r_osq", [P, TILES * RH, RV])
    ss = sb("r_ss", [P, TILES * RH])
    rs = sb("r_rs", [P, TILES * RH])
    power = sb("r_power", [P, TILES * RH])
    oT = sb("r_oT", [P, 2, T])
    NO = TILES * RH * RV
    xcopy, qk, vg, qktaken, rotated = sem("r_xcopy"), sem("r_qk"), sem("r_vg"), sem("r_qktaken"), sem("r_rotated")
    vgtaken, scored, decayed, summed = sem("r_vgtaken"), sem("r_scored"), sem("r_decayed"), sem("r_summed")
    otaken, squared, ssum, inv, chain = sem("r_otaken"), sem("r_squared"), sem("r_ssum"), sem("r_inv"), sem("r_chain")
    gated, turned, took, wo_done, added = sem("r_gated"), sem("r_turned"), sem("r_took"), sem("r_wo"), sem("r_added")
    ready = sem("r_ready")

    with nc.Block() as block:
        @block.gpsimd
        def _(pool):
            nc.gpsimd.memset(power[:], -0.5).then_inc(ready, 1)
            pool.wait_ge(ready, passed(1))
            with pool.Fori(0, B) as b:
                pool.wait_ge(vg, passed(b))
                pool.sem_inc(sem("gate"), 1)
                nc.gpsimd.tensor_copy(xa[:], norm[:, bass.ds(b * T, T)]).then_inc(xcopy, 1)
                pool.wait_ge(ssum, passed(b + 1))
                nc.gpsimd.tensor_tensor(rs[:], ss[:], power[:], ALU.pow).then_inc(inv, 1)

        @block.tensor
        def _(pe):
            with pe.Fori(0, B) as b:
                pe.wait_ge(xcopy, passed(b + 1))
                pe.wait_ge(added, passed(b))
                for j in range(4):
                    last = nc.tensor.matmul(banks[:, j % 2, (j // 2) * T:(j // 2 + 1) * T], w[:, j, :], xa[:],
                                            start=True, stop=True)
                last.then_inc(qk, 1)
                for t in range(TILES):
                    cols = slice(t * RH * RV, (t + 1) * RH * RV)
                    nc.tensor.matmul(banks[:, 2, cols], xa[:, t * P:(t + 1) * P], wv[:], start=True, stop=True)
                    last = nc.tensor.matmul(banks[:, 3, cols], xa[:, t * P:(t + 1) * P], wg[:], start=True, stop=True)
                last.then_inc(vg, 1)
                pe.wait_ge(rotated, passed(b + 1))
                for hd in range(RH):
                    rows = slice(hd * RK, (hd + 1) * RK)
                    nc.tensor.matmul(banks[:, 4 + hd, 0:2 * P], rot[rows, 1, 0:P], rot[rows, 0, :],
                                     start=True, stop=True)
                    last = nc.tensor.matmul(banks[:, 4 + hd, 2 * P:3 * P], rot[rows, 1, P:2 * P],
                                            rot[rows, 0, P:2 * P], start=True, stop=True)
                last.then_inc(scored, 1)
                pe.wait_ge(vgtaken, passed(b * 2 + 2))
                pe.wait_ge(decayed, passed(b * 2 + 2))
                for hd in range(RH):
                    cols = slice(hd * RV, (hd + 1) * RV)
                    nc.tensor.matmul(banks[:, 2, hd * RV:(hd + 1) * RV], att[:, hd, 0, :], v[:, 0, cols],
                                     start=True, stop=True)
                    for k in range(2):
                        last = nc.tensor.matmul(banks[:, 2, (RH + hd) * RV:(RH + hd + 1) * RV], att[:, hd, 1 + k, :],
                                                v[:, k, cols], start=(k == 0), stop=(k == 1))
                last.then_inc(summed, 1)
                pe.wait_ge(gated, passed(b + 1))
                for t in range(TILES):
                    for c in range(2):
                        last = nc.tensor.transpose(
                            banks[:, 0, (c * 2 + t) * P:(c * 2 + t + 1) * P],
                            osb[:, t * RH:(t + 1) * RH, :].rearrange("p h d -> p (h d)")[:, c * P:(c + 1) * P],
                            ident[:])
                last.then_inc(turned, 1)
                pe.wait_ge(took, passed(b + 1))
                for c in range(2):
                    last = nc.tensor.matmul(banks[:, 1, 0:T], wo[:, c, :], oT[:, c, :], start=(c == 0), stop=(c == 1))
                last.then_inc(wo_done, 1)

        @block.vector
        def _(dve):
            with dve.Fori(0, B) as b:
                dve.wait_ge(qk, passed(b + 1))
                nc.vector.tensor_tensor(rot[:].rearrange("p a t -> p (a t)"), banks[:, 0, :],
                                        tab[:, 0, :, :].rearrange("p a t -> p (a t)"), ALU.mult).then_inc(qktaken, 1)
                nc.vector.tensor_tensor(rot2[:].rearrange("p a t -> p (a t)"), banks[:, 1, :],
                                        tab[:, 1, :, :].rearrange("p a t -> p (a t)"), ALU.mult).then_inc(qktaken, 1)
                dve.wait_ge(qktaken, passed(b * 2 + 2))
                nc.vector.tensor_tensor(rot[:], rot[:], rot2[:], ALU.add).then_inc(rotated, 1)
                dve.wait_ge(scored, passed(b + 1))
                nc.vector.tensor_tensor(att[:, :, 0:2, :].rearrange("p h a q -> p h (a q)"), banks[:, 4:8, 0:2 * P],
                                        decay[:], ALU.mult).then_inc(decayed, 1)
                nc.vector.tensor_tensor(att[:, :, 2, :], banks[:, 4:8, 2 * P:3 * P], decay[:, :, 0:P], ALU.mult)\
                    .then_inc(decayed, 1)
                dve.wait_ge(squared, passed(b + 1))
                nc.vector.tensor_reduce(ss[:], osq[:], AX, ALU.add).then_inc(chain, 1)
                dve.wait_ge(chain, passed(b * 3 + 1))
                nc.vector.tensor_scalar(ss[:], ss[:], 1.0 / RV, EPS, ALU.mult, ALU.add).then_inc(ssum, 1)
                nc.vector.tensor_tensor(osb[:], banks[:, 2, :].rearrange("p (h d) -> p h d", d=RV),
                                        gn[:].unsqueeze(1).broadcast_to([P, TILES * RH, RV]), ALU.mult)\
                    .then_inc(chain, 1)
                dve.wait_ge(inv, passed(b + 1))
                dve.wait_ge(chain, passed(b * 3 + 2))
                nc.vector.tensor_tensor(osb[:], osb[:], rs[:].unsqueeze(2).broadcast_to([P, TILES * RH, RV]),
                                        ALU.mult).then_inc(chain, 1)
                dve.wait_ge(chain, passed(b * 3 + 3))
                nc.vector.tensor_tensor(osb[:].rearrange("p h d -> p (h d)"), osb[:].rearrange("p h d -> p (h d)"),
                                        g[:].rearrange("p t n -> p (t n)"), ALU.mult).then_inc(gated, 1)
                dve.wait_ge(wo_done, passed(b + 1))
                rows = xT[:, bass.ds(b, 1), PAD:PAD + T].rearrange("p b t -> p (b t)")
                nc.vector.tensor_tensor(rows, rows, banks[:, 1, 0:T], ALU.add).then_inc(added, 1)

        @block.scalar
        def _(act):
            with act.Fori(0, B) as b:
                act.wait_ge(vg, passed(b + 1))
                nc.scalar.activation(g[:].rearrange("p t n -> p (t n)"), banks[:, 3, :], ACT.Silu)\
                    .then_inc(vgtaken, 1)
                nc.scalar.activation(v[:].rearrange("p t n -> p (t n)"), banks[:, 2, :], ACT.Copy)\
                    .then_inc(vgtaken, 1)
                act.wait_ge(summed, passed(b + 1))
                nc.scalar.activation(osq[:].rearrange("p h d -> p (h d)"), banks[:, 2, :], ACT.Square)\
                    .then_inc(squared, 1)
                act.wait_ge(turned, passed(b + 1))
                nc.scalar.activation(oT[:].rearrange("p c t -> p (c t)"), banks[:, 0, :], ACT.Copy).then_inc(took, 1)


@scoped
def window_attention(nc, sem, sb, layer, h, xT, spare0, spare1, banks, ident, wqkv, wo, base, scl, tab, mask,
                     m_w1, m_w2, m_col):
    N = B * STEPS
    LAG = 4
    xs = [sb(f"w_xs{t}", [P, WIN + P]) for t in range(TILES)]
    sq = sb("w_sq", [P, 2, HALF, WD])
    t1 = [sb(f"w_t1{i}", [P, 2 * HALF * WD]) for i in range(2)]
    t2 = [sb(f"w_t2{i}", [P, 2 * HALF * WD]) for i in range(2)]
    ss = [sb(f"w_ss{i}", [P, 2 * HALF]) for i in range(2)]
    rn = [sb(f"w_rn{i}", [P, 2 * HALF]) for i in range(2)]
    power = sb("w_power", [P, 2 * HALF])
    qT = [sb(f"w_qT{i}", [P, NPAIR, P]) for i in range(2)]
    kT = sb("w_kT", [P, WH // 2, WIN + T])
    vd = [sb(f"w_vd{j}", [P, NWIN, NPAIR * WD]) for j in range(STEPS)]
    pr = [sb(f"w_pr{i}", [P, NPAIR, 2, 2 * WIN]) for i in range(2)]
    mn = [sb(f"w_mn{i}", [P, HALF]) for i in range(2)]
    tot = [sb(f"w_tot{i}", [P, HALF]) for i in range(2)]
    rl = [sb(f"w_rl{i}", [P, HALF]) for i in range(2)]
    prT = sb("w_prT", [P, NPAIR, P])
    on = [sb(f"w_on{i}", [P, NPAIR, 2, WD]) for i in range(2)]
    oT = [sb(f"w_oT{i}", [P, NPAIR, P]) for i in range(WH // HALF)]

    S = {n: sem("w_" + n) for n in (
        "weights mlp_weights shifted0 shifted1 qk q_squared k_squared k_rotated q_rotated sums guarded added rnorm normed turned "
        "k_turned q_turned v_made v_taken scored masked minned exped inverse p_turned p_taken "
        "valued divided o_turned o_taken projected residual ready tabled").split()}
    C = 2 * HALF * WD // 2

    def pairs(bank):
        return banks[:, bank:bank + 2, 0:NPAIR * WD].rearrange("p a (g d) -> p a g d", d=WD)

    def pipeline(eng, iteration):
        def one(j, seq, live):
            iteration(j, seq, lambda lag: layer * N + seq * STEPS + (j - lag + 1), live)
        for j in range(STEPS):
            one(j, 0, lambda lag: lag <= j)
        with eng.Fori(1, B) as seq:
            for j in range(STEPS):
                one(j, seq, lambda lag: True)
        for j in range(LAG):
            one(j, B, lambda lag: lag > j)

    with nc.Block() as block:
        @block.sync
        def _(sp):
            for dst, name in ((m_w1, "m_w1"), (m_w2, "m_w2"), (m_col, "m_col")):
                sp.dma_start(dst[:], h[name][bass.ds(layer, 1)].squeeze(0)).then_inc(S["mlp_weights"], 16)
            sp.wait_ge(S["mlp_weights"], layer * 48 + 48)
            sp.sem_inc(sem("gate"), 1)

        @block.gpsimd
        def _(pool):
            nc.gpsimd.memset(power[:], -0.5).then_inc(S["ready"], 1)
            nc.gpsimd.memset(kT[:, :, 0:WIN], 0.0).then_inc(S["ready"], 1)
            pool.wait_ge(S["ready"], passed(layer * 2 + 2))

            def shift(t, seq):
                src = xT[:, bass.ds(seq, 1), :].rearrange("p b t -> p (b t)")
                lo = PAD - WIN + t * P
                nc.gpsimd.tensor_copy(xs[t][0:64, :], src[0:64, lo:lo + WIN + P]).then_inc(S[f"shifted{t}"], 1)
                made = (layer * (B + 1 - t) + seq) * 2
                pool.wait_ge(S[f"shifted{t}"], passed(made + 1))
                pool.sem_inc(sem("gate"), 1)
                nc.gpsimd.tensor_copy(xs[t][64:P, :], src[64:P, lo - 1:lo - 1 + WIN + P])\
                    .then_inc(S[f"shifted{t}"], 1)
                pool.wait_ge(S[f"shifted{t}"], passed(made + 2))
                pool.sem_inc(sem("gate"), 1)

            pool.sem_inc(sem("gate"), 1)
            shift(0, 0)

            def iteration(j, seq, n, live):
                if live(0):
                    if j % 2 == 0:
                        if live(1):
                            pool.wait_ge(S["v_made"], passed(n(1) * 2))
                            pool.sem_inc(sem("gate"), 1)
                        if j == 0:
                            shift(1, seq)
                        else:
                            shift(0, seq + 1)
                    pool.wait_ge(S["guarded"], passed(n(0)))
                    nc.gpsimd.tensor_tensor(rn[j % 2][:], ss[j % 2][:], power[:], ALU.pow).then_inc(S["rnorm"], 1)
            pipeline(pool, iteration)

        @block.tensor
        def _(pe):
            pe.wait_ge(S["weights"], layer * 48 + 48)

            def iteration(j, seq, n, live):
                t, hh = j // 2, j % 2
                j1, j2, j3 = (j - 1) % STEPS, (j - 2) % STEPS, (j - 3) % STEPS
                x = xs[t]

                def values(a):
                    pe.wait_ge(S["v_taken"], passed((n(0) - 1) * 2 + a))
                    for w in (2 * a, 2 * a + 1):
                        for par in range(2):
                            cols = wqkv[:, 2 * INNER + hh * C:2 * INNER + (hh + 1) * C]\
                                .rearrange("p (g a d) -> p a g d", a=2, d=WD)[:, par]
                            lo = (w - 2 * a) * NPAIR * WD
                            last = nc.tensor.matmul(
                                banks[64 * par:64 * par + 64, 2, lo:lo + NPAIR * WD].rearrange("p (g d) -> p g d", d=WD),
                                x[:, WIN * w:WIN * (w + 2)], cols, start=True, stop=True)
                    last.then_inc(S["v_made"], 1)

                if live(0):
                    pe.wait_ge(S["k_squared"], passed(n(0) - 1))
                    pe.wait_ge(S["q_rotated"], passed((n(0) - 1) * 2))
                    if hh == 0:
                        pe.wait_ge(S[f"shifted{t}"], passed((layer * (B + 1 - t) + seq) * 2 + 2))
                    for i in range(2):
                        last = nc.tensor.matmul(banks[:, i, :], x[:, WIN:], wqkv[:, i * INNER + hh * C:i * INNER + (hh + 1) * C],
                                                start=True, stop=True)
                        last.then_inc(S["qk"], 1)
                if live(0):
                    values(0)
                if live(1):
                    pe.wait_ge(S["normed"], passed(n(1)))
                    if live(3):
                        pe.wait_ge(S["divided"], passed(n(3)))
                    for i in range(2):
                        for g in range(NPAIR):
                            lo = i * C + g * P
                            last = nc.tensor.transpose(banks[:, 3 + i, g * P:(g + 1) * P], t1[j1 % 2][:, lo:lo + P],
                                                       ident[:])
                        last.then_inc(S["turned"], 1)
                if live(2):
                    pe.wait_ge(S["exped"], passed(n(2)))
                    if live(4):
                        pe.wait_ge(S["residual"], passed(n(4)))
                    for g in range(NPAIR):
                        last = nc.tensor.transpose(banks[:, 7, g * P:(g + 1) * P],
                                                   pr[j2 % 2][:, g].rearrange("p a k -> p (a k)"), ident[:])
                    last.then_inc(S["p_turned"], 1)
                if live(0):
                    values(1)
                if live(1):
                    pe.wait_ge(S["k_turned"], passed(n(1)))
                    pe.wait_ge(S["q_turned"], passed(n(1)))
                    if live(2):
                        pe.wait_ge(S["masked"], passed(n(2)))
                    pe.sem_inc(sem("gate"), 1)
                    tk, hk = j1 // 2, j1 % 2
                    for par in range(2):
                        rows = slice(64 * par, 64 * par + 64)
                        for g in range(NPAIR):
                            for w in range(NWIN):
                                last = nc.tensor.matmul(
                                    banks[WIN * w:WIN * (w + 1), 5 + par, g * WD:(g + 1) * WD],
                                    qT[j1 % 2][rows, g, WIN * w:WIN * (w + 1)],
                                    kT[rows, hk * NPAIR + g, tk * P + WIN * w:tk * P + WIN * (w + 2)],
                                    start=True, stop=True)
                    last.then_inc(S["scored"], 1)
                if live(3):
                    if live(2):
                        pe.wait_ge(S["p_taken"], passed(n(2)))
                    else:
                        pe.wait_ge(S["residual"], passed(n(4)))
                    pe.wait_ge(S["divided"], passed(n(3)))
                    for g in range(NPAIR):
                        last = nc.tensor.transpose(banks[:, 7, g * P:(g + 1) * P],
                                                   on[j3 % 2][:, g].rearrange("p a d -> p (a d)"), ident[:])
                    last.then_inc(S["o_turned"], 1)
                if live(2):
                    pe.wait_ge(S["p_taken"], passed(n(2)))
                    pe.wait_ge(S["v_taken"], passed(n(2) * 2))
                    pe.sem_inc(sem("gate"), 1)
                    for par in range(2):
                        rows = slice(64 * par, 64 * par + 64)
                        for g in range(NPAIR):
                            for w in range(NWIN):
                                last = nc.tensor.matmul(
                                    banks[WIN * w:WIN * (w + 1), 3 + par, g * WD:(g + 1) * WD],
                                    prT[rows, g, WIN * w:WIN * (w + 1)], vd[j2][rows, w, g * WD:(g + 1) * WD],
                                    start=True, stop=True)
                    last.then_inc(S["valued"], 1)
                if live(3):
                    pe.wait_ge(S["o_taken"], passed(n(3)))
                    for g in range(NPAIR):
                        last = nc.tensor.matmul(banks[:, 7, 0:P], wo[:, j3 % 2 * NPAIR + g, :], oT[j3 % 2][:, g, :],
                                                start=(g == 0), stop=(g == NPAIR - 1))
                    last.then_inc(S["projected"], 1)
            pipeline(pe, iteration)

        @block.vector
        def _(dve):
            dve.wait_ge(S["weights"], layer * 48 + 48)
            nc.vector.tensor_tensor(tab[:], base[:], scl[:].unsqueeze(1).broadcast_to([P, 2 * TILES, 2 * WD]),
                                    ALU.mult).then_inc(S["tabled"], 1)
            dve.wait_ge(S["tabled"], passed(layer + 1))

            def iteration(j, seq, n, live):
                t = j // 2
                j1, j2, j3 = (j - 1) % STEPS, (j - 2) % STEPS, (j - 3) % STEPS
                if live(4):
                    dve.wait_ge(S["projected"], passed(n(4)))
                    s = seq - 1
                    lo = PAD + (j // 2) * P
                    rows = xT[:, bass.ds(s, 1), lo:lo + P].rearrange("p b t -> p (b t)")
                    nc.vector.tensor_tensor(rows, rows, banks[:, 7, 0:P], ALU.add).then_inc(S["residual"], 1)
                if live(0):
                    for i, name in ((1, "k_rotated"), (0, "q_rotated")):
                        if i == 1:
                            dve.wait_ge(S["qk"], passed(n(0) * 2))
                            if live(2):
                                dve.wait_ge(S["turned"], passed(n(2) * 2))
                        else:
                            dve.wait_ge(S["q_squared"], passed(n(0)))
                        src = banks[:, i, :].rearrange("p (h d) -> p h d", d=WD)
                        for cs, dst in ((0, t1), (1, t2)):
                            nc.vector.tensor_tensor(
                                dst[j % 2][:, i * C:(i + 1) * C].rearrange("p (h d) -> p h d", d=WD), src,
                                tab[:, 2 * t + cs, i * WD:(i + 1) * WD].unsqueeze(1).broadcast_to([P, HALF, WD]),
                                ALU.mult).then_inc(S[name], 1)
                    dve.wait_ge(S["k_squared"], passed(n(0)))
                    nc.vector.tensor_reduce(ss[j % 2][:], sq[:].rearrange("p a h d -> p (a h) d"), AX, ALU.add)\
                        .then_inc(S["sums"], 1)
                    dve.wait_ge(S["sums"], passed(n(0)))
                    nc.vector.tensor_scalar(ss[j % 2][:], ss[j % 2][:], 1e-24, None, ALU.max)\
                        .then_inc(S["guarded"], 1)
                if live(1):
                    dve.wait_ge(S["scored"], passed(n(1)))
                    p = pr[j1 % 2]
                    rows = p[:].rearrange("p g a k -> p (g a) k")
                    nc.vector.tensor_tensor(p[:].rearrange("p g a k -> p a g k"),
                                            mask[:, j1 // 2, :].unsqueeze(1).unsqueeze(1)
                                            .broadcast_to([P, 2, NPAIR, 2 * WIN]), pairs(5), ALU.subtract)\
                        .then_inc(S["masked"], 1)
                    dve.wait_ge(S["masked"], passed(n(1)))
                    nc.vector.tensor_reduce(mn[j1 % 2][:], rows, AX, ALU.min).then_inc(S["minned"], 1)
                if live(2):
                    dve.wait_ge(S["exped"], passed(n(2)))
                    nc.vector.reciprocal(rl[j2 % 2][:], tot[j2 % 2][:]).then_inc(S["inverse"], 1)
                    dve.wait_ge(S["inverse"], passed(n(2)))
                if live(0):
                    dve.wait_ge(S["q_rotated"], passed(n(0) * 2))
                    v1 = t1[j % 2][:].rearrange("p (h s d) -> p h s d", s=2, d=WD // 2)
                    v2 = t2[j % 2][:].rearrange("p (h s d) -> p h s d", s=2, d=WD // 2)
                    nc.vector.tensor_tensor(v1, v1, v2[:, :, ::-1, :], ALU.add).then_inc(S["added"], 1)
                    dve.wait_ge(S["rnorm"], passed(n(0)))
                    dve.wait_ge(S["added"], passed(n(0)))
                    v1 = t1[j % 2][:].rearrange("p (h d) -> p h d", d=WD)
                    nc.vector.tensor_tensor(v1, v1, rn[j % 2][:].unsqueeze(2).broadcast_to([P, 2 * HALF, WD]),
                                            ALU.mult).then_inc(S["normed"], 1)
                if live(2):
                    dve.wait_ge(S["valued"], passed(n(2)))
                    nc.vector.tensor_tensor(on[j2 % 2][:].rearrange("p g a d -> p a g d"), pairs(3),
                                            rl[j2 % 2][:].rearrange("p (g a) -> p a g", a=2).unsqueeze(3)
                                            .broadcast_to([P, 2, NPAIR, WD]), ALU.mult).then_inc(S["divided"], 1)
            pipeline(dve, iteration)

        @block.scalar
        def _(act):
            def iteration(j, seq, n, live):
                j1, j2, j3 = (j - 1) % STEPS, (j - 2) % STEPS, (j - 3) % STEPS

                def values(a):
                    act.wait_ge(S["v_made"], passed((n(0) - 1) * 2 + a + 1))
                    nc.scalar.activation(vd[j][:, 2 * a:2 * a + 2, :].rearrange("p w n -> p (w n)"), banks[:, 2, :],
                                         ACT.Copy).then_inc(S["v_taken"], 1)
                if live(0):
                    act.wait_ge(S["qk"], passed(n(0) * 2 - 1))
                    act.wait_ge(S["sums"], passed(n(0) - 1))
                    nc.scalar.activation(sq[:, 0].rearrange("p h d -> p (h d)"), banks[:, 0, :], ACT.Square)\
                        .then_inc(S["q_squared"], 1)
                if live(0):
                    values(0)
                    act.wait_ge(S["k_rotated"], passed(n(0) * 2))
                    nc.scalar.activation(sq[:, 1].rearrange("p h d -> p (h d)"), banks[:, 1, :], ACT.Square)\
                        .then_inc(S["k_squared"], 1)
                if live(1):
                    act.wait_ge(S["turned"], passed(n(1) * 2))
                    nc.scalar.activation(qT[j1 % 2][:].rearrange("p g q -> p (g q)"), banks[:, 3, :], ACT.Copy)\
                        .then_inc(S["q_turned"], 1)
                    hk, lo = j1 % 2, WIN + (j1 // 2) * P
                    nc.scalar.activation(kT[:, hk * NPAIR:(hk + 1) * NPAIR, lo:lo + P],
                                         banks[:, 4, :].rearrange("p (g k) -> p g k", k=P), ACT.Copy)\
                        .then_inc(S["k_turned"], 1)
                if live(2):
                    act.wait_ge(S["p_turned"], passed(n(2)))
                    nc.scalar.activation(prT[:].rearrange("p g q -> p (g q)"), banks[:, 7, :], ACT.Copy)\
                        .then_inc(S["p_taken"], 1)
                if live(0):
                    values(1)
                if live(3):
                    act.wait_ge(S["o_turned"], passed(n(3)))
                    nc.scalar.activation(oT[j3 % 2][:].rearrange("p g q -> p (g q)"), banks[:, 7, :], ACT.Copy)\
                        .then_inc(S["o_taken"], 1)
                if live(1):
                    act.wait_ge(S["minned"], passed(n(1)))
                    for g in range(NPAIR):
                        for par in range(2):
                            row, i = pr[j1 % 2][:, g, par, :], 2 * g + par
                            last = nc.scalar.activation(row, row, ACT.Exp, bias=mn[j1 % 2][:, i:i + 1], scale=-1.0,
                                                        accum_out=tot[j1 % 2][:, i:i + 1])
                    last.then_inc(S["exped"], 1)
            pipeline(act, iteration)


def load_window_weights(sp, weights, h, layer, wqkv, wo, scl):
    def of(name):
        return h[name][bass.ds(layer, 1)] if not isinstance(layer, int) else h[name][layer:layer + 1]
    sp.dma_start(wqkv[:], of("w_qkv").squeeze(0)).then_inc(weights, 16)
    sp.dma_start(wo[:], of("w_o").squeeze(0)).then_inc(weights, 16)
    sp.dma_start(scl[:], of("w_scl").broadcast_to([P, 2 * WD])).then_inc(weights, 16)


@scoped
def gated_mlp(nc, sem, sb, layer, xT, norm, banks, w1, w2, col):
    gel = [sb(f"m_gel{m}", [MC, CH]) for m in range(MG)]
    hid = [[sb(f"m_hid{k}{m}", [MC, CH]) for m in range(MG)] for k in range(2)]
    up, gelued, made = sem("m_up"), sem("m_gelued"), sem("m_made")
    down, residual, weights = sem("m_down"), sem("m_residual"), sem("w_weights")
    done = layer * NCH

    def b1(m, vg):
        return col[0:MC, 3 + 2 * m + vg:4 + 2 * m + vg]

    with nc.Block() as block:
        @block.sync
        def _(sp):
            sp.wait_ge(weights, (layer + 2) * 48)
            sp.sem_inc(sem("gate"), 1)

        @block.tensor
        def _(pe):
            def w_up(c, m, first=False):
                if not first:
                    pe.wait_ge(made, passed((done + c - 1) * MG + m + 1))
                for vg in range(2):
                    last = nc.tensor.matmul(banks[0:MC, 2 * m + vg, :], w1[:, 2 * m + vg, :],
                                            norm[:, bass.ds(c * CH, CH)], start=True, stop=True)
                last.then_inc(up, 1)

            def w_down(c, k, m):
                if m == 0:
                    pe.wait_ge(residual, passed(done + c - k))
                pe.wait_ge(made, passed((done + c) * MG + m + 1))
                last = nc.tensor.matmul(banks[:, 6 + k, :], w2[:, m, :], hid[k][m][:],
                                        start=(m == 0), stop=(m == MG - 1))
                if m == MG - 1:
                    last.then_inc(down, 1)

            for m in range(MG):
                w_up(0, m, True)
            with pe.Fori(0, NCH // 2 - 1) as i:
                for k in range(2):
                    for m in range(MG):
                        w_up(i * 2 + k + 1, m)
                        w_down(i * 2 + k, k, m)
            for m in range(MG):
                w_up(NCH - 1, m)
                w_down(NCH - 2, 0, m)
            for m in range(MG):
                w_down(NCH - 1, 1, m)

        @block.scalar
        def _(act):
            def gelus(c, first=False):
                for m in range(MG):
                    act.wait_ge(up, passed((done + c) * MG + m + 1))
                    if not first:
                        act.wait_ge(made, passed((done + c - 1) * MG + m + 1))
                    nc.scalar.activation(gel[m][:], banks[0:MC, 2 * m + 1, :], ACT.Gelu, bias=b1(m, 1))\
                        .then_inc(gelued, 1)

            gelus(0, True)
            gelus(1)
            with act.Fori(1, NCH // 2) as i:
                gelus(i * 2)
                gelus(i * 2 + 1)

        @block.vector
        def _(dve):
            def hidden(c, k):
                for m in range(MG):
                    dve.wait_ge(gelued, passed((done + c) * MG + m + 1))
                    nc.vector.scalar_tensor_tensor(out=hid[k][m][:], in0=banks[0:MC, 2 * m, :], scalar=b1(m, 0),
                                                   in1=gel[m][:], op0=ALU.add, op1=ALU.mult).then_inc(made, 1)

            def add(c, k):
                dve.wait_ge(down, passed(done + c + 1))
                rows = xT[:, bass.ds(c * PER, PER), PAD:PAD + T]
                nc.vector.scalar_tensor_tensor(out=rows, in0=banks[:, 6 + k, :].rearrange("p (b t) -> p b t", b=PER),
                                               scalar=col[:, 2:3], in1=rows, op0=ALU.add, op1=ALU.add)\
                    .then_inc(residual, 1)

            hidden(0, 0)
            with dve.Fori(0, NCH // 2 - 1) as i:
                for k in range(2):
                    hidden(i * 2 + k + 1, 1 - k)
                    add(i * 2 + k, k)
            hidden(NCH - 1, 1)
            add(NCH - 2, 0)
            add(NCH - 1, 1)


def arranged(x, **w):
    f = np.float32
    h = {k: np.asarray(v) for k, v in w.items()}
    t = {}
    t["x"] = np.asarray(x).transpose(2, 0, 1)
    t["ident"] = np.eye(P, dtype=f)
    t["a_w"] = np.stack([h["L0_attn_" + n].T for n in ("Wq", "Wk", "Wv", "Wo")], 1)
    p = np.arange(P)
    t["a_hm"] = (p[:, None] // AD == np.arange(AH)).astype(f)
    t["a_mask"] = np.stack([np.zeros((P, P)), np.where(p[None] <= p[:, None], 0, NEG)], 1).astype(f)
    t["e_wr"] = h["L0_ffn_Wr"].T
    t["e_a"] = h["L0_ffn_A"].reshape(EC, P, D).transpose(1, 0, 2)
    t["e_b"] = h["L0_ffn_Bw"].transpose(0, 2, 1).reshape(EC, P, D).transpose(1, 0, 2)
    t["e_spread"] = (np.arange(E * R)[None] // R == np.arange(E)[:, None]).astype(f)
    t["e_before"] = (np.arange(E)[None] < np.arange(E)[:, None]).astype(f)

    def swapped(m):
        return m.reshape(D, RH, 2, RK // 2)[:, :, ::-1].reshape(D, RH * RK)
    t["r_w"] = np.stack([h["L1_attn_Wq"], swapped(h["L1_attn_Wq"]), h["L1_attn_Wk"], swapped(h["L1_attn_Wk"])], 1)
    t["r_wv"], t["r_wg"] = h["L1_attn_Wv"], h["L1_attn_Wg"]
    t["r_wo"] = h["L1_attn_Wo"].reshape(2, P, D).transpose(1, 0, 2)
    t["r_gn"] = h["L1_attn_gn_weight"]
    freq = (f(1) / f(10000) ** (np.arange(0, RK, 2, dtype=f) / f(RK))).astype(f)
    ang = (np.arange(T, dtype=f)[None] * freq[:, None]).astype(f)
    cos, sin = np.tile(np.cos(ang), (2 * RH, 1)), np.tile(np.concatenate([-np.sin(ang), np.sin(ang)]), (RH, 1))
    both = np.stack([cos, sin], 1)
    t["r_tab"] = np.stack([both * f(RK ** -0.5), both], 2).astype(f)
    gamma = 1 - 2.0 ** (-5.0 - np.arange(RH))
    rel = np.arange(T)[None] - p[:, None]
    t["r_decay"] = np.where(rel[:, None] >= 0, gamma[None, :, None] ** np.maximum(rel, 0)[:, None], 0).astype(f)

    half = np.arange(0, WD, 2, dtype=f)
    freq = (f(1) / f(10000) ** (half / f(WD))).astype(f)
    pos = np.arange(T, dtype=f)
    ang = (pos[:, None] * freq[None]).astype(f)
    power = ((pos - T // 2) / f(WIN // 2)).astype(f)
    scale = ((half + f(0.4 * WD)) / f(1.4 * WD)).astype(f)[None] ** power[:, None]
    cos, sin = np.cos(ang), np.sin(ang)
    tab = np.stack([np.stack([np.concatenate([cos * m, cos * m], 1) for m in (scale * f(8), 1 / scale)], 1),
                    np.stack([np.concatenate([sin * m, -sin * m], 1) for m in (scale * f(8), 1 / scale)], 1)], 1)
    t["w_base"] = tab.reshape(TILES, P, 2, 2 * WD).transpose(1, 0, 2, 3).reshape(P, 2 * TILES, 2 * WD).astype(f)
    i, j = (p % WIN)[:, None], np.arange(2 * WIN)[None]
    seen = (j >= i) & (j <= i + WIN)
    first = seen & ((j >= WIN) | (p[:, None] >= WIN))
    t["w_mask"] = np.where(np.stack([first] + [seen] * (TILES - 1), 1), 0, -NEG).astype(f)
    t["w_qkv"] = h["L1_ffn_Wqkv"]
    t["w_o"] = h["L1_ffn_Wo"].reshape(DEPTH, WH // 2, P, D).transpose(0, 2, 1, 3)
    t["w_scl"] = np.concatenate([h["L1_ffn_q_scale"], h["L1_ffn_k_scale"]], 1)

    def groups(m):
        m = m.reshape(*m.shape[:-1], 2, MLP)
        m = np.concatenate([m, np.zeros((*m.shape[:-1], MG * MC - MLP), m.dtype)], -1)
        return np.moveaxis(m.reshape(*m.shape[:-1], MG, MC), -2, -3).reshape(*m.shape[:-2], 2 * MG, MC)
    t["m_w1"] = groups(h["L1_ffn_W1"])
    w2 = h["L1_ffn_W2"]
    w2 = np.concatenate([w2, np.zeros((DEPTH, MG * MC - MLP, D), w2.dtype)], 1)
    t["m_w2"] = w2.reshape(DEPTH, MG, MC, D).transpose(0, 2, 1, 3)
    b1 = groups(h["L1_ffn_b1"])
    b1 = np.concatenate([b1, np.zeros((DEPTH, 2 * MG, P - MC), b1.dtype)], 2).transpose(0, 2, 1)
    t["m_col"] = np.concatenate([np.stack([h["L1_ffn_ln_g"], h["L1_ffn_ln_b"], h["L1_ffn_b2"]], 2), b1], 2)
    return {k: np.ascontiguousarray(v) for k, v in t.items()}


def kernel(L0_attn_x, **weights):
    from concourse import bacc
    from concourse.bass_utils import run_bass_kernel_spmd

    nc = bacc.Bacc("TRN2", target_bir_lowering=False, num_devices=1)
    arrays = arranged(L0_attn_x, **weights)
    h = {k: nc.dram_tensor(k + "_in", a.shape, mybir.dt.from_np(a.dtype), kind="ExternalInput").ap()
         for k, a in arrays.items()}
    out = nc.dram_tensor("out", (D, B, T), F32, kind="ExternalOutput").ap()
    program(nc, h, out)
    r = run_bass_kernel_spmd(nc, [{k + "_in": a for k, a in arrays.items()}], core_ids=[0])
    return np.ascontiguousarray(r.results[0]["out"].transpose(1, 2, 0))
```

```python
from contextlib import ExitStack

import numpy as np

import concourse.bass as bass
from concourse import mybir

F32 = mybir.dt.float32
ALU = mybir.AluOpType
ACT = mybir.ActivationFunctionType
AX = mybir.AxisListType.X

P = 128
B, T, D = 16, 256, 128
PAD = 40
TILES = T // P
NEG = -1e30
EPS = 1e-5

CH = 512
NCH = B * T // CH
BEHIND = 2
PER = CH // T

AH, AD = 16, 8
A_SCALE = 1.0 / float(np.sqrt(np.float32(AD)))

E, R = 8, 64
EC = E * R // P

RH, RK, RV = 4, 32, 64

DEPTH, WH, WD, WIN = 6, 16, 64, 32
INNER = WH * WD
HALF = 8
STEPS = TILES * (WH // HALF)
NPAIR = HALF // 2
NWIN = P // WIN
MLP = 341
MC, MG = 114, 3

COUNTED = """
ln_mean ln_centred ln_squared ln_var ln_logged ln_inverse ln_scaled
a_xcopy a_proj a_vproj a_qmasked a_ktaken a_vtaken a_scored a_masked a_maxed a_biased a_exped a_turned a_taken
a_summed a_totalled a_odone a_oturned a_otaken a_wo_done a_added
e_gated e_mixed e_made e_applied e_added
r_xcopy r_qk r_vg r_qktaken r_rotated r_vgtaken r_scored r_decayed r_summed r_squared r_sums r_ssum r_inv
r_weighted r_scaled r_kmasked
r_gated r_turned r_took r_wo r_added r_ready
w_shifted0 w_shifted1 w_qk w_q_squared w_k_squared w_k_rotated w_q_rotated w_sums w_guarded w_added w_rnorm
w_normed w_turned w_k_turned w_q_turned w_v_made w_v_taken w_scored w_masked w_maxed w_biased w_exped
w_inverse w_p_turned w_p_taken w_valued w_divided w_o_turned w_o_taken w_projected w_residual w_ready w_tabled
m_up m_gelued m_made m_down m_residual
""".split()


def passed(count):
    return count + 1


def scoped(phase):
    def run(nc, sem, *args):
        with ExitStack() as stack:
            phase(nc, sem, lambda name, shape: stack.enter_context(nc.sbuf_tensor(name, shape, F32)), *args)
    return run


def program(nc, h, out):
    def sb(name, shape):
        return nc.alloc_sbuf_tensor(name, shape, F32)

    sems = {}

    def sem(name):
        if name not in sems:
            sems[name] = nc.alloc_semaphore(name)
        return sems[name]

    xT = sb("xT", [P, B + 1, PAD + T])
    ident = sb("ident", [P, P])
    mean_w = sb("mean_w", [P, P])
    half_mean = [sb(f"half_mean{i}", [P, P]) for i in range(2)]
    norm = sb("norm", [P, B * T])
    logv = sb("logv", [P, B * T])
    eps_col = sb("eps_col", [P, 1])
    banks = nc.alloc_psum_tensor("banks", [P, 8, 512], F32)

    a_w = sb("a_w", [P, 4, P])
    a_hm = sb("a_hm", [P, AH])
    a_mask = sb("a_mask", [P, 2, P])
    e_wr = sb("e_wr", [P, E])
    e_a = sb("e_a", [P, EC, P])
    e_b = sb("e_b", [P, EC, P])
    e_spread = sb("e_spread", [E, EC * P])
    e_before = sb("e_before", [B, E, E])
    r_w = sb("r_w", [P, 4, P])
    r_hm = sb("r_hm", [P, RH])
    r_wv = sb("r_wv", [P, RH * RV])
    r_wg = sb("r_wg", [P, RH * RV])
    r_wo = sb("r_wo", [P, 2, P])
    r_gn = sb("r_gn", [P, RV])
    r_tab = sb("r_tab", [P, 2, 2, T])
    r_decay = sb("r_decay", [P, RH, T])

    w_qkv = sb("w_qkv", [P, 3 * INNER])
    w_o = sb("w_o", [P, WH // 2, P])
    w_base = sb("w_base", [P, 2 * TILES, 2 * WD])
    w_scl = sb("w_scl", [P, 2 * WD])
    w_tab = sb("w_tab", [P, 2 * TILES, 2 * WD])
    w_mask = sb("w_mask", [P, TILES, 2 * WIN])
    m_w1 = sb("m_w1", [P, 2 * MG, MC])
    m_w2 = sb("m_w2", [MC, MG, P])
    m_col = sb("m_col", [P, 3 + 2 * MG])

    loaded = sem("loaded")
    n_loads = [0]

    with nc.Block() as block:
        @block.sync
        def _(sp):
            def load(dst, src):
                sp.dma_start(dst, src).then_inc(loaded, 16)
                n_loads[0] += 1
            for b in range(0, B, 4):
                load(xT[:, b:b + 4, PAD:], h["x"][:, b:b + 4, :])
            for dst, name in ((ident, "ident"), (a_w, "a_w"), (a_hm, "a_hm"), (a_mask, "a_mask"),
                              (e_wr, "e_wr"), (e_a, "e_a"), (e_b, "e_b"), (e_spread, "e_spread"),
                              (r_w, "r_w"), (r_wv, "r_wv"), (r_wg, "r_wg"), (r_wo, "r_wo"),
                              (r_tab, "r_tab"), (r_hm, "r_hm"), (r_decay, "r_decay"), (w_base, "w_base"),
                              (w_mask, "w_mask")):
                load(dst[:], h[name])
            load(e_before[:], h["e_before"].partition_broadcast(B))
            load(r_gn[:], h["r_gn"].partition_broadcast(P))
            load_window_weights(sp, sem("w_weights"), h, 0, w_qkv, w_o, w_scl)
            for name in COUNTED:
                sp.sem_inc(sem(name), 1)
            sp.wait_ge(loaded, 16 * n_loads[0])

        @block.vector
        def _(dve):
            nc.vector.memset(xT[:, :, 0:PAD], 0.0)
            nc.vector.memset(xT[:, B, PAD:], 0.0)
            nc.vector.memset(mean_w[:], 1.0 / D)
            for i in range(2):
                for half in range(2):
                    nc.vector.memset(half_mean[i][64 * half:64 * half + 64], 1.0 / D if half == i else 0.0)
            nc.vector.memset(eps_col[:], EPS)

    layer_norm(nc, sem, 0, False, xT, norm, logv, mean_w, half_mean, eps_col, banks, None)
    head_attention(nc, sem, xT, norm, banks, ident, a_w, a_hm, a_mask)
    layer_norm(nc, sem, 1, False, xT, norm, logv, mean_w, half_mean, eps_col, banks, None)
    experts(nc, sem, xT, norm, banks, ident, e_wr, e_a, e_b, e_spread, e_before)
    layer_norm(nc, sem, 2, False, xT, norm, logv, mean_w, half_mean, eps_col, banks, None)
    retention(nc, sem, xT, norm, logv, banks, ident, eps_col, r_w, r_wv, r_wg, r_wo, r_gn, r_tab, r_decay, r_hm)

    layer_norm(nc, sem, 3, False, xT, norm, logv, mean_w, half_mean, eps_col, banks, None)
    kept = sb("kept", [P, B, T])
    moved = sem("moved")
    with nc.Block() as block:
        @block.vector
        def _(dve):
            for b in range(0, B, PER):
                nc.vector.tensor_copy(kept[:, b:b + PER, :], xT[:, b:b + PER, PAD:PAD + T]).then_inc(moved, 1)

        @block.scalar
        def _(act):
            for b in range(0, B, PER):
                act.wait_ge(moved, b // PER + 1)
                nc.scalar.activation(xT[:, b:b + PER, PAD:PAD + T],
                                     norm[:, b * T:(b + PER) * T].rearrange("p (b t) -> p b t", b=PER), ACT.Copy)

    with nc.Fori(0, DEPTH) as layer:
        window_attention(nc, sem, layer, h, xT, norm, logv, banks, ident, w_qkv, w_o, w_base, w_scl, w_tab,
                         w_mask, m_w1, m_w2, m_col)
        layer_norm(nc, sem, layer + 4, True, xT, norm, logv, mean_w, half_mean, eps_col, banks, m_col,
                   lambda sp: load_window_weights(sp, sem("w_weights"), h, (layer + 1) % DEPTH, w_qkv, w_o, w_scl))
        gated_mlp(nc, sem, layer, xT, norm, banks, m_w1, m_w2, m_col)

    stored, summed = sem("stored"), sem("summed")
    with nc.Block() as block:
        @block.vector
        def _(dve):
            for b in range(0, B, PER):
                nc.vector.tensor_tensor(kept[:, b:b + PER, :], kept[:, b:b + PER, :], xT[:, b:b + PER, PAD:PAD + T],
                                        ALU.add).then_inc(summed, 1)

        @block.sync
        def _(sp):
            for b in range(0, B, PER):
                sp.wait_ge(summed, b // PER + 1)
                sp.dma_start(out[:, b:b + PER, :], kept[:, b:b + PER, :]).then_inc(stored, 16)
            sp.wait_ge(stored, 16 * (B // PER))


def layer_norm(nc, sem, turn, mlp, xT, norm, logv, mean_w, half_mean, eps_col, banks, col, prefetch=None):
    mean_in, centred = sem("ln_mean"), sem("ln_centred")
    squared, var_in, logged = sem("ln_squared"), sem("ln_var"), sem("ln_logged")
    inverse, scaled = sem("ln_inverse"), sem("ln_scaled")
    done = NCH * turn

    parts = [(slice(0, P // 2), 0), (slice(P // 2, P), 1)] if mlp else [(slice(0, P), 0)]
    mean_of = half_mean if mlp else [mean_w]

    def chunk(buf, c):
        return buf[:, c * CH:(c + 1) * CH]

    def of(buf):
        return buf.rearrange("p (b t) -> p b t", b=PER)

    def stream(c, rows, back):
        return xT[rows, c * PER:(c + 1) * PER, PAD - back:PAD - back + T]

    with nc.Block() as block:
        if prefetch:
            @block.sync
            def _(sp):
                prefetch(sp)

        @block.tensor
        def _(pe):
            def variance(c):
                pe.wait_ge(squared, passed(done + c + 1))
                nc.tensor.matmul(banks[:, c, :], mean_w[:], chunk(logv, c), start=True, stop=True).then_inc(var_in, 1)

            for c in range(NCH):
                for m, (rows, back) in zip(mean_of, parts):
                    last = nc.tensor.matmul(of(banks[:, c, :]), m[:], stream(c, slice(0, P), back),
                                            start=(rows.start == 0), stop=(rows.stop == P))
                last.then_inc(mean_in, 1)
                if c >= BEHIND:
                    variance(c - BEHIND)
            for c in range(NCH - BEHIND, NCH):
                variance(c)

        @block.vector
        def _(dve):
            for c in range(NCH):
                dve.wait_ge(mean_in, passed(done + c + 1))
                for rows, back in parts:
                    nc.vector.tensor_tensor(of(chunk(norm, c)[rows]), stream(c, rows, back),
                                            of(banks[rows, c, :]), ALU.subtract).then_inc(centred, 2 // len(parts))
            dve.wait_ge(centred, passed((done + NCH) * 2))
            for c in range(NCH):
                dve.wait_ge(inverse, passed(done + c + 1))
                nc.vector.tensor_tensor(chunk(norm, c), chunk(norm, c), chunk(logv, c), ALU.mult).then_inc(scaled, 1)
            if mlp:
                dve.wait_ge(scaled, passed(done + NCH))
                for c in range(NCH // 2, NCH):
                    nc.vector.tensor_scalar(chunk(norm, c), chunk(norm, c), col[:, 0:1], col[:, 1:2],
                                            ALU.mult, ALU.add)

        @block.gpsimd
        def _(pool):
            for c in range(NCH):
                pool.wait_ge(centred, passed((done + c + 1) * 2))
                nc.gpsimd.tensor_tensor(chunk(logv, c), chunk(norm, c), chunk(norm, c), ALU.mult).then_inc(squared, 1)

        @block.scalar
        def _(act):
            for c in range(NCH):
                act.wait_ge(var_in, passed(done + c + 1))
                nc.scalar.activation(chunk(logv, c), banks[:, c, :], ACT.Ln, bias=eps_col[:]).then_inc(logged, 1)
            act.wait_ge(logged, passed(done + NCH))
            for c in range(NCH):
                nc.scalar.activation(chunk(logv, c), chunk(logv, c), ACT.Exp, scale=-0.5).then_inc(inverse, 1)
            if mlp:
                for c in range(NCH // 2):
                    act.wait_ge(scaled, passed(done + c + 1))
                    nc.scalar.activation(chunk(norm, c), chunk(norm, c), ACT.Identity, bias=col[:, 1:2],
                                         scale=col[:, 0:1])


@scoped
def head_attention(nc, sem, sb, xT, norm, banks, ident, w, head_mask, mask):
    xa = sb("a_x", [P, T])
    q = sb("a_q", [P, T])
    kT = sb("a_kT", [P, T])
    qm = [sb(f"a_qm{i}", [P, 4, T]) for i in range(2)]
    v = sb("a_v", [P, TILES, P])
    KEYS = [P, 2 * P]
    probs = [sb(f"a_probs{i}", [P, 4 * 3 * P]) for i in range(2)]
    probsT = [sb(f"a_probsT{i}", [P, 12, P]) for i in range(2)]
    mx = sb("a_max", [P, 2, 8])
    bias = sb("a_bias", [P, 2, 8])
    total = sb("a_total", [P, 4, 2, 4])
    rtotal = sb("a_rtotal", [P, 4, 2, 4])
    o = sb("a_o", [P, TILES, P])
    oT = sb("a_oT", [P, T])

    xcopy, proj, vproj = sem("a_xcopy"), sem("a_proj"), sem("a_vproj")
    qmasked, ktaken, vtaken = sem("a_qmasked"), sem("a_ktaken"), sem("a_vtaken")
    scored, masked, maxed, biased = sem("a_scored"), sem("a_masked"), sem("a_maxed"), sem("a_biased")
    exped, turned, taken, summed = sem("a_exped"), sem("a_turned"), sem("a_taken"), sem("a_summed")
    totalled, odone, oturned, otaken = sem("a_totalled"), sem("a_odone"), sem("a_oturned"), sem("a_otaken")
    wo_done, added = sem("a_wo_done"), sem("a_added")

    def part(buf, tile):
        lo = 0 if tile == 0 else 4 * P
        return buf[:, lo:lo + 4 * KEYS[tile]].rearrange("p (s k) -> p s k", s=4)

    def score_bank(tile):
        if tile == 0:
            return banks[:, 2, :].rearrange("p (s k) -> p s k", s=4)
        return banks[:, 3:5, :].rearrange("p b (s k) -> p (b s) k", s=2)

    def pipeline(eng, sequence):
        sequence(0, True, False)
        with eng.Fori(1, B - 1) as b:
            sequence(b, False, False)
        sequence(B - 1, False, True)

    def ahead(b, r):
        return (b, r + 2) if r < 2 else (b + 1, r - 2)

    with nc.Block() as block:
        @block.gpsimd
        def _(pool):
            def copy(b):
                pool.wait_ge(vproj, passed(b))
                pool.sem_inc(sem("gate"), 1)
                nc.gpsimd.tensor_copy(xa[:], norm[:, bass.ds(b * T, T)]).then_inc(xcopy, 1)

            def mask_queries(b, r, early=False):
                if not early:
                    pool.wait_ge(scored, passed(b * 4 + r - 1))
                if r == 0:
                    pool.wait_ge(ktaken, passed(b + 1))
                heads = head_mask[:, 4 * r:4 * r + 4].unsqueeze(2).broadcast_to([P, 4, T])
                nc.gpsimd.tensor_tensor(qm[r % 2][:], q[:].unsqueeze(1).broadcast_to([P, 4, T]), heads,
                                        ALU.mult).then_inc(qmasked, 1)

            def sequence(b, first, last):
                mask_queries(b, 2)
                mask_queries(b, 3)
                if not last:
                    copy(b + 1)
                    mask_queries(b + 1, 0)
                    mask_queries(b + 1, 1)

            copy(0)
            mask_queries(0, 0, True)
            mask_queries(0, 1, True)
            pipeline(pool, sequence)

        @block.tensor
        def _(pe):
            def project(b):
                pe.wait_ge(xcopy, passed(b + 1))
                nc.tensor.matmul(banks[:, 0, 0:T], w[:, 0, :], xa[:], start=True, stop=True)
                nc.tensor.matmul(banks[:, 0, T:2 * T], w[:, 1, :], xa[:], start=True, stop=True).then_inc(proj, 1)

            def project_values(b):
                pe.wait_ge(ktaken, passed(b + 1))
                for t in range(TILES):
                    last = nc.tensor.matmul(banks[:, 0, t * P:(t + 1) * P], xa[:, t * P:(t + 1) * P], w[:, 2, :],
                                            start=True, stop=True)
                last.then_inc(vproj, 1)

            def scores(b, r):
                n = b * 4 + r
                pe.wait_ge(qmasked, passed(n + 1))
                if r == 0:
                    pe.wait_ge(ktaken, passed(b + 1))
                pe.wait_ge(masked, passed(n * 2))
                for t in range(TILES):
                    for s in range(4):
                        last = nc.tensor.matmul(score_bank(t)[:, s, :], qm[r % 2][:, s, t * P:(t + 1) * P],
                                                kT[:, 0:KEYS[t]], start=True, stop=True)
                last.then_inc(scored, 1)

            def turn(b, r):
                n = b * 4 + r
                pe.wait_ge(exped, passed(n + 1))
                pe.wait_ge(taken, passed(n * 2))
                for j in range(12):
                    last = nc.tensor.transpose(banks[:, 5 + j // 4, (j % 4) * P:(j % 4 + 1) * P],
                                               probs[r % 2][:, j * P:(j + 1) * P], ident[:])
                last.then_inc(turned, 1)

            def values(b, r):
                n = b * 4 + r
                if r == 0:
                    pe.wait_ge(odone, passed(b))
                    pe.wait_ge(vtaken, passed(b + 1))
                pe.wait_ge(taken, passed(n * 2 + 2))
                pt = probsT[r % 2]
                for s in range(4):
                    hd = 4 * r + s
                    cols = slice(hd * AD, (hd + 1) * AD)
                    nc.tensor.matmul(banks[:, 1, hd * AD:(hd + 1) * AD], pt[:, s, :], v[:, 0, cols],
                                     start=True, stop=True)
                    for k in range(2):
                        last = nc.tensor.matmul(banks[:, 1, P + hd * AD:P + (hd + 1) * AD],
                                                pt[:, 4 + 2 * s + k, :], v[:, k, cols],
                                                start=(k == 0), stop=(k == 1))
                last.then_inc(summed, 1)

            def turn_outputs(b):
                pe.wait_ge(vtaken, passed(b + 1))
                pe.wait_ge(odone, passed(b + 1))
                for t in range(TILES):
                    last = nc.tensor.transpose(banks[:, 0, t * P:(t + 1) * P], o[:, t, :], ident[:])
                last.then_inc(oturned, 1)

            def project_outputs(b):
                pe.wait_ge(otaken, passed(b + 1))
                nc.tensor.matmul(banks[:, 0, T:2 * T], w[:, 3, :], oT[:], start=True, stop=True).then_inc(wo_done, 1)

            def sequence(b, first, last):
                for r in range(4):
                    turn(b, r)
                    if r == 0 and not first:
                        pe.wait_ge(vtaken, passed(b + 1))
                        turn_outputs(b - 1)
                    if r < 2 or not last:
                        scores(*ahead(b, r))
                    if r == 0 and not first:
                        project_outputs(b - 1)
                    if r == 1 and not last:
                        pe.wait_ge(added, passed(b))
                        project(b + 1)
                    if r == 2 and not last:
                        project_values(b + 1)
                    values(b, r)

            project(0)
            project_values(0)
            scores(0, 0)
            scores(0, 1)
            pe.wait_ge(vtaken, passed(1))
            pipeline(pe, sequence)
            turn_outputs(B - 1)
            project_outputs(B - 1)

        @block.vector
        def _(dve):
            def softmax(b, r):
                n = b * 4 + r
                dve.wait_ge(scored, passed(n + 1))
                nc.vector.tensor_tensor(part(probs[r % 2], 0), score_bank(0),
                                        mask[:, 1, :].unsqueeze(1).broadcast_to([P, 4, P]), ALU.add)\
                    .then_inc(masked, 1)
                nc.vector.tensor_tensor(part(probs[r % 2], 1), score_bank(1),
                                        mask[:].rearrange("p a k -> p (a k)").unsqueeze(1)
                                        .broadcast_to([P, 4, 2 * P]), ALU.add).then_inc(masked, 1)
                dve.wait_ge(masked, passed(n * 2 + 2))
                for t in range(TILES):
                    nc.vector.tensor_reduce(mx[:, r % 2, t * 4:t * 4 + 4], part(probs[r % 2], t), AX, ALU.max)\
                        .then_inc(maxed, 1)
                dve.wait_ge(maxed, passed(n * 2 + 2))
                nc.vector.tensor_scalar(bias[:, r % 2, :], mx[:, r % 2, :], -A_SCALE, None, ALU.mult)\
                    .then_inc(biased, 1)

            def take(b, r):
                n = b * 4 + r
                dve.wait_ge(turned, passed(n + 1))
                nc.vector.tensor_copy(probsT[r % 2][:, 4:12, :].rearrange("p j q -> p (j q)"),
                                      banks[:, 6:8, :].rearrange("p b c -> p (b c)")).then_inc(taken, 1)
                dve.wait_ge(exped, passed(n + 1))
                if r == 0:
                    dve.wait_ge(odone, passed(b))
                nc.vector.reciprocal(rtotal[:, r], total[:, r]).then_inc(totalled, 1)

            def add(b):
                dve.wait_ge(wo_done, passed(b + 1))
                rows = xT[:, bass.ds(b, 1), PAD:PAD + T].rearrange("p b t -> p (b t)")
                nc.vector.tensor_tensor(rows, rows, banks[:, 0, T:2 * T], ALU.add).then_inc(added, 1)

            def sequence(b, first, last):
                for r in range(4):
                    take(b, r)
                    if r < 2 or not last:
                        softmax(*ahead(b, r))
                    if r == 0 and not first:
                        add(b - 1)
                dve.wait_ge(summed, passed(b * 4 + 4))
                dve.wait_ge(totalled, passed(b * 4 + 4))
                for t in range(TILES):
                    last = nc.vector.tensor_tensor(
                        o[:, t, :].rearrange("p (r s d) -> p r s d", r=4, s=4),
                        banks[:, 1, t * P:(t + 1) * P].rearrange("p (r s d) -> p r s d", r=4, s=4),
                        rtotal[:, :, t, :].unsqueeze(3).broadcast_to([P, 4, 4, AD]), ALU.mult)
                last.then_inc(odone, 1)

            softmax(0, 0)
            softmax(0, 1)
            pipeline(dve, sequence)
            add(B - 1)

        @block.scalar
        def _(act):
            def take_queries_keys(b):
                act.wait_ge(proj, passed(b + 1))
                nc.scalar.activation(q[:], banks[:, 0, 0:T], ACT.Copy)
                nc.scalar.activation(kT[:], banks[:, 0, T:2 * T], ACT.Copy).then_inc(ktaken, 1)

            def take_values(b):
                act.wait_ge(summed, passed(b * 4))
                act.wait_ge(vproj, passed(b + 1))
                nc.scalar.activation(v[:].rearrange("p t n -> p (t n)"), banks[:, 0, 0:T], ACT.Copy)\
                    .then_inc(vtaken, 1)

            def exps(b, r):
                act.wait_ge(biased, passed(b * 4 + r + 1))
                for t in range(TILES):
                    for s in range(4):
                        i = t * 4 + s
                        last = nc.scalar.activation(part(probs[r % 2], t)[:, s, :], part(probs[r % 2], t)[:, s, :],
                                                    ACT.Exp, bias=bias[:, r % 2, i:i + 1], scale=A_SCALE,
                                                    accum_out=total[:, r, t, s:s + 1])
                last.then_inc(exped, 1)

            def take(b, r):
                act.wait_ge(turned, passed(b * 4 + r + 1))
                nc.scalar.activation(probsT[r % 2][:, 0:4, :].rearrange("p j q -> p (j q)"), banks[:, 5, :],
                                     ACT.Copy).then_inc(taken, 1)

            def take_outputs(b):
                act.wait_ge(oturned, passed(b + 1))
                nc.scalar.activation(oT[:], banks[:, 0, 0:T], ACT.Copy).then_inc(otaken, 1)

            def sequence(b, first, last):
                for r in range(4):
                    take(b, r)
                    if r == 0 and not first:
                        take_outputs(b - 1)
                    if r < 3:
                        exps(b, r + 1)
                    elif not last:
                        exps(b + 1, 0)
                    if r == 1 and not last:
                        take_queries_keys(b + 1)
                if not last:
                    take_values(b + 1)

            take_queries_keys(0)
            take_values(0)
            exps(0, 0)
            pipeline(act, sequence)
            take_outputs(B - 1)


@scoped
def experts(nc, sem, sb, xT, norm, banks, ident, wr, ea, eb, spread, before):
    lg = sb("e_lg", [B, E])
    top = sb("e_top", [B, 1])
    ahead = sb("e_ahead", [B, E, E])
    ties = sb("e_ties", [B, E, E])
    rank = sb("e_rank", [B, E])
    ex = sb("e_ex", [B, E])
    tot = sb("e_tot", [B, 1])
    gates = sb("e_gates", [B, E])
    gT = sb("e_gT", [E, B])
    gcol = sb("e_gcol", [P, EC, B])
    bg = [sb(f"e_bg{i}", [P, EC, P]) for i in range(2)]
    wb = [sb(f"e_wb{i}", [P, P]) for i in range(2)]
    chain, on_pe, on_act = sem("e_chain"), sem("e_pe"), sem("e_act")
    gated, mixed, made, applied, added = (sem("e_gated"), sem("e_mixed"), sem("e_made"), sem("e_applied"),
                                          sem("e_added"))
    steps = [0]

    with nc.Block() as block:
        @block.tensor
        def _(pe):
            first = norm[:].rearrange("p (b t) -> p b t", b=B)[:, :, 0]
            nc.tensor.matmul(banks[0:B, 4, 0:E], first, wr[:], start=True, stop=True).then_inc(on_pe, 1)
            pe.wait_ge(on_act, 2)
            nc.tensor.transpose(banks[0:E, 5, 0:B], gates[:], ident[0:B, 0:B]).then_inc(on_pe, 1)
            pe.wait_ge(on_act, 3)
            for c in range(EC):
                last = nc.tensor.matmul(banks[:, 6, c * B:(c + 1) * B], spread[:, c * P:(c + 1) * P], gT[:],
                                        start=True, stop=True)
            last.then_inc(on_pe, 1)
            with pe.Fori(0, B // 2) as i:
                for k in range(2):
                    b = i * 2 + k
                    pe.wait_ge(gated, passed(b + 1))
                    pe.wait_ge(made, passed(i * 2))
                    for c in range(EC):
                        last = nc.tensor.matmul(banks[:, k, 0:P], ea[:, c, :], bg[k][:, c, :],
                                                start=(c == 0), stop=(c == EC - 1))
                    last.then_inc(mixed, 1)
                for k in range(2):
                    b = i * 2 + k
                    pe.wait_ge(made, passed(b + 1))
                    pe.wait_ge(added, passed(i * 2))
                    nc.tensor.matmul(banks[:, 2 + k, 0:T], wb[k][:], norm[:, bass.ds(b * T, T)],
                                     start=True, stop=True).then_inc(applied, 1)

        @block.vector
        def _(dve):
            def link(ins):
                steps[0] += 1
                ins.then_inc(chain, 1)
                dve.wait_ge(chain, steps[0])
            dve.wait_ge(on_pe, 1)
            link(nc.vector.tensor_copy(lg[:], banks[0:B, 4, 0:E]))
            link(nc.vector.tensor_reduce(top[:], lg[:], AX, ALU.max))
            other, own = lg[:].unsqueeze(1).broadcast_to([B, E, E]), lg[:].unsqueeze(2).broadcast_to([B, E, E])
            link(nc.vector.tensor_tensor(ahead[:], other, own, ALU.is_gt))
            link(nc.vector.tensor_tensor(ties[:], other, own, ALU.is_equal))
            link(nc.vector.tensor_tensor(ties[:], ties[:], before[:], ALU.mult))
            link(nc.vector.tensor_tensor(ahead[:], ahead[:], ties[:], ALU.add))
            link(nc.vector.tensor_reduce(rank[:], ahead[:], AX, ALU.add))
            link(nc.vector.tensor_scalar(rank[:], rank[:], 2.0, None, ALU.is_lt))
            link(nc.vector.tensor_scalar(ex[:], lg[:], top[:], None, ALU.subtract))
            dve.wait_ge(on_act, 1)
            link(nc.vector.tensor_tensor(ex[:], ex[:], rank[:], ALU.mult))
            link(nc.vector.tensor_reduce(tot[:], ex[:], AX, ALU.add))
            link(nc.vector.reciprocal(tot[:], tot[:]))
            nc.vector.tensor_scalar(gates[:], ex[:], tot[:], None, ALU.mult).then_inc(on_act, 1)
            dve.wait_ge(on_pe, 2)
            nc.vector.tensor_copy(gT[:], banks[0:E, 5, 0:B]).then_inc(on_act, 1)
            dve.wait_ge(on_pe, 3)
            link(nc.vector.tensor_copy(gcol[:].rearrange("p c b -> p (c b)"), banks[:, 6, 0:EC * B]))
            with dve.Fori(0, B // 2) as i:
                for k in range(2):
                    b = i * 2 + k
                    dve.wait_ge(mixed, passed(i * 2))
                    nc.vector.tensor_tensor(bg[k][:], eb[:], gcol[:, :, bass.ds(b, 1)].broadcast_to([P, EC, P]),
                                            ALU.mult).then_inc(gated, 1)
                for k in range(2):
                    b = i * 2 + k
                    dve.wait_ge(mixed, passed(b + 1))
                    dve.wait_ge(applied, passed(i * 2))
                    nc.vector.tensor_tensor(wb[k][:], banks[:, k, 0:P], ident[:], ALU.add).then_inc(made, 1)
                for k in range(2):
                    b = i * 2 + k
                    dve.wait_ge(applied, passed(b + 1))
                    rows = xT[:, bass.ds(b, 1), PAD:PAD + T].rearrange("p b t -> p (b t)")
                    nc.vector.tensor_tensor(rows, rows, banks[:, 2 + k, 0:T], ALU.add).then_inc(added, 1)

        @block.scalar
        def _(act):
            act.wait_ge(chain, 9)
            nc.scalar.activation(ex[:], ex[:], ACT.Exp).then_inc(on_act, 1)


@scoped
def retention(nc, sem, sb, xT, norm, spare, banks, ident, eps_col, w, wv, wg, wo, gn, tab, decay, head_mask):
    xa = sb("r_x", [P, T])
    rot = sb("r_rot", [P, 2, T])
    rot2 = sb("r_rot2", [P, 2, T])
    km = sb("r_km", [P, RH, T])
    v = [sb(f"r_v{i}", [P, TILES, RH * RV]) for i in range(2)]
    g = [sb(f"r_g{i}", [P, TILES, RH * RV]) for i in range(2)]
    att = sb("r_att", [P, RH, 3, P])
    osb = [sb(f"r_o{i}", [P, TILES * RH, RV]) for i in range(2)]
    osq = sb("r_osq", [P, TILES * RH, RV])
    ss = sb("r_ss", [P, TILES * RH])
    rs = sb("r_rs", [P, TILES * RH])
    power = sb("r_power", [P, TILES * RH])
    oT = sb("r_oT", [P, 2, T])
    xcopy, qk, vg, qktaken, rotated = sem("r_xcopy"), sem("r_qk"), sem("r_vg"), sem("r_qktaken"), sem("r_rotated")
    vgtaken, scored, decayed, summed = sem("r_vgtaken"), sem("r_scored"), sem("r_decayed"), sem("r_summed")
    squared, sums, ssum, inv = sem("r_squared"), sem("r_sums"), sem("r_ssum"), sem("r_inv")
    weighted, scaled = sem("r_weighted"), sem("r_scaled")
    gated, turned, took, wo_done, added = sem("r_gated"), sem("r_turned"), sem("r_took"), sem("r_wo"), sem("r_added")
    ready, kmasked = sem("r_ready"), sem("r_kmasked")

    def pipeline(eng, iteration):
        for i in range(2):
            iteration(i, i, lambda lag: lag <= i)
        with eng.Fori(1, B // 2) as half:
            for k in range(2):
                iteration(half * 2 + k, k, lambda lag: True)
        for i in range(B, B + 2):
            iteration(i, i % 2, lambda lag: lag > i - B)

    with nc.Block() as block:
        @block.gpsimd
        def _(pool):
            nc.gpsimd.memset(power[:], -0.5).then_inc(ready, 1)
            pool.wait_ge(ready, passed(1))

            def iteration(i, k, live):
                if live(0):
                    pool.wait_ge(vg, passed(i))
                    pool.sem_inc(sem("gate"), 1)
                    nc.gpsimd.tensor_copy(xa[:], norm[:, bass.ds(i * T, T)]).then_inc(xcopy, 1)
                    pool.wait_ge(rotated, passed(i + 1))
                    pool.wait_ge(scored, passed(i))
                    nc.gpsimd.tensor_tensor(km[:], rot[:, 1, :].unsqueeze(1).broadcast_to([P, RH, T]),
                                            head_mask[:].unsqueeze(2).broadcast_to([P, RH, T]), ALU.mult)\
                        .then_inc(kmasked, 1)
                if live(1):
                    pool.wait_ge(ssum, passed(i))
                    nc.gpsimd.tensor_tensor(rs[:], ss[:], power[:], ALU.pow).then_inc(inv, 1)
            pipeline(pool, iteration)

        @block.tensor
        def _(pe):
            def iteration(i, k, live):
                if live(0):
                    pe.wait_ge(xcopy, passed(i + 1))
                    pe.wait_ge(qktaken, passed(i * 2))
                    if live(2):
                        pe.wait_ge(took, passed(i - 2))
                    for j in range(4):
                        last = nc.tensor.matmul(banks[:, j % 2, (j // 2) * T:(j // 2 + 1) * T], w[:, j, :], xa[:],
                                                start=True, stop=True)
                    last.then_inc(qk, 1)
                    pe.wait_ge(vgtaken, passed(i * 2))
                    if live(2):
                        pe.wait_ge(added, passed(i - 2))
                    for t in range(TILES):
                        cols = slice(t * RH * RV, (t + 1) * RH * RV)
                        nc.tensor.matmul(banks[:, 2, cols], xa[:, t * P:(t + 1) * P], wv[:], start=True, stop=True)
                        last = nc.tensor.matmul(banks[:, 3, cols], xa[:, t * P:(t + 1) * P], wg[:],
                                                start=True, stop=True)
                    last.then_inc(vg, 1)
                if live(1):
                    pe.wait_ge(vgtaken, passed(i * 2))
                    pe.wait_ge(decayed, passed(i * 2))
                    pe.wait_ge(weighted, passed(i - 1))
                    u = v[1 - k]
                    for hd in range(RH):
                        cols = slice(hd * RV, (hd + 1) * RV)
                        nc.tensor.matmul(banks[:, 7, hd * RV:(hd + 1) * RV], att[:, hd, 0, :], u[:, 0, cols],
                                         start=True, stop=True)
                        for c in range(2):
                            last = nc.tensor.matmul(banks[:, 7, (RH + hd) * RV:(RH + hd + 1) * RV],
                                                    att[:, hd, 1 + c, :], u[:, c, cols], start=(c == 0), stop=(c == 1))
                    last.then_inc(summed, 1)
                if live(2):
                    pe.wait_ge(gated, passed(i - 1))
                    if live(0):
                        pe.wait_ge(qktaken, passed(i * 2 + 2))
                    else:
                        pe.wait_ge(took, passed(i - 2))
                    for t in range(TILES):
                        for c in range(2):
                            last = nc.tensor.transpose(
                                banks[:, 0, (c * 2 + t) * P:(c * 2 + t + 1) * P],
                                osb[k][:, t * RH:(t + 1) * RH, :].rearrange("p h d -> p (h d)")[:, c * P:(c + 1) * P],
                                ident[:])
                    last.then_inc(turned, 1)
                if live(0):
                    pe.wait_ge(rotated, passed(i + 1))
                    pe.wait_ge(kmasked, passed(i + 1))
                    pe.wait_ge(decayed, passed(i * 2))
                    for hd in range(RH):
                        nc.tensor.matmul(banks[:, 4 + hd // 2, (hd % 2) * T:(hd % 2 + 1) * T], km[:, hd, 0:P],
                                         rot[:, 0, :], start=True, stop=True)
                        last = nc.tensor.matmul(banks[:, 6, hd * P:(hd + 1) * P], km[:, hd, P:2 * P],
                                                rot[:, 0, P:2 * P], start=True, stop=True)
                    last.then_inc(scored, 1)
                if live(2):
                    pe.wait_ge(took, passed(i - 1))
                    if live(0):
                        pe.wait_ge(vgtaken, passed(i * 2 + 2))
                    else:
                        pe.wait_ge(added, passed(i - 2))
                    for c in range(2):
                        last = nc.tensor.matmul(banks[:, 3, 0:T], wo[:, c, :], oT[:, c, :], start=(c == 0), stop=(c == 1))
                    last.then_inc(wo_done, 1)
            pipeline(pe, iteration)

        @block.vector
        def _(dve):
            def iteration(i, k, live):
                if live(0):
                    dve.wait_ge(qk, passed(i + 1))
                    dve.wait_ge(scored, passed(i))
                    dve.wait_ge(rotated, passed(i))
                    nc.vector.tensor_tensor(rot[:].rearrange("p a t -> p (a t)"), banks[:, 0, :],
                                            tab[:, 0, :, :].rearrange("p a t -> p (a t)"), ALU.mult).then_inc(qktaken, 1)
                    nc.vector.tensor_tensor(rot2[:].rearrange("p a t -> p (a t)"), banks[:, 1, :],
                                            tab[:, 1, :, :].rearrange("p a t -> p (a t)"), ALU.mult).then_inc(qktaken, 1)
                    dve.wait_ge(qktaken, passed(i * 2 + 2))
                    nc.vector.tensor_tensor(rot[:], rot[:], rot2[:], ALU.add).then_inc(rotated, 1)
                o = osb[1 - k]
                if live(1):
                    dve.wait_ge(squared, passed(i))
                    dve.wait_ge(inv, passed(i - 1))
                    nc.vector.tensor_reduce(ss[:], osq[:], AX, ALU.add).then_inc(sums, 1)
                    dve.wait_ge(sums, passed(i))
                    nc.vector.tensor_scalar(ss[:], ss[:], 1.0 / RV, EPS, ALU.mult, ALU.add).then_inc(ssum, 1)
                    if live(2):
                        dve.wait_ge(turned, passed(i - 2))
                    nc.vector.tensor_tensor(o[:], banks[:, 7, :].rearrange("p (h d) -> p h d", d=RV),
                                            gn[:].unsqueeze(1).broadcast_to([P, TILES * RH, RV]), ALU.mult)\
                        .then_inc(weighted, 1)
                if live(0):
                    dve.wait_ge(scored, passed(i + 1))
                    nc.vector.tensor_tensor(att[:, :, 0:2, :].rearrange("p h a q -> p h (a q)"),
                                            banks[:, 4:6, :].rearrange("p b (h q) -> p (b h) q", q=T),
                                            decay[:], ALU.mult).then_inc(decayed, 1)
                    nc.vector.tensor_tensor(att[:, :, 2, :], banks[:, 6, :].rearrange("p (h q) -> p h q", q=P),
                                            decay[:, :, 0:P], ALU.mult).then_inc(decayed, 1)
                if live(1):
                    dve.wait_ge(inv, passed(i))
                    dve.wait_ge(weighted, passed(i))
                    nc.vector.tensor_tensor(o[:], o[:], rs[:].unsqueeze(2).broadcast_to([P, TILES * RH, RV]),
                                            ALU.mult).then_inc(scaled, 1)
                    dve.wait_ge(scaled, passed(i))
                    nc.vector.tensor_tensor(o[:].rearrange("p h d -> p (h d)"), o[:].rearrange("p h d -> p (h d)"),
                                            g[1 - k][:].rearrange("p t n -> p (t n)"), ALU.mult).then_inc(gated, 1)
                if live(2):
                    dve.wait_ge(wo_done, passed(i - 1))
                    rows = xT[:, bass.ds(i - 2, 1), PAD:PAD + T].rearrange("p b t -> p (b t)")
                    nc.vector.tensor_tensor(rows, rows, banks[:, 3, 0:T], ALU.add).then_inc(added, 1)
            pipeline(dve, iteration)

        @block.scalar
        def _(act):
            def iteration(i, k, live):
                if live(0):
                    act.wait_ge(vg, passed(i + 1))
                    if live(2):
                        act.wait_ge(gated, passed(i - 1))
                    nc.scalar.activation(g[k][:].rearrange("p t n -> p (t n)"), banks[:, 3, :], ACT.Silu)\
                        .then_inc(vgtaken, 1)
                    nc.scalar.activation(v[k][:].rearrange("p t n -> p (t n)"), banks[:, 2, :], ACT.Copy)\
                        .then_inc(vgtaken, 1)
                if live(1):
                    act.wait_ge(summed, passed(i))
                    act.wait_ge(ssum, passed(i - 1))
                    nc.scalar.activation(osq[:].rearrange("p h d -> p (h d)"), banks[:, 7, :], ACT.Square)\
                        .then_inc(squared, 1)
                if live(2):
                    act.wait_ge(turned, passed(i - 1))
                    nc.scalar.activation(oT[:].rearrange("p c t -> p (c t)"), banks[:, 0, :], ACT.Copy).then_inc(took, 1)
            pipeline(act, iteration)


@scoped
def window_attention(nc, sem, sb, layer, h, xT, spare0, spare1, banks, ident, wqkv, wo, base, scl, tab, mask,
                     m_w1, m_w2, m_col):
    N = B * STEPS
    LAG = 4
    xs = [sb(f"w_xs{t}", [P, WIN + P]) for t in range(TILES)]
    sq = sb("w_sq", [P, 2, HALF, WD])
    t1 = [sb(f"w_t1{i}", [P, 2 * HALF * WD]) for i in range(2)]
    t2 = [sb(f"w_t2{i}", [P, 2 * HALF * WD]) for i in range(2)]
    ss = [sb(f"w_ss{i}", [P, 2 * HALF]) for i in range(2)]
    rn = [sb(f"w_rn{i}", [P, 2 * HALF]) for i in range(2)]
    power = sb("w_power", [P, 2 * HALF])
    qT = [sb(f"w_qT{i}", [P, NPAIR, P]) for i in range(2)]
    kT = sb("w_kT", [P, WH // 2, WIN + T])
    vd = [sb(f"w_vd{j}", [P, NWIN, NPAIR * WD]) for j in range(STEPS)]
    pr = [sb(f"w_pr{i}", [P, NPAIR, 2, 2 * WIN]) for i in range(2)]
    mx = [sb(f"w_mx{i}", [P, HALF]) for i in range(2)]
    bias = [sb(f"w_bias{i}", [P, HALF]) for i in range(2)]
    tot = [sb(f"w_tot{i}", [P, HALF]) for i in range(2)]
    rl = [sb(f"w_rl{i}", [P, HALF]) for i in range(2)]
    prT = sb("w_prT", [P, NPAIR, P])
    on = [sb(f"w_on{i}", [P, NPAIR, 2, WD]) for i in range(2)]
    oT = [sb(f"w_oT{i}", [P, NPAIR, P]) for i in range(WH // HALF)]

    S = {n: sem("w_" + n) for n in (
        "weights mlp_weights shifted0 shifted1 qk q_squared k_squared k_rotated q_rotated sums guarded added rnorm normed turned "
        "k_turned q_turned v_made v_taken scored masked maxed biased exped inverse p_turned p_taken "
        "valued divided o_turned o_taken projected residual ready tabled").split()}
    C = 2 * HALF * WD // 2

    def pairs(bank):
        return banks[:, bank:bank + 2, 0:NPAIR * WD].rearrange("p a (g d) -> p a g d", d=WD)

    def pipeline(eng, iteration):
        def one(j, seq, live):
            iteration(j, seq, lambda lag: layer * N + seq * STEPS + (j - lag + 1), live)
        for j in range(STEPS):
            one(j, 0, lambda lag: lag <= j)
        with eng.Fori(1, B) as seq:
            for j in range(STEPS):
                one(j, seq, lambda lag: True)
        for j in range(LAG):
            one(j, B, lambda lag: lag > j)

    with nc.Block() as block:
        @block.sync
        def _(sp):
            for dst, name in ((m_w1, "m_w1"), (m_w2, "m_w2"), (m_col, "m_col")):
                sp.dma_start(dst[:], h[name][bass.ds(layer, 1)].squeeze(0)).then_inc(S["mlp_weights"], 16)
            sp.wait_ge(S["mlp_weights"], layer * 48 + 48)
            sp.sem_inc(sem("gate"), 1)

        @block.gpsimd
        def _(pool):
            nc.gpsimd.memset(power[:], -0.5).then_inc(S["ready"], 1)
            nc.gpsimd.memset(kT[:, :, 0:WIN], 0.0).then_inc(S["ready"], 1)
            pool.wait_ge(S["ready"], passed(layer * 2 + 2))

            def shift(t, seq):
                src = xT[:, bass.ds(seq, 1), :].rearrange("p b t -> p (b t)")
                lo = PAD - WIN + t * P
                nc.gpsimd.tensor_copy(xs[t][0:64, :], src[0:64, lo:lo + WIN + P]).then_inc(S[f"shifted{t}"], 1)
                made = (layer * (B + 1 - t) + seq) * 2
                pool.wait_ge(S[f"shifted{t}"], passed(made + 1))
                pool.sem_inc(sem("gate"), 1)
                nc.gpsimd.tensor_copy(xs[t][64:P, :], src[64:P, lo - 1:lo - 1 + WIN + P])\
                    .then_inc(S[f"shifted{t}"], 1)
                pool.wait_ge(S[f"shifted{t}"], passed(made + 2))
                pool.sem_inc(sem("gate"), 1)

            pool.sem_inc(sem("gate"), 1)
            shift(0, 0)

            def iteration(j, seq, n, live):
                if live(0):
                    if j % 2 == 0:
                        if live(1):
                            pool.wait_ge(S["v_made"], passed(n(1) * 2))
                            pool.sem_inc(sem("gate"), 1)
                        if j == 0:
                            shift(1, seq)
                        else:
                            shift(0, seq + 1)
                    pool.wait_ge(S["guarded"], passed(n(0)))
                    if live(2):
                        pool.wait_ge(S["exped"], passed(n(2)))
                    nc.gpsimd.tensor_tensor(rn[j % 2][:], ss[j % 2][:], power[:], ALU.pow).then_inc(S["rnorm"], 1)
            pipeline(pool, iteration)

        @block.tensor
        def _(pe):
            pe.wait_ge(S["weights"], layer * 48 + 48)

            def iteration(j, seq, n, live):
                t, hh = j // 2, j % 2
                j1, j2, j3 = (j - 1) % STEPS, (j - 2) % STEPS, (j - 3) % STEPS
                x = xs[t]

                def values(a):
                    pe.wait_ge(S["v_taken"], passed((n(0) - 1) * 2 + a))
                    for w in (2 * a, 2 * a + 1):
                        for par in range(2):
                            cols = wqkv[:, 2 * INNER + hh * C:2 * INNER + (hh + 1) * C]\
                                .rearrange("p (g a d) -> p a g d", a=2, d=WD)[:, par]
                            lo = (w - 2 * a) * NPAIR * WD
                            last = nc.tensor.matmul(
                                banks[64 * par:64 * par + 64, 2, lo:lo + NPAIR * WD].rearrange("p (g d) -> p g d", d=WD),
                                x[:, WIN * w:WIN * (w + 2)], cols, start=True, stop=True)
                    last.then_inc(S["v_made"], 1)

                if live(0):
                    pe.wait_ge(S["k_squared"], passed(n(0) - 1))
                    pe.wait_ge(S["q_rotated"], passed((n(0) - 1) * 2))
                    if hh == 0:
                        pe.wait_ge(S[f"shifted{t}"], passed((layer * (B + 1 - t) + seq) * 2 + 2))
                    for i in range(2):
                        last = nc.tensor.matmul(banks[:, i, :], x[:, WIN:], wqkv[:, i * INNER + hh * C:i * INNER + (hh + 1) * C],
                                                start=True, stop=True)
                        last.then_inc(S["qk"], 1)
                if live(0):
                    values(0)
                if live(1):
                    pe.wait_ge(S["added"], passed(n(1)))
                    if live(3):
                        pe.wait_ge(S["divided"], passed(n(3)))
                    for i in range(2):
                        if i == 1:
                            pe.wait_ge(S["normed"], passed(n(1)))
                        for g in range(NPAIR):
                            lo = i * C + g * P
                            last = nc.tensor.transpose(banks[:, 3 + i, g * P:(g + 1) * P], t1[j1 % 2][:, lo:lo + P],
                                                       ident[:])
                        last.then_inc(S["turned"], 1)
                if live(2):
                    pe.wait_ge(S["exped"], passed(n(2)))
                    if live(4):
                        pe.wait_ge(S["residual"], passed(n(4)))
                    for g in range(NPAIR):
                        last = nc.tensor.transpose(banks[:, 7, g * P:(g + 1) * P],
                                                   pr[j2 % 2][:, g].rearrange("p a k -> p (a k)"), ident[:])
                    last.then_inc(S["p_turned"], 1)
                if live(0):
                    values(1)
                if live(1):
                    pe.wait_ge(S["k_turned"], passed(n(1)))
                    pe.wait_ge(S["q_turned"], passed(n(1)))
                    if live(2):
                        pe.wait_ge(S["masked"], passed(n(2)))
                    pe.sem_inc(sem("gate"), 1)
                    tk, hk = j1 // 2, j1 % 2
                    for par in range(2):
                        rows = slice(64 * par, 64 * par + 64)
                        for g in range(NPAIR):
                            for w in range(NWIN):
                                last = nc.tensor.matmul(
                                    banks[WIN * w:WIN * (w + 1), 5 + par, g * WD:(g + 1) * WD],
                                    qT[j1 % 2][rows, g, WIN * w:WIN * (w + 1)],
                                    kT[rows, hk * NPAIR + g, tk * P + WIN * w:tk * P + WIN * (w + 2)],
                                    start=True, stop=True)
                    last.then_inc(S["scored"], 1)
                if live(3):
                    if live(2):
                        pe.wait_ge(S["p_taken"], passed(n(2)))
                    else:
                        pe.wait_ge(S["residual"], passed(n(4)))
                    pe.wait_ge(S["divided"], passed(n(3)))
                    for g in range(NPAIR):
                        last = nc.tensor.transpose(banks[:, 7, g * P:(g + 1) * P],
                                                   on[j3 % 2][:, g].rearrange("p a d -> p (a d)"), ident[:])
                    last.then_inc(S["o_turned"], 1)
                if live(2):
                    pe.wait_ge(S["p_taken"], passed(n(2)))
                    pe.wait_ge(S["v_taken"], passed(n(2) * 2))
                    pe.sem_inc(sem("gate"), 1)
                    for par in range(2):
                        rows = slice(64 * par, 64 * par + 64)
                        for g in range(NPAIR):
                            for w in range(NWIN):
                                last = nc.tensor.matmul(
                                    banks[WIN * w:WIN * (w + 1), 3 + par, g * WD:(g + 1) * WD],
                                    prT[rows, g, WIN * w:WIN * (w + 1)], vd[j2][rows, w, g * WD:(g + 1) * WD],
                                    start=True, stop=True)
                    last.then_inc(S["valued"], 1)
                if live(3):
                    pe.wait_ge(S["o_taken"], passed(n(3)))
                    for g in range(NPAIR):
                        last = nc.tensor.matmul(banks[:, 7, 0:P], wo[:, j3 % 2 * NPAIR + g, :], oT[j3 % 2][:, g, :],
                                                start=(g == 0), stop=(g == NPAIR - 1))
                    last.then_inc(S["projected"], 1)
            pipeline(pe, iteration)

        @block.vector
        def _(dve):
            dve.wait_ge(S["weights"], layer * 48 + 48)
            nc.vector.tensor_tensor(tab[:], base[:], scl[:].unsqueeze(1).broadcast_to([P, 2 * TILES, 2 * WD]),
                                    ALU.mult).then_inc(S["tabled"], 1)
            dve.wait_ge(S["tabled"], passed(layer + 1))

            def iteration(j, seq, n, live):
                t = j // 2
                j1, j2, j3 = (j - 1) % STEPS, (j - 2) % STEPS, (j - 3) % STEPS
                if live(4):
                    dve.wait_ge(S["projected"], passed(n(4)))
                    s = seq - 1
                    lo = PAD + (j // 2) * P
                    rows = xT[:, bass.ds(s, 1), lo:lo + P].rearrange("p b t -> p (b t)")
                    nc.vector.tensor_tensor(rows, rows, banks[:, 7, 0:P], ALU.add).then_inc(S["residual"], 1)
                if live(0):
                    for i, name in ((1, "k_rotated"), (0, "q_rotated")):
                        if i == 1:
                            dve.wait_ge(S["qk"], passed(n(0) * 2))
                            if live(2):
                                dve.wait_ge(S["turned"], passed(n(2) * 2))
                        else:
                            dve.wait_ge(S["q_squared"], passed(n(0)))
                        src = banks[:, i, :].rearrange("p (h d) -> p h d", d=WD)
                        for cs, dst in ((0, t1), (1, t2)):
                            nc.vector.tensor_tensor(
                                dst[j % 2][:, i * C:(i + 1) * C].rearrange("p (h d) -> p h d", d=WD), src,
                                tab[:, 2 * t + cs, i * WD:(i + 1) * WD].unsqueeze(1).broadcast_to([P, HALF, WD]),
                                ALU.mult).then_inc(S[name], 1)
                    dve.wait_ge(S["q_rotated"], passed(n(0) * 2))
                    v1 = t1[j % 2][:].rearrange("p (h s d) -> p h s d", s=2, d=WD // 2)
                    v2 = t2[j % 2][:].rearrange("p (h s d) -> p h s d", s=2, d=WD // 2)
                    nc.vector.tensor_tensor(v1, v1, v2[:, :, ::-1, :], ALU.add).then_inc(S["added"], 1)
                    dve.wait_ge(S["k_squared"], passed(n(0)))
                    nc.vector.tensor_reduce(ss[j % 2][:], sq[:].rearrange("p a h d -> p (a h) d"), AX, ALU.add)\
                        .then_inc(S["sums"], 1)
                    dve.wait_ge(S["sums"], passed(n(0)))
                    nc.vector.tensor_scalar(ss[j % 2][:], ss[j % 2][:], 1e-24, None, ALU.max)\
                        .then_inc(S["guarded"], 1)
                if live(1):
                    dve.wait_ge(S["scored"], passed(n(1)))
                    p = pr[j1 % 2]
                    rows = p[:].rearrange("p g a k -> p (g a) k")
                    nc.vector.tensor_tensor(p[:].rearrange("p g a k -> p a g k"), pairs(5),
                                            mask[:, j1 // 2, :].unsqueeze(1).unsqueeze(1)
                                            .broadcast_to([P, 2, NPAIR, 2 * WIN]), ALU.add).then_inc(S["masked"], 1)
                    dve.wait_ge(S["masked"], passed(n(1)))
                    nc.vector.tensor_reduce(mx[j1 % 2][:], rows, AX, ALU.max).then_inc(S["maxed"], 1)
                    dve.wait_ge(S["maxed"], passed(n(1)))
                    dve.wait_ge(S["rnorm"], passed(n(1)))
                    nc.vector.scalar_tensor_tensor(out=bias[j1 % 2][:], in0=mx[j1 % 2][:], scalar=-1.0,
                                                   in1=rn[j1 % 2][:, 0:HALF], op0=ALU.mult, op1=ALU.mult)\
                        .then_inc(S["biased"], 1)
                if live(2):
                    dve.wait_ge(S["exped"], passed(n(2)))
                    nc.vector.reciprocal(rl[j2 % 2][:], tot[j2 % 2][:]).then_inc(S["inverse"], 1)
                    dve.wait_ge(S["inverse"], passed(n(2)))
                if live(2):
                    dve.wait_ge(S["valued"], passed(n(2)))
                    nc.vector.tensor_tensor(on[j2 % 2][:].rearrange("p g a d -> p a g d"), pairs(3),
                                            rl[j2 % 2][:].rearrange("p (g a) -> p a g", a=2).unsqueeze(3)
                                            .broadcast_to([P, 2, NPAIR, WD]), ALU.mult).then_inc(S["divided"], 1)
                if live(0):
                    dve.wait_ge(S["rnorm"], passed(n(0)))
                    dve.wait_ge(S["added"], passed(n(0)))
                    v1 = t1[j % 2][:, C:2 * C].rearrange("p (h d) -> p h d", d=WD)
                    nc.vector.tensor_tensor(v1, v1, rn[j % 2][:, HALF:].unsqueeze(2).broadcast_to([P, HALF, WD]),
                                            ALU.mult).then_inc(S["normed"], 1)
            pipeline(dve, iteration)

        @block.scalar
        def _(act):
            def iteration(j, seq, n, live):
                j1, j2, j3 = (j - 1) % STEPS, (j - 2) % STEPS, (j - 3) % STEPS

                def values(a):
                    act.wait_ge(S["v_made"], passed((n(0) - 1) * 2 + a + 1))
                    nc.scalar.activation(vd[j][:, 2 * a:2 * a + 2, :].rearrange("p w n -> p (w n)"), banks[:, 2, :],
                                         ACT.Copy).then_inc(S["v_taken"], 1)
                if live(0):
                    act.wait_ge(S["qk"], passed(n(0) * 2 - 1))
                    act.wait_ge(S["sums"], passed(n(0) - 1))
                    nc.scalar.activation(sq[:, 0].rearrange("p h d -> p (h d)"), banks[:, 0, :], ACT.Square)\
                        .then_inc(S["q_squared"], 1)
                if live(0):
                    values(0)
                    act.wait_ge(S["k_rotated"], passed(n(0) * 2))
                    nc.scalar.activation(sq[:, 1].rearrange("p h d -> p (h d)"), banks[:, 1, :], ACT.Square)\
                        .then_inc(S["k_squared"], 1)
                if live(1):
                    act.wait_ge(S["turned"], passed(n(1) * 2))
                    nc.scalar.activation(qT[j1 % 2][:].rearrange("p g q -> p (g q)"), banks[:, 3, :], ACT.Copy)\
                        .then_inc(S["q_turned"], 1)
                    hk, lo = j1 % 2, WIN + (j1 // 2) * P
                    nc.scalar.activation(kT[:, hk * NPAIR:(hk + 1) * NPAIR, lo:lo + P],
                                         banks[:, 4, :].rearrange("p (g k) -> p g k", k=P), ACT.Copy)\
                        .then_inc(S["k_turned"], 1)
                if live(2):
                    act.wait_ge(S["p_turned"], passed(n(2)))
                    nc.scalar.activation(prT[:].rearrange("p g q -> p (g q)"), banks[:, 7, :], ACT.Copy)\
                        .then_inc(S["p_taken"], 1)
                if live(0):
                    values(1)
                if live(3):
                    act.wait_ge(S["o_turned"], passed(n(3)))
                    nc.scalar.activation(oT[j3 % 2][:].rearrange("p g q -> p (g q)"), banks[:, 7, :], ACT.Copy)\
                        .then_inc(S["o_taken"], 1)
                if live(1):
                    act.wait_ge(S["biased"], passed(n(1)))
                    for g in range(NPAIR):
                        for par in range(2):
                            row, i = pr[j1 % 2][:, g, par, :], 2 * g + par
                            last = nc.scalar.activation(row, row, ACT.Exp, bias=bias[j1 % 2][:, i:i + 1],
                                                        scale=rn[j1 % 2][:, i:i + 1], accum_out=tot[j1 % 2][:, i:i + 1])
                    last.then_inc(S["exped"], 1)
            pipeline(act, iteration)


def load_window_weights(sp, weights, h, layer, wqkv, wo, scl):
    def of(name):
        return h[name][bass.ds(layer, 1)] if not isinstance(layer, int) else h[name][layer:layer + 1]
    sp.dma_start(wqkv[:], of("w_qkv").squeeze(0)).then_inc(weights, 16)
    sp.dma_start(wo[:], of("w_o").squeeze(0)).then_inc(weights, 16)
    sp.dma_start(scl[:], of("w_scl").broadcast_to([P, 2 * WD])).then_inc(weights, 16)


@scoped
def gated_mlp(nc, sem, sb, layer, xT, norm, banks, w1, w2, col):
    gel = [sb(f"m_gel{m}", [MC, CH]) for m in range(MG)]
    hid = [[sb(f"m_hid{k}{m}", [MC, CH]) for m in range(MG)] for k in range(2)]
    up, gelued, made = sem("m_up"), sem("m_gelued"), sem("m_made")
    down, residual, weights = sem("m_down"), sem("m_residual"), sem("w_weights")
    done = layer * NCH

    def b1(m, vg):
        return col[0:MC, 3 + 2 * m + vg:4 + 2 * m + vg]

    with nc.Block() as block:
        @block.sync
        def _(sp):
            sp.wait_ge(weights, (layer + 2) * 48)
            sp.sem_inc(sem("gate"), 1)

        @block.tensor
        def _(pe):
            def w_up(c, m, first=False):
                if not first:
                    pe.wait_ge(made, passed((done + c - 1) * MG + m + 1))
                for vg in range(2):
                    last = nc.tensor.matmul(banks[0:MC, 2 * m + vg, :], w1[:, 2 * m + vg, :],
                                            norm[:, bass.ds(c * CH, CH)], start=True, stop=True)
                last.then_inc(up, 1)

            def w_down(c, k, m):
                if m == 0:
                    pe.wait_ge(residual, passed(done + c - k))
                pe.wait_ge(made, passed((done + c) * MG + m + 1))
                last = nc.tensor.matmul(banks[:, 6 + k, :], w2[:, m, :], hid[k][m][:],
                                        start=(m == 0), stop=(m == MG - 1))
                if m == MG - 1:
                    last.then_inc(down, 1)

            for m in range(MG):
                w_up(0, m, True)
            with pe.Fori(0, NCH // 2 - 1) as i:
                for k in range(2):
                    for m in range(MG):
                        w_up(i * 2 + k + 1, m)
                        w_down(i * 2 + k, k, m)
            for m in range(MG):
                w_up(NCH - 1, m)
                w_down(NCH - 2, 0, m)
            for m in range(MG):
                w_down(NCH - 1, 1, m)

        @block.scalar
        def _(act):
            def gelus(c, first=False):
                for m in range(MG):
                    act.wait_ge(up, passed((done + c) * MG + m + 1))
                    if not first:
                        act.wait_ge(made, passed((done + c - 1) * MG + m + 1))
                    nc.scalar.activation(gel[m][:], banks[0:MC, 2 * m + 1, :], ACT.Gelu, bias=b1(m, 1))\
                        .then_inc(gelued, 1)

            gelus(0, True)
            gelus(1)
            with act.Fori(1, NCH // 2) as i:
                gelus(i * 2)
                gelus(i * 2 + 1)

        @block.vector
        def _(dve):
            def hidden(c, k):
                for m in range(MG):
                    dve.wait_ge(gelued, passed((done + c) * MG + m + 1))
                    nc.vector.scalar_tensor_tensor(out=hid[k][m][:], in0=banks[0:MC, 2 * m, :], scalar=b1(m, 0),
                                                   in1=gel[m][:], op0=ALU.add, op1=ALU.mult).then_inc(made, 1)

            def add(c, k):
                dve.wait_ge(down, passed(done + c + 1))
                rows = xT[:, bass.ds(c * PER, PER), PAD:PAD + T]
                nc.vector.scalar_tensor_tensor(out=rows, in0=banks[:, 6 + k, :].rearrange("p (b t) -> p b t", b=PER),
                                               scalar=col[:, 2:3], in1=rows, op0=ALU.add, op1=ALU.add)\
                    .then_inc(residual, 1)

            hidden(0, 0)
            with dve.Fori(0, NCH // 2 - 1) as i:
                for k in range(2):
                    hidden(i * 2 + k + 1, 1 - k)
                    add(i * 2 + k, k)
            hidden(NCH - 1, 1)
            add(NCH - 2, 0)
            add(NCH - 1, 1)


def arranged(x, **w):
    f = np.float32
    h = {k: np.asarray(v) for k, v in w.items()}
    t = {}
    t["x"] = np.asarray(x).transpose(2, 0, 1)
    t["ident"] = np.eye(P, dtype=f)
    t["a_w"] = np.stack([h["L0_attn_" + n].T for n in ("Wq", "Wk", "Wv", "Wo")], 1)
    p = np.arange(P)
    t["a_hm"] = (p[:, None] // AD == np.arange(AH)).astype(f)
    t["a_mask"] = np.stack([np.zeros((P, P)), np.where(p[None] <= p[:, None], 0, NEG)], 1).astype(f)
    t["e_wr"] = h["L0_ffn_Wr"].T
    t["e_a"] = h["L0_ffn_A"].reshape(EC, P, D).transpose(1, 0, 2)
    t["e_b"] = h["L0_ffn_Bw"].transpose(0, 2, 1).reshape(EC, P, D).transpose(1, 0, 2)
    t["e_spread"] = (np.arange(E * R)[None] // R == np.arange(E)[:, None]).astype(f)
    t["e_before"] = (np.arange(E)[None] < np.arange(E)[:, None]).astype(f)

    def swapped(m):
        return m.reshape(D, RH, 2, RK // 2)[:, :, ::-1].reshape(D, RH * RK)
    t["r_w"] = np.stack([h["L1_attn_Wq"], swapped(h["L1_attn_Wq"]), h["L1_attn_Wk"], swapped(h["L1_attn_Wk"])], 1)
    t["r_wv"], t["r_wg"] = h["L1_attn_Wv"], h["L1_attn_Wg"]
    t["r_wo"] = h["L1_attn_Wo"].reshape(2, P, D).transpose(1, 0, 2)
    t["r_gn"] = h["L1_attn_gn_weight"]
    freq = (f(1) / f(10000) ** (np.arange(0, RK, 2, dtype=f) / f(RK))).astype(f)
    ang = (np.arange(T, dtype=f)[None] * freq[:, None]).astype(f)
    cos, sin = np.tile(np.cos(ang), (2 * RH, 1)), np.tile(np.concatenate([-np.sin(ang), np.sin(ang)]), (RH, 1))
    both = np.stack([cos, sin], 1)
    t["r_tab"] = np.stack([both * f(RK ** -0.5), both], 2).astype(f)
    t["r_hm"] = (p[:, None] // RK == np.arange(RH)).astype(f)
    gamma = 1 - 2.0 ** (-5.0 - np.arange(RH))
    rel = np.arange(T)[None] - p[:, None]
    t["r_decay"] = np.where(rel[:, None] >= 0, gamma[None, :, None] ** np.maximum(rel, 0)[:, None], 0).astype(f)

    half = np.arange(0, WD, 2, dtype=f)
    freq = (f(1) / f(10000) ** (half / f(WD))).astype(f)
    pos = np.arange(T, dtype=f)
    ang = (pos[:, None] * freq[None]).astype(f)
    power = ((pos - T // 2) / f(WIN // 2)).astype(f)
    scale = ((half + f(0.4 * WD)) / f(1.4 * WD)).astype(f)[None] ** power[:, None]
    cos, sin = np.cos(ang), np.sin(ang)
    tab = np.stack([np.stack([np.concatenate([cos * m, cos * m], 1) for m in (scale * f(8), 1 / scale)], 1),
                    np.stack([np.concatenate([sin * m, -sin * m], 1) for m in (scale * f(8), 1 / scale)], 1)], 1)
    t["w_base"] = tab.reshape(TILES, P, 2, 2 * WD).transpose(1, 0, 2, 3).reshape(P, 2 * TILES, 2 * WD).astype(f)
    i, j = (p % WIN)[:, None], np.arange(2 * WIN)[None]
    seen = (j >= i) & (j <= i + WIN)
    first = seen & ((j >= WIN) | (p[:, None] >= WIN))
    t["w_mask"] = np.where(np.stack([first] + [seen] * (TILES - 1), 1), 0, NEG).astype(f)
    t["w_qkv"] = h["L1_ffn_Wqkv"]
    t["w_o"] = h["L1_ffn_Wo"].reshape(DEPTH, WH // 2, P, D).transpose(0, 2, 1, 3)
    t["w_scl"] = np.concatenate([h["L1_ffn_q_scale"], h["L1_ffn_k_scale"]], 1)

    def groups(m):
        m = m.reshape(*m.shape[:-1], 2, MLP)
        m = np.concatenate([m, np.zeros((*m.shape[:-1], MG * MC - MLP), m.dtype)], -1)
        return np.moveaxis(m.reshape(*m.shape[:-1], MG, MC), -2, -3).reshape(*m.shape[:-2], 2 * MG, MC)
    t["m_w1"] = groups(h["L1_ffn_W1"])
    w2 = h["L1_ffn_W2"]
    w2 = np.concatenate([w2, np.zeros((DEPTH, MG * MC - MLP, D), w2.dtype)], 1)
    t["m_w2"] = w2.reshape(DEPTH, MG, MC, D).transpose(0, 2, 1, 3)
    b1 = groups(h["L1_ffn_b1"])
    b1 = np.concatenate([b1, np.zeros((DEPTH, 2 * MG, P - MC), b1.dtype)], 2).transpose(0, 2, 1)
    t["m_col"] = np.concatenate([np.stack([h["L1_ffn_ln_g"], h["L1_ffn_ln_b"], h["L1_ffn_b2"]], 2), b1], 2)
    return {k: np.ascontiguousarray(v) for k, v in t.items()}


def kernel(L0_attn_x, **weights):
    from concourse import bacc
    from concourse.bass_utils import run_bass_kernel_spmd

    nc = bacc.Bacc("TRN2", target_bir_lowering=False, num_devices=1)
    arrays = arranged(L0_attn_x, **weights)
    h = {k: nc.dram_tensor(k + "_in", a.shape, mybir.dt.from_np(a.dtype), kind="ExternalInput").ap()
         for k, a in arrays.items()}
    out = nc.dram_tensor("out", (D, B, T), F32, kind="ExternalOutput").ap()
    program(nc, h, out)
    r = run_bass_kernel_spmd(nc, [{k + "_in": a for k, a in arrays.items()}], core_ids=[0])
    return np.ascontiguousarray(r.results[0]["out"].transpose(1, 2, 0))
```
